# Optimizing a Trainium2 kernel written in Bass

```python
import numpy as np
import jax
import jax.numpy as jnp

def _softmax(x, axis=-1):
    return jax.nn.softmax(x, axis=axis)

def _gelu(x):
    return jax.nn.gelu(x, approximate=True)

def _silu(x):
    return jax.nn.silu(x)

def _sigmoid(x):
    return jax.nn.sigmoid(x)

def _layernorm(x, axis=-1, eps=1e-05):
    m = jnp.mean(x, axis=axis, keepdims=True)
    v = jnp.var(x, axis=axis, keepdims=True)
    return (x - m) / jnp.sqrt(v + eps)

def _scatter_add(tgt, idx, src, axis=0):
    return tgt.at[idx].add(src)

def _segment_sum(src, seg, n):
    return jax.ops.segment_sum(src, seg, n)
kernel_name = 'mk_hybrid_d1_jaxref_r4_82addc'

def setup_inputs(seed: int=0):
    np.random.seed(seed)
    _w = jnp.asarray

    def _L0_attn_a_setup():
        import jax, jax.numpy as jnp
        import numpy as np
        N_HEADS = 16
        SEG = 64
        D_MODEL = 256
        NOISE_EPS = 1e-05

        def _forward(hidden_states, Wq, Wk, Wv, Wc, terrace_mix, index_decays, mega_decays):
            b, L, d = hidden_states.shape
            H, seg = (N_HEADS, SEG)
            Dh = d // H
            r = L // seg
            q = (hidden_states @ Wq.T).reshape(b, L, H, Dh)
            k = (hidden_states @ Wk.T).reshape(b, L, H, Dh)
            v = (hidden_states @ Wv.T).reshape(b, L, H, Dh)
            scores = jnp.einsum('bnhd,bmhd->bhnm', q, k) / jnp.sqrt(jnp.float32(Dh))
            idx = jnp.arange(L)
            causal = idx[:, None] >= idx[None, :]
            dblk = (idx // seg)[:, None] - (idx // seg)[None, :]
            neg = jnp.float32(-jnp.inf)
            scores = jnp.where(causal, scores, neg)
            terrace_allowed = causal & ((dblk == 0) | (dblk == 1))
            scores_t = jnp.where(terrace_allowed, scores, neg)
            att_t = jax.nn.softmax(scores_t, axis=-1)
            out_t = jnp.einsum('bhnm,bmhd->bhnd', att_t, v).reshape(b, H, r, seg, Dh)
            att = jax.nn.softmax(scores, axis=-1)
            awc = att.reshape(b, H, r, seg, L) * jnp.exp(index_decays)[None, :, None, :, None]
            pcs = awc.sum(axis=-2)
            mega = jnp.clip(jnp.exp(mega_decays * seg), 0.0, 2.0)
            s_seq = jnp.moveaxis(pcs, 2, 0)

            def step(carry, s):
                return (carry * mega[None, :, None] + s, carry)
            _, outs = jax.lax.scan(step, jnp.zeros_like(s_seq[0]), s_seq)
            w = jnp.moveaxis(outs, 0, 2)
            w = w / (w.sum(axis=-1, keepdims=True) + NOISE_EPS)
            kv = jnp.einsum('bhrs,bshd,bshe->brhde', w, k, v)
            qc = q.reshape(b, r, seg, H, Dh)
            out_lin = jnp.einsum('brlhd,brhde->bhrle', qc, kv)
            tw = jax.nn.sigmoid(terrace_mix)[None, None, None, :, None]
            y = tw * out_t + (1.0 - tw) * out_lin
            y = y.reshape(b, H, L, Dh).transpose(0, 2, 1, 3).reshape(b, L, d)
            return y @ Wc.T
        key = jax.random.key(seed)
        ks = jax.random.split(key, 8)
        b, L, d = (1, 512, D_MODEL)
        sc = 0.02
        hidden_states = jax.random.normal(ks[0], (b, L, d), jnp.float32)
        Wq = sc * jax.random.normal(ks[1], (d, d), jnp.float32)
        Wk = sc * jax.random.normal(ks[2], (d, d), jnp.float32)
        Wv = sc * jax.random.normal(ks[3], (d, d), jnp.float32)
        Wc = sc * jax.random.normal(ks[4], (d, d), jnp.float32)
        terrace_mix = 0.5 * jnp.ones((SEG,), jnp.float32)
        index_decays = -0.1 * jnp.ones((N_HEADS, SEG), jnp.float32) + 0.01 * jax.random.normal(ks[5], (N_HEADS, SEG), jnp.float32)
        mega_decays = -0.1 * jnp.ones((N_HEADS,), jnp.float32) + 0.01 * jax.random.normal(ks[6], (N_HEADS,), jnp.float32)
        return dict(hidden_states=hidden_states, Wq=Wq, Wk=Wk, Wv=Wv, Wc=Wc, terrace_mix=terrace_mix, index_decays=index_decays, mega_decays=mega_decays)
    _L0_attn_a_in = _L0_attn_a_setup()

    def _L0_attn_b_setup():
        import jax, jax.numpy as jnp
        import numpy as np
        import math
        NUM_HEADS = 4
        NUM_MEM = 4
        TOPK = 2
        CAPACITY = 0.5
        GATE_NORM = 16.0
        EPS = 1e-05
        B, S, D = (4, 512, 256)
        DK, DV = (128, 256)
        HDK, HDV = (DK // NUM_HEADS, DV // NUM_HEADS)
        LOW = 16

        def _transform(x, routing_mask, sel):
            b, s0, d = x.shape
            k = sel.shape[2]
            xr = jnp.repeat(x, k, axis=1)
            s = s0 * k
            mem_flat = sel.reshape(b, -1).reshape(-1)
            batch_idx = jnp.repeat(jnp.arange(b), s)
            combined = batch_idx * NUM_MEM + mem_flat
            sorted_idx = jnp.argsort(combined)
            x_sorted = xr.reshape(b * s, d)[sorted_idx]
            counts = routing_mask.sum(1)
            offset = jnp.cumsum(counts, axis=1)
            flat_off = (offset + jnp.arange(b)[:, None] * s).reshape(-1)
            cap_len = math.ceil(s0 * CAPACITY)
            prev = jnp.concatenate([jnp.zeros((1,), flat_off.dtype), flat_off[:-1]])
            idx = jnp.arange(cap_len)[None, :] + prev[:, None]
            trunc = idx + counts.reshape(-1)[:, None] - cap_len
            mask = (trunc < flat_off[:, None]) & (trunc >= 0) & (trunc >= prev[:, None])
            trunc = jnp.where(mask, trunc, 0)
            gathered = x_sorted[trunc.reshape(-1)]
            tx = gathered.reshape(b * NUM_MEM, cap_len, d) * mask[..., None]
            tx = tx.reshape(b, NUM_MEM, cap_len, d).transpose(1, 0, 2, 3)
            return (tx, trunc, sorted_idx, mask)

        def _reconstruct(ty, trunc, sorted_idx, rw, mask, b, s0):
            M, _, cap, H, dv = ty.shape
            g = ty.transpose(1, 0, 2, 3, 4).reshape(b * M * cap, H, dv)
            g = g * mask.reshape(-1)[:, None, None]
            res = jnp.zeros((b * s0 * TOPK, H, dv), ty.dtype).at[trunc.reshape(-1)].add(g)
            inv = jnp.argsort(sorted_idx)
            out = res[inv].reshape(b, s0, TOPK, H, dv)
            return (out * rw[..., None, None]).sum(2)

        def _gla(q, k, v, gk):

            def step(Smat, inp):
                qt, kt, vt, gt = inp
                Smat = Smat * jnp.exp(gt)[..., None] + kt[..., None] * vt[..., None, :]
                o = jnp.einsum('...k,...kv->...v', qt, Smat)
                return (Smat, o)
            S0 = jnp.zeros(q.shape[1:-1] + (q.shape[-1], v.shape[-1]), q.dtype)
            _, o = jax.lax.scan(step, S0, (q, k, v, gk))
            return o

        def _forward(x, w_gate, w_q, w_k, w_v, w_gk1, w_gk2, b_gk, w_ks, w_vs, w_gk1s, w_gk2s, b_gks, w_g, w_o, norm_w):
            b, s0, d = x.shape
            scale = HDK ** (-0.5)
            probs = jax.nn.softmax(x @ w_gate, -1)
            rw, sel = jax.lax.top_k(probs, TOPK)
            rw = rw / rw.sum(-1, keepdims=True)
            routing_mask = jax.nn.one_hot(sel, NUM_MEM, dtype=jnp.int32).sum(2)
            tx, trunc, sorted_idx, mask = _transform(x, routing_mask, sel)
            cap = tx.shape[2]
            q = jnp.einsum('mbtd,dk->mbtk', tx, w_q).reshape(NUM_MEM, b, cap, NUM_HEADS, HDK) * scale
            k = jnp.einsum('mbtd,mdk->mbtk', tx, w_k).reshape(NUM_MEM, b, cap, NUM_HEADS, HDK)
            v = jnp.einsum('mbtd,mdk->mbtk', tx, w_v).reshape(NUM_MEM, b, cap, NUM_HEADS, HDV)
            gk = jnp.einsum('mbtr,mrk->mbtk', jnp.einsum('mbtd,mdr->mbtr', tx, w_gk1), w_gk2) + b_gk[:, None, None, :]
            gk = (jax.nn.log_sigmoid(gk) / GATE_NORM).reshape(NUM_MEM, b, cap, NUM_HEADS, HDK)
            to_t = lambda a: jnp.moveaxis(a, 2, 0)
            o_mem = jnp.moveaxis(_gla(to_t(q), to_t(k), to_t(v), to_t(gk)), 0, 2)
            o_rout = _reconstruct(o_mem, trunc, sorted_idx, rw, mask, b, s0)
            qs = (x @ w_q).reshape(b, s0, NUM_HEADS, HDK) * scale
            ks = (x @ w_ks).reshape(b, s0, NUM_HEADS, HDK)
            vs = (x @ w_vs).reshape(b, s0, NUM_HEADS, HDV)
            gks = (jax.nn.log_sigmoid(x @ w_gk1s @ w_gk2s + b_gks) / GATE_NORM).reshape(b, s0, NUM_HEADS, HDK)
            tt = lambda a: jnp.moveaxis(a, 1, 0)
            o_sh = jnp.moveaxis(_gla(tt(qs), tt(ks), tt(vs), tt(gks)), 0, 1)
            o = o_rout + o_sh
            g = (x @ w_g).reshape(b, s0, NUM_HEADS, HDV)
            o = o * jax.lax.rsqrt(jnp.mean(o * o, -1, keepdims=True) + EPS) * norm_w
            o = o * (g * jax.nn.sigmoid(g))
            return o.reshape(b, s0, DV) @ w_o
        key = jax.random.key(seed)
        ks = jax.random.split(key, 17)
        n = lambda i, shp: 0.02 * jax.random.normal(ks[i], shp, dtype=jnp.float32)
        return {'x': jax.random.normal(ks[0], (B, S, D), dtype=jnp.float32), 'w_gate': n(1, (D, NUM_MEM)), 'w_q': n(2, (D, DK)), 'w_k': n(3, (NUM_MEM, D, DK)), 'w_v': n(4, (NUM_MEM, D, DV)), 'w_gk1': n(5, (NUM_MEM, D, LOW)), 'w_gk2': n(6, (NUM_MEM, LOW, DK)), 'b_gk': n(7, (NUM_MEM, DK)), 'w_ks': n(8, (D, DK)), 'w_vs': n(9, (D, DV)), 'w_gk1s': n(10, (D, LOW)), 'w_gk2s': n(11, (LOW, DK)), 'b_gks': n(12, (DK,)), 'w_g': n(13, (D, DV)), 'w_o': n(14, (DV, D)), 'norm_w': jnp.ones((HDV,), dtype=jnp.float32)}
    _L0_attn_b_in = _L0_attn_b_setup()

    def _L0_ffn_setup():
        import jax, jax.numpy as jnp
        import numpy as np
        H = 256
        M = 128
        E = 16
        TOP_K = 2
        SCALE = 2.5
        NORM_TOPK = True
        B, S = (1, 256)

        def _moe(x, gate_w, w_gate, w_up, w_down, ws_gate, ws_up, ws_down):
            T = x.shape[0]
            shared = jax.nn.silu(x @ ws_gate) * (x @ ws_up) @ ws_down
            scores = jax.nn.sigmoid(x.astype(jnp.float32) @ gate_w.T.astype(jnp.float32))
            topk_w, topk_idx = jax.lax.top_k(scores, TOP_K)
            if NORM_TOPK and TOP_K > 1:
                topk_w = topk_w / (topk_w.sum(-1, keepdims=True) + 1e-20)
            topk_w = topk_w * SCALE
            route = jnp.zeros((T, E), topk_w.dtype).at[jnp.arange(T)[:, None], topk_idx].set(topk_w)
            g = jnp.einsum('th,ehm->etm', x, w_gate)
            u = jnp.einsum('th,ehm->etm', x, w_up)
            eo = jnp.einsum('etm,emh->eth', jax.nn.silu(g) * u, w_down)
            routed = jnp.einsum('te,eth->th', route.astype(x.dtype), eo)
            return routed + shared
        key = jax.random.key(seed)
        ks = jax.random.split(key, 8)
        std = 0.02
        return {'hidden_states': jax.random.normal(ks[0], (B, S, H), jnp.float32), 'gate_w': jax.random.normal(ks[1], (E, H), jnp.float32) * std, 'w_gate': jax.random.normal(ks[2], (E, H, M), jnp.float32) * std, 'w_up': jax.random.normal(ks[3], (E, H, M), jnp.float32) * std, 'w_down': jax.random.normal(ks[4], (E, M, H), jnp.float32) * std, 'ws_gate': jax.random.normal(ks[5], (H, M), jnp.float32) * std, 'ws_up': jax.random.normal(ks[6], (H, M), jnp.float32) * std, 'ws_down': jax.random.normal(ks[7], (M, H), jnp.float32) * std}
    _L0_ffn_in = _L0_ffn_setup()
    _d = {'L0_attn_a_hidden_states': _L0_attn_a_in['hidden_states'], 'L0_attn_a_Wq': _L0_attn_a_in['Wq'], 'L0_attn_a_Wk': _L0_attn_a_in['Wk'], 'L0_attn_a_Wv': _L0_attn_a_in['Wv'], 'L0_attn_a_Wc': _L0_attn_a_in['Wc'], 'L0_attn_a_terrace_mix': _L0_attn_a_in['terrace_mix'], 'L0_attn_a_index_decays': _L0_attn_a_in['index_decays'], 'L0_attn_a_mega_decays': _L0_attn_a_in['mega_decays'], 'L0_attn_b_w_gate': _L0_attn_b_in['w_gate'], 'L0_attn_b_w_q': _L0_attn_b_in['w_q'], 'L0_attn_b_w_k': _L0_attn_b_in['w_k'], 'L0_attn_b_w_v': _L0_attn_b_in['w_v'], 'L0_attn_b_w_gk1': _L0_attn_b_in['w_gk1'], 'L0_attn_b_w_gk2': _L0_attn_b_in['w_gk2'], 'L0_attn_b_b_gk': _L0_attn_b_in['b_gk'], 'L0_attn_b_w_ks': _L0_attn_b_in['w_ks'], 'L0_attn_b_w_vs': _L0_attn_b_in['w_vs'], 'L0_attn_b_w_gk1s': _L0_attn_b_in['w_gk1s'], 'L0_attn_b_w_gk2s': _L0_attn_b_in['w_gk2s'], 'L0_attn_b_b_gks': _L0_attn_b_in['b_gks'], 'L0_attn_b_w_g': _L0_attn_b_in['w_g'], 'L0_attn_b_w_o': _L0_attn_b_in['w_o'], 'L0_attn_b_norm_w': _L0_attn_b_in['norm_w'], 'L0_ffn_gate_w': _L0_ffn_in['gate_w'], 'L0_ffn_w_gate': _L0_ffn_in['w_gate'], 'L0_ffn_w_up': _L0_ffn_in['w_up'], 'L0_ffn_w_down': _L0_ffn_in['w_down'], 'L0_ffn_ws_gate': _L0_ffn_in['ws_gate'], 'L0_ffn_ws_up': _L0_ffn_in['ws_up'], 'L0_ffn_ws_down': _L0_ffn_in['ws_down']}
    _x0 = _d['L0_attn_a_hidden_states']
    _d['L0_attn_a_hidden_states'] = jax.random.normal(jax.random.fold_in(jax.random.key(seed), 1), (2, 2048, 256), dtype=_x0.dtype)
    del _x0
    return _d

def reference(L0_attn_a_hidden_states, L0_attn_a_Wq, L0_attn_a_Wk, L0_attn_a_Wv, L0_attn_a_Wc, L0_attn_a_terrace_mix, L0_attn_a_index_decays, L0_attn_a_mega_decays, L0_attn_b_w_gate, L0_attn_b_w_q, L0_attn_b_w_k, L0_attn_b_w_v, L0_attn_b_w_gk1, L0_attn_b_w_gk2, L0_attn_b_b_gk, L0_attn_b_w_ks, L0_attn_b_w_vs, L0_attn_b_w_gk1s, L0_attn_b_w_gk2s, L0_attn_b_b_gks, L0_attn_b_w_g, L0_attn_b_w_o, L0_attn_b_norm_w, L0_ffn_gate_w, L0_ffn_w_gate, L0_ffn_w_up, L0_ffn_w_down, L0_ffn_ws_gate, L0_ffn_ws_up, L0_ffn_ws_down):

    def _L0_attn_a_ref(hidden_states, Wq, Wk, Wv, Wc, terrace_mix, index_decays, mega_decays):
        import jax, jax.numpy as jnp
        import numpy as np
        N_HEADS = 16
        SEG = 64
        D_MODEL = 256
        NOISE_EPS = 1e-05

        def _forward(hidden_states, Wq, Wk, Wv, Wc, terrace_mix, index_decays, mega_decays):
            b, L, d = hidden_states.shape
            H, seg = (N_HEADS, SEG)
            Dh = d // H
            r = L // seg
            q = (hidden_states @ Wq.T).reshape(b, L, H, Dh)
            k = (hidden_states @ Wk.T).reshape(b, L, H, Dh)
            v = (hidden_states @ Wv.T).reshape(b, L, H, Dh)
            scores = jnp.einsum('bnhd,bmhd->bhnm', q, k) / jnp.sqrt(jnp.float32(Dh))
            idx = jnp.arange(L)
            causal = idx[:, None] >= idx[None, :]
            dblk = (idx // seg)[:, None] - (idx // seg)[None, :]
            neg = jnp.float32(-jnp.inf)
            scores = jnp.where(causal, scores, neg)
            terrace_allowed = causal & ((dblk == 0) | (dblk == 1))
            scores_t = jnp.where(terrace_allowed, scores, neg)
            att_t = jax.nn.softmax(scores_t, axis=-1)
            out_t = jnp.einsum('bhnm,bmhd->bhnd', att_t, v).reshape(b, H, r, seg, Dh)
            att = jax.nn.softmax(scores, axis=-1)
            awc = att.reshape(b, H, r, seg, L) * jnp.exp(index_decays)[None, :, None, :, None]
            pcs = awc.sum(axis=-2)
            mega = jnp.clip(jnp.exp(mega_decays * seg), 0.0, 2.0)
            s_seq = jnp.moveaxis(pcs, 2, 0)

            def step(carry, s):
                return (carry * mega[None, :, None] + s, carry)
            _, outs = jax.lax.scan(step, jnp.zeros_like(s_seq[0]), s_seq)
            w = jnp.moveaxis(outs, 0, 2)
            w = w / (w.sum(axis=-1, keepdims=True) + NOISE_EPS)
            kv = jnp.einsum('bhrs,bshd,bshe->brhde', w, k, v)
            qc = q.reshape(b, r, seg, H, Dh)
            out_lin = jnp.einsum('brlhd,brhde->bhrle', qc, kv)
            tw = jax.nn.sigmoid(terrace_mix)[None, None, None, :, None]
            y = tw * out_t + (1.0 - tw) * out_lin
            y = y.reshape(b, H, L, Dh).transpose(0, 2, 1, 3).reshape(b, L, d)
            return y @ Wc.T
        return _forward(hidden_states, Wq, Wk, Wv, Wc, terrace_mix, index_decays, mega_decays)

    def _L0_attn_b_ref(x, w_gate, w_q, w_k, w_v, w_gk1, w_gk2, b_gk, w_ks, w_vs, w_gk1s, w_gk2s, b_gks, w_g, w_o, norm_w):
        import jax, jax.numpy as jnp
        import numpy as np
        import math
        NUM_HEADS = 4
        NUM_MEM = 4
        TOPK = 2
        CAPACITY = 0.5
        GATE_NORM = 16.0
        EPS = 1e-05
        B, S, D = (4, 512, 256)
        DK, DV = (128, 256)
        HDK, HDV = (DK // NUM_HEADS, DV // NUM_HEADS)
        LOW = 16

        def _transform(x, routing_mask, sel):
            b, s0, d = x.shape
            k = sel.shape[2]
            xr = jnp.repeat(x, k, axis=1)
            s = s0 * k
            mem_flat = sel.reshape(b, -1).reshape(-1)
            batch_idx = jnp.repeat(jnp.arange(b), s)
            combined = batch_idx * NUM_MEM + mem_flat
            sorted_idx = jnp.argsort(combined)
            x_sorted = xr.reshape(b * s, d)[sorted_idx]
            counts = routing_mask.sum(1)
            offset = jnp.cumsum(counts, axis=1)
            flat_off = (offset + jnp.arange(b)[:, None] * s).reshape(-1)
            cap_len = math.ceil(s0 * CAPACITY)
            prev = jnp.concatenate([jnp.zeros((1,), flat_off.dtype), flat_off[:-1]])
            idx = jnp.arange(cap_len)[None, :] + prev[:, None]
            trunc = idx + counts.reshape(-1)[:, None] - cap_len
            mask = (trunc < flat_off[:, None]) & (trunc >= 0) & (trunc >= prev[:, None])
            trunc = jnp.where(mask, trunc, 0)
            gathered = x_sorted[trunc.reshape(-1)]
            tx = gathered.reshape(b * NUM_MEM, cap_len, d) * mask[..., None]
            tx = tx.reshape(b, NUM_MEM, cap_len, d).transpose(1, 0, 2, 3)
            return (tx, trunc, sorted_idx, mask)

        def _reconstruct(ty, trunc, sorted_idx, rw, mask, b, s0):
            M, _, cap, H, dv = ty.shape
            g = ty.transpose(1, 0, 2, 3, 4).reshape(b * M * cap, H, dv)
            g = g * mask.reshape(-1)[:, None, None]
            res = jnp.zeros((b * s0 * TOPK, H, dv), ty.dtype).at[trunc.reshape(-1)].add(g)
            inv = jnp.argsort(sorted_idx)
            out = res[inv].reshape(b, s0, TOPK, H, dv)
            return (out * rw[..., None, None]).sum(2)

        def _gla(q, k, v, gk):

            def step(Smat, inp):
                qt, kt, vt, gt = inp
                Smat = Smat * jnp.exp(gt)[..., None] + kt[..., None] * vt[..., None, :]
                o = jnp.einsum('...k,...kv->...v', qt, Smat)
                return (Smat, o)
            S0 = jnp.zeros(q.shape[1:-1] + (q.shape[-1], v.shape[-1]), q.dtype)
            _, o = jax.lax.scan(step, S0, (q, k, v, gk))
            return o

        def _forward(x, w_gate, w_q, w_k, w_v, w_gk1, w_gk2, b_gk, w_ks, w_vs, w_gk1s, w_gk2s, b_gks, w_g, w_o, norm_w):
            b, s0, d = x.shape
            scale = HDK ** (-0.5)
            probs = jax.nn.softmax(x @ w_gate, -1)
            rw, sel = jax.lax.top_k(probs, TOPK)
            rw = rw / rw.sum(-1, keepdims=True)
            routing_mask = jax.nn.one_hot(sel, NUM_MEM, dtype=jnp.int32).sum(2)
            tx, trunc, sorted_idx, mask = _transform(x, routing_mask, sel)
            cap = tx.shape[2]
            q = jnp.einsum('mbtd,dk->mbtk', tx, w_q).reshape(NUM_MEM, b, cap, NUM_HEADS, HDK) * scale
            k = jnp.einsum('mbtd,mdk->mbtk', tx, w_k).reshape(NUM_MEM, b, cap, NUM_HEADS, HDK)
            v = jnp.einsum('mbtd,mdk->mbtk', tx, w_v).reshape(NUM_MEM, b, cap, NUM_HEADS, HDV)
            gk = jnp.einsum('mbtr,mrk->mbtk', jnp.einsum('mbtd,mdr->mbtr', tx, w_gk1), w_gk2) + b_gk[:, None, None, :]
            gk = (jax.nn.log_sigmoid(gk) / GATE_NORM).reshape(NUM_MEM, b, cap, NUM_HEADS, HDK)
            to_t = lambda a: jnp.moveaxis(a, 2, 0)
            o_mem = jnp.moveaxis(_gla(to_t(q), to_t(k), to_t(v), to_t(gk)), 0, 2)
            o_rout = _reconstruct(o_mem, trunc, sorted_idx, rw, mask, b, s0)
            qs = (x @ w_q).reshape(b, s0, NUM_HEADS, HDK) * scale
            ks = (x @ w_ks).reshape(b, s0, NUM_HEADS, HDK)
            vs = (x @ w_vs).reshape(b, s0, NUM_HEADS, HDV)
            gks = (jax.nn.log_sigmoid(x @ w_gk1s @ w_gk2s + b_gks) / GATE_NORM).reshape(b, s0, NUM_HEADS, HDK)
            tt = lambda a: jnp.moveaxis(a, 1, 0)
            o_sh = jnp.moveaxis(_gla(tt(qs), tt(ks), tt(vs), tt(gks)), 0, 1)
            o = o_rout + o_sh
            g = (x @ w_g).reshape(b, s0, NUM_HEADS, HDV)
            o = o * jax.lax.rsqrt(jnp.mean(o * o, -1, keepdims=True) + EPS) * norm_w
            o = o * (g * jax.nn.sigmoid(g))
            return o.reshape(b, s0, DV) @ w_o
        return _forward(x, w_gate, w_q, w_k, w_v, w_gk1, w_gk2, b_gk, w_ks, w_vs, w_gk1s, w_gk2s, b_gks, w_g, w_o, norm_w)

    def _L0_ffn_ref(hidden_states, gate_w, w_gate, w_up, w_down, ws_gate, ws_up, ws_down):
        import jax, jax.numpy as jnp
        import numpy as np
        H = 256
        M = 128
        E = 16
        TOP_K = 2
        SCALE = 2.5
        NORM_TOPK = True
        B, S = (1, 256)

        def _moe(x, gate_w, w_gate, w_up, w_down, ws_gate, ws_up, ws_down):
            T = x.shape[0]
            shared = jax.nn.silu(x @ ws_gate) * (x @ ws_up) @ ws_down
            scores = jax.nn.sigmoid(x.astype(jnp.float32) @ gate_w.T.astype(jnp.float32))
            topk_w, topk_idx = jax.lax.top_k(scores, TOP_K)
            if NORM_TOPK and TOP_K > 1:
                topk_w = topk_w / (topk_w.sum(-1, keepdims=True) + 1e-20)
            topk_w = topk_w * SCALE
            route = jnp.zeros((T, E), topk_w.dtype).at[jnp.arange(T)[:, None], topk_idx].set(topk_w)
            g = jnp.einsum('th,ehm->etm', x, w_gate)
            u = jnp.einsum('th,ehm->etm', x, w_up)
            eo = jnp.einsum('etm,emh->eth', jax.nn.silu(g) * u, w_down)
            routed = jnp.einsum('te,eth->th', route.astype(x.dtype), eo)
            return routed + shared
        b, s, h = hidden_states.shape
        x = hidden_states.reshape(-1, h)
        out = _moe(x, gate_w, w_gate, w_up, w_down, ws_gate, ws_up, ws_down)
        return out.reshape(b, s, h)
    x = L0_attn_a_hidden_states
    x = x + _L0_attn_a_ref(_layernorm(x, axis=-1), L0_attn_a_Wq, L0_attn_a_Wk, L0_attn_a_Wv, L0_attn_a_Wc, L0_attn_a_terrace_mix, L0_attn_a_index_decays, L0_attn_a_mega_decays)
    x = x + _L0_ffn_ref(_layernorm(x, axis=-1), L0_ffn_gate_w, L0_ffn_w_gate, L0_ffn_w_up, L0_ffn_w_down, L0_ffn_ws_gate, L0_ffn_ws_up, L0_ffn_ws_down)
    x = x + _L0_attn_b_ref(_layernorm(x, axis=-1), L0_attn_b_w_gate, L0_attn_b_w_q, L0_attn_b_w_k, L0_attn_b_w_v, L0_attn_b_w_gk1, L0_attn_b_w_gk2, L0_attn_b_b_gk, L0_attn_b_w_ks, L0_attn_b_w_vs, L0_attn_b_w_gk1s, L0_attn_b_w_gk2s, L0_attn_b_b_gks, L0_attn_b_w_g, L0_attn_b_w_o, L0_attn_b_norm_w)
    x = x + _L0_ffn_ref(_layernorm(x, axis=-1), L0_ffn_gate_w, L0_ffn_w_gate, L0_ffn_w_up, L0_ffn_w_down, L0_ffn_ws_gate, L0_ffn_ws_up, L0_ffn_ws_down)
    return x

_drawn_inputs = setup_inputs


def setup_inputs(seed=0):
    import zlib

    import numpy as np

    out = dict(_drawn_inputs(seed))
    spreads = {'L0_attn_a_terrace_mix': (0.5, 0.6), 'L0_attn_b_norm_w': (1.0, 0.6)}
    factors = {'L0_attn_a_Wq': 8.0,
     'L0_attn_a_Wk': 8.0,
     'L0_attn_a_Wv': 6.754,
     'L0_attn_a_Wc': 6.847,
     'L0_attn_a_index_decays': 8.0,
     'L0_attn_a_mega_decays': 8.0,
     'L0_attn_b_w_gk1': 64.0,
     'L0_attn_b_w_gk2': 64.0,
     'L0_attn_b_b_gk': 64.0,
     'L0_attn_b_w_gk1s': 64.0,
     'L0_attn_b_w_gk2s': 64.0,
     'L0_attn_b_b_gks': 64.0,
     'L0_attn_b_w_gate': 8.0,
     'L0_attn_b_w_q': 6.509,
     'L0_attn_b_w_k': 8.0,
     'L0_attn_b_w_v': 8.0,
     'L0_attn_b_w_ks': 8.0,
     'L0_attn_b_w_vs': 8.0,
     'L0_attn_b_w_g': 6.515,
     'L0_attn_b_w_o': 6.474,
     'L0_ffn_gate_w': 8.0,
     'L0_ffn_w_gate': 8.0,
     'L0_ffn_w_up': 8.0,
     'L0_ffn_w_down': 8.0,
     'L0_ffn_ws_gate': 8.0,
     'L0_ffn_ws_up': 8.0,
     'L0_ffn_ws_down': 8.0}
    for name, (base, spread) in spreads.items():
        noise = np.random.default_rng([zlib.crc32(name.encode()), seed]).standard_normal(out[name].shape)
        drawn = base * np.exp(spread * noise) if base else spread * noise
        out[name] = jnp.asarray(drawn.astype(out[name].dtype))
    for name, factor in factors.items():
        out[name] = (out[name] * factor).astype(out[name].dtype)
    return out
```

```python
import numpy as np
import concourse.bass as bass
from concourse import mybir
from contextlib import ExitStack

F32 = mybir.dt.float32
BF16 = mybir.dt.bfloat16
U32 = mybir.dt.uint32
ALU = mybir.AluOpType
ACT = mybir.ActivationFunctionType
AX = mybir.AxisListType
ds = bass.ds

P = 128
B, L, D = 2, 2048, 256
T = B * L
KC = D // P
NT = L // P
LN_EPS = 1e-5

H, DH, SEG = 16, 16, 64
R = L // SEG
HH = H // 2
NOISE_EPS = 1e-5
MASKED = -1.0e30
CW = 1024
Q_PARTS = ((0, 3), (0, 2), (0, 1))
K_REPS = (3, 2, 1)
SLOTS = 6


class Mem:

    def __init__(self, nc, ctx, tag):
        self.nc, self.ctx, self.tag = nc, ctx, tag
        self.sems = []
        ctx.callback(self.clear)

    def sb(self, name, shape, dt=F32):
        return self.ctx.enter_context(self.nc.sbuf_tensor(self.tag + name, shape, dt))

    def ps(self, name, shape, dt=F32):
        return self.ctx.enter_context(self.nc.psum_tensor(self.tag + name, shape, dt))

    def sem(self, name):
        self.sems.append(self.nc.alloc_semaphore(self.tag + name))
        return self.sems[-1]

    def clear(self):
        self.nc.clear_and_free_semaphores(self.sems)
        self.nc.all_engine_barrier()


def wait_here(eng, sem, value, passed):
    eng.wait_ge(sem, value)
    eng.sem_inc(passed, 1)


def rows(dram, at, tiles):
    return dram[ds(at, tiles * P), :].rearrange("(t p) n -> p t n", p=P)


def make_identity(pool, ident, made):
    pool.memset(ident[:, :], 0.0).then_inc(made, 1)
    pool.wait_ge(made, 1)
    pool.affine_select(out=ident[:, :], in_=ident[:, :], compare_op=ALU.not_equal, fill=1.0, base=0,
                       pattern=[[-1, P]], channel_multiplier=1).then_inc(made, 1)


def phase_project(nc, x, wq, wk, wkv, q_parts, k_parts, q_full, k_tok, v_tok):
    with ExitStack() as ctx:
        m = Mem(nc, ctx, "pj_")
        G = 4
        W = G * P
        ident = m.sb("ident", [P, P])
        wq_s, wk_s = m.sb("wq", [P, KC, D]), m.sb("wk", [P, KC, D])
        wkv_s = m.sb("wkv", [P, KC, 2 * D])
        x_s = m.sb("x", [P, G, D])
        stats, mv = m.sb("stats", [P, G, 6]), m.sb("mv", [P, G, 2])
        std, rstd = m.sb("std", [P, G]), m.sb("rstd", [P, G])
        eps = m.sb("eps", [P, 1])
        hn = m.sb("hn", [P, G, D])
        hT = m.sb("hT", [P, KC, W])
        full = m.sb("full", [P, 4, W])
        part = m.sb("part", [P, 4, 3, W], BF16)
        rest = m.sb("rest", [P, 2, W])
        kv = m.sb("kv", [P, 2, B, H, NT * DH])
        p_T = m.ps("T", [P, KC, W])
        p_qk = [m.ps(f"qk{j}", [P, W]) for j in range(4)]
        p_kv = [m.ps(f"kv{j}", [P, 2 * D]) for j in range(2)]
        w_in, x_in = m.sem("w_in"), m.sem("x_in")
        made, eps_set = m.sem("made"), m.sem("eps_set")
        stat_done, var_done, std_done, rstd_done = m.sem("stat"), m.sem("var"), m.sem("std"), m.sem("rstd")
        hn_done, T_done, hT_done = m.sem("hn"), m.sem("T"), m.sem("hT")
        qk_done, full_done, kv_done, kv_kept = m.sem("qk"), m.sem("full"), m.sem("kv_mm"), m.sem("kv_kept")
        part_done, stored, kv_stored = m.sem("part"), m.sem("stored"), m.sem("kv_stored")
        steps = L // W
        NS = B * steps
        sp_passed, dve_passed = m.sem("sp_passed"), m.sem("dve_passed")
        block = ctx.enter_context(nc.Block())

        @block.sync
        def _(sp):
            sp.dma_start(wq_s[:, :, :], wq).then_inc(w_in, 16)
            sp.dma_start(wk_s[:, :, :], wk).then_inc(w_in, 16)
            sp.dma_start(wkv_s[:, :, :], wkv).then_inc(w_in, 16)
            sp.sem_inc(hn_done, 1)
            sp.sem_inc(stored, 1)
            with sp.Fori(0, B) as b:
                with sp.Fori(0, steps) as st:
                    n = b * steps + st
                    wait_here(sp, hn_done, n * G + 1, sp_passed)
                    sp.dma_start(x_s[:, :, :], rows(x, b * L + st * W, G)).then_inc(x_in, 16)
                    for j in range(4):
                        wait_here(sp, part_done, n * 16 + 4 * j + 4, sp_passed)
                        dst, half = (q_parts, k_parts)[j // 2], j % 2 * P
                        sp.dma_start(dst[:, ds(b * D + half, P), ds(st * W, W)].rearrange("s p t -> p s t"),
                                     part[:, j, :, :]).then_inc(stored, 16)
                        if j < 2:
                            sp.dma_start(q_full[half:half + P, ds(b * L + st * W, W)], full[:, j, :]).then_inc(stored, 16)
            sp.wait_ge(kv_kept, NS * G + 2)
            for j, dst in enumerate((k_tok, v_tok)):
                sp.dma_start(dst.rearrange("h p n -> p h n"),
                             kv[:, j, :, :, :].rearrange("p b h n -> p (b h) n")).then_inc(kv_stored, 16)
            sp.wait_ge(kv_stored, 32)
            sp.wait_ge(stored, NS * 96 + 1)

        @block.gpsimd
        def _(pool):
            make_identity(pool, ident, made)
            pool.memset(eps[:, :], LN_EPS).then_inc(eps_set, 1)

        @block.vector
        def _(dve):
            with dve.Fori(0, NS) as n:
                dve.wait_ge(x_in, n * 16 + 16)
                for t in range(G):
                    nc.vector.bn_stats(stats[:, t, :], x_s[:, t, :]).then_inc(stat_done, 1)
                wait_here(dve, stat_done, n * G + G, dve_passed)
                for t in range(G):
                    nc.vector.bn_aggr(mv[:, t, :], stats[:, t, :]).then_inc(var_done, 1)
                dve.wait_ge(std_done, n + 1)
                nc.vector.reciprocal(rstd[:, :], std[:, :]).then_inc(rstd_done, 1)
                dve.wait_ge(rstd_done, n + 1)
                for t in range(G):
                    ins = nc.vector.tensor_scalar(hn[:, t, :], x_s[:, t, :], mv[:, t, 0:1], rstd[:, t:t + 1],
                                                  ALU.subtract, ALU.mult)
                    ins.then_inc(hn_done, 1)
                dve.wait_ge(stored, n * 96 + 1)
                for j in range(4):
                    dve.wait_ge(full_done, n * 4 + j + 1)
                    nc.vector.tensor_copy(part[:, j, 0, :], full[:, j, :]).then_inc(part_done, 1)
                    dve.wait_ge(part_done, n * 16 + 4 * j + 1)
                    nc.vector.tensor_tensor(rest[:, j % 2, :], full[:, j, :], part[:, j, 0, :],
                                            ALU.subtract).then_inc(part_done, 1)
                    dve.wait_ge(part_done, n * 16 + 4 * j + 2)
                    nc.vector.tensor_copy(part[:, j, 1, :], rest[:, j % 2, :]).then_inc(part_done, 1)
                    dve.wait_ge(part_done, n * 16 + 4 * j + 3)
                    nc.vector.tensor_tensor(part[:, j, 2, :], rest[:, j % 2, :], part[:, j, 1, :],
                                            ALU.subtract).then_inc(part_done, 1)

        @block.scalar
        def _(act):
            act.wait_ge(eps_set, 1)
            with act.Fori(0, B) as b:
                with act.Fori(0, steps) as s:
                    n = b * steps + s
                    act.wait_ge(var_done, n * G + G)
                    nc.scalar.activation(std[:, :], mv[:, :, 1], ACT.Sqrt, bias=eps[:, 0:1]).then_inc(std_done, 1)
                    for k in range(KC):
                        act.wait_ge(T_done, n * KC + k + 1)
                        nc.scalar.copy(hT[:, k, :], p_T[:, k, :]).then_inc(hT_done, 1)
                    act.wait_ge(stored, n * 96 + 1)
                    for j in range(4):
                        act.wait_ge(qk_done, n * 4 + j + 1)
                        nc.scalar.copy(full[:, j, :], p_qk[j][:, :]).then_inc(full_done, 1)
                    for t in range(G):
                        act.wait_ge(kv_done, n * G + t + 1)
                        for j in range(2):
                            dst = kv[:, j, ds(b, 1), :, ds(s * (G * DH) + t * DH, DH)].rearrange(
                                "p a h e -> p (a h) e")
                            ins = nc.scalar.copy(dst, p_kv[t % 2][:, j * D:(j + 1) * D].rearrange(
                                "p (h e) -> p h e", h=H))
                        ins.then_inc(kv_kept, 1)

        @block.tensor
        def _(pe):
            pe.wait_ge(made, 2)
            pe.wait_ge(w_in, 48)
            pe.sem_inc(kv_kept, 2)
            with pe.Fori(0, NS) as n:
                pe.wait_ge(hn_done, n * G + G + 1)
                for k in range(KC):
                    for t in range(G):
                        ins = nc.tensor.transpose(p_T[:, k, t * P:(t + 1) * P], hn[:, t, k * P:(k + 1) * P], ident[:, :])
                    ins.then_inc(T_done, 1)
                pe.wait_ge(hT_done, n * KC + KC)
                for j in range(4):
                    w = (wq_s, wk_s)[j // 2]
                    for k in range(KC):
                        ins = nc.tensor.matmul(p_qk[j][:, :], w[:, k, (j % 2) * P:(j % 2 + 1) * P], hT[:, k, :],
                                               start=(k == 0), stop=(k == KC - 1))
                    ins.then_inc(qk_done, 1)
                for t in range(G):
                    pe.wait_ge(kv_kept, n * G + t + 1)
                    for k in range(KC):
                        ins = nc.tensor.matmul(p_kv[t % 2][:, :], hT[:, k, t * P:(t + 1) * P], wkv_s[:, k, :],
                                               start=(k == 0), stop=(k == KC - 1))
                    ins.then_inc(kv_done, 1)
                pe.wait_ge(full_done, n * 4 + 4)


def phase_attend(nc, q_parts, k_parts, k_tok, v_tok, terrace_mix, index_decays, mega_decays, y_dram, kv_dram):
    with ExitStack() as ctx:
        m = Mem(nc, ctx, "at_")
        SCALE = float(DH) ** -0.5
        TW = SEG + P
        KVW = DH * DH + 1
        chunks = [[(c, min(CW, i * P - c)) for c in range(0, i * P, CW)] for i in range(NT)]
        first_chunk = [sum(len(c) for c in chunks[:i]) for i in range(NT + 1)]
        NCH = first_chunk[NT]
        assert NCH % 2 == 0
        first_t = [0] + [1 + 2 * i for i in range(NT)]
        NTX = first_t[NT]
        ident = m.sb("ident", [P, P])
        mask = m.sb("mask", [P, TW])
        tw, tmix = m.sb("tw", [P, 1]), m.sb("tmix", [P, 1])
        dec = m.sb("dec", [P, H])
        eid = m.sb("eid", [P, H, 2])
        lam, lam_raw = m.sb("lam", [R, H]), m.sb("lam_raw", [R, H])
        gap = m.sb("gap", [R, R])
        gap_i = m.sb("gap_i", [R, R], mybir.dt.int32)
        decay = m.sb("decay", [R, H, R])
        sq, sk = m.sb("sq", [SLOTS * DH, 2, L], BF16), m.sb("sk", [SLOTS * DH, 2, L], BF16)
        kh, vh = m.sb("kh", [P, 2, NT * DH]), m.sb("vh", [P, 2, NT * DH])
        vs = m.sb("vs", [SEG, 2, NT * DH])
        kvo = m.sb("kvo", [P, NT, KVW])
        eid_h, decay_h = m.sb("eid_h", [P, 2, 2]), m.sb("decay_h", [R, 2, R])
        E = m.sb("E", [P, 2, L])
        Wm = m.sb("Wm", [P, 2, TW])
        Tt = m.sb("Tt", [P, 2, TW])
        TTs = m.sb("TTs", [P, 2 * P])
        mx, nm = m.sb("mx", [P, NT, 4]), m.sb("nm", [P, NT, 4])
        top = m.sb("top", [P, NT])
        dm, f = m.sb("dm", [P, NT, 4]), m.sb("f", [P, NT, 4])
        rs, rp = m.sb("rs", [P, NT, 4]), m.sb("rp", [P, NT])
        fr, tot, inv = m.sb("fr", [P, NT, 4]), m.sb("tot", [P, NT, 2]), m.sb("inv", [P, NT, 2])
        c2 = m.sb("c2", [P, 2, 3, 2])
        Y_h = m.sb("Y_h", [P, 2, NT, DH])
        Y = m.sb("Y", [P, B, NT, D])
        pcs_s = m.sb("pcs_s", [P, NT * R])
        kvr, kvn = m.sb("kvr", [R, KVW]), m.sb("kvn", [R, 2, DH * DH])
        den, rden = m.sb("den", [R, 1]), m.sb("rden", [R, 1])
        S = [m.ps(f"S{j}", [P, CW]) for j in range(2)]
        S_W = m.ps("S_W", [P, 512])
        TT = m.ps("TT", [P, 512])
        pcs = m.ps("pcs", [P, NT * R])
        misc = m.ps("misc", [P, 512])

        made, cin, cdone = m.sem("made"), m.sem("const_in"), m.sem("const_done")
        loaded = [m.sem(f"loaded{u}") for u in range(2)]
        LOADS = 16 * (2 * SLOTS + 3)
        passed = m.sem("passed")
        pool_passed = m.sem("pool_passed")
        s_small, s_kvo = m.sem("small"), m.sem("kvo")
        s_S, s_E = m.sem("S_done"), m.sem("E_done")
        s_W, s_T = m.sem("W_done"), m.sem("T_done")
        s_mx, s_nm = m.sem("mx"), m.sem("nm")
        s_dm, s_f, s_c2 = m.sem("dm"), m.sem("f"), m.sem("c2")
        s_step = m.sem("step")
        s_TT, s_TTs = m.sem("TT"), m.sem("TTs")
        s_P, s_O, s_Oe = m.sem("pcs_mm"), m.sem("O"), m.sem("O_read")
        s_pc, s_KV, s_kvr, s_K2 = m.sem("pcs_copy"), m.sem("KV"), m.sem("kvr"), m.sem("KV2")
        s_den, s_kvn = m.sem("den"), m.sem("kvn")
        s_Y, y_out = m.sem("Y"), m.sem("y_out")
        s_top, s_Wm = m.sem("top"), m.sem("W_read")
        kv_out = [m.sem(f"kv_out{u}") for u in range(2)]
        dve_passed, pe_passed = m.sem("dve_passed"), m.sem("pe_passed")
        E_CR, W_CR, T_CR, P_CR, O_CR = 2, 1, 2, 2, 1
        KV_CR, K2_CR, Y_CR, KVN_CR, PC_CR, TTS_CR, OUT_CR = 1, 2, 2, 1, 1, 1, 1
        NHEAD = B * H
        block = ctx.enter_context(nc.Block())

        @block.sync
        def _(sp):
            for u in range(2):
                sp.dma_start(tmix[u * SEG:(u + 1) * SEG, :], terrace_mix).then_inc(cin, 16)
                sp.dma_start(dec[u * SEG:(u + 1) * SEG, :], index_decays).then_inc(cin, 16)
            sp.dma_start(lam_raw[:, :], mega_decays.to_broadcast([R, H])).then_inc(cin, 16)
            for sem, credits in ((s_E, E_CR), (s_Wm, W_CR), (s_T, T_CR), (s_P, P_CR), (s_O, O_CR), (s_KV, KV_CR),
                                 (s_K2, K2_CR), (s_Y, Y_CR), (s_kvn, KVN_CR), (s_pc, PC_CR), (s_TTs, TTS_CR),
                                 (kv_out[0], OUT_CR), (kv_out[1], OUT_CR)):
                sp.sem_inc(sem, credits)

            def load(head, u):
                slot = 0
                for lo, hi in Q_PARTS:
                    for part in range(lo, hi):
                        sp.dma_start(sq[slot * DH:(slot + 1) * DH, u, :],
                                     q_parts[part, ds(head * DH, DH), :]).then_inc(loaded[u], 16)
                        slot += 1
                slot = 0
                for part, reps in enumerate(K_REPS):
                    for _ in range(reps):
                        sp.dma_start(sk[slot * DH:(slot + 1) * DH, u, :],
                                     k_parts[part, ds(head * DH, DH), :]).then_inc(loaded[u], 16)
                        slot += 1
                for dst, src in ((kh[:, u, :], k_tok[ds(head, 1), :, :]), (vh[:, u, :], v_tok[ds(head, 1), :, :]),
                                 (vs[:, u, DH:NT * DH], v_tok[ds(head, 1), SEG:P, 0:(NT - 1) * DH])):
                    sp.dma_start(dst, src.rearrange("a p n -> (a p) n")).then_inc(loaded[u], 16)

            def store(head, u):
                wait_here(sp, s_kvn, KVN_CR + head + 1, passed)
                sp.dma_start(kv_dram[ds(head, 1), :, :].rearrange("a r n -> (a r) n"), kvn[:, u, :]
                             ).then_inc(kv_out[u], 16)

            load(0, 0)
            load(1, 1)
            with sp.Fori(0, NHEAD // 2 - 1) as q:
                for u in range(2):
                    store(q * 2 + u, u)
                    load(q * 2 + (u + 2), u)
            for u in range(2):
                store(NHEAD - 2 + u, u)
            sp.wait_ge(s_Y, Y_CR + NHEAD)
            for b in range(B):
                sp.dma_start(y_dram[b * L:(b + 1) * L, :].rearrange("(t p) n -> p t n", p=P),
                             Y[:, b, :, :]).then_inc(y_out, 16)
            sp.wait_ge(y_out, 16 * B)
            for u in range(2):
                sp.wait_ge(kv_out[u], OUT_CR + 8 * NHEAD)

        @block.gpsimd
        def _(pool):
            make_identity(pool, ident, made)
            pool.memset(mask[:, :], 0.0).then_inc(made, 1)
            pool.wait_ge(made, 3)
            pool.affine_select(out=mask[:, :], in_=mask[:, :], compare_op=ALU.is_ge, fill=MASKED, base=SEG,
                               pattern=[[-1, TW]], channel_multiplier=1).then_inc(made, 1)
            pool.wait_ge(made, 4)
            pool.memset(mask[SEG:P, 0:SEG], MASKED).then_inc(made, 1)
            pool.wait_ge(made, 5)
            pool.memset(eid[:, :, :], 0.0).then_inc(made, 1)
            pool.iota(gap_i[:, :], pattern=[[1, R]], base=-1, channel_multiplier=-1).then_inc(made, 1)
            pool.memset(kvo[:, :, DH * DH:KVW], 1.0).then_inc(made, 1)
            pool.wait_ge(cdone, 3 + H)
            pool.affine_select(out=decay[:, :, :], in_=decay[:, :, :], compare_op=ALU.is_gt, fill=0.0, base=0,
                               pattern=[[0, H], [1, R]], channel_multiplier=-1).then_inc(made, 1)
            pool.wait_ge(made, 9)
            with pool.Fori(0, B) as b:
                with pool.Fori(0, H // 2) as hp:
                    for u in range(2):
                        n = b * H + hp * 2 + u
                        wait_here(pool, s_K2, K2_CR - 1 + n, pool_passed)
                        pool.tensor_copy(eid_h[:, u, :], eid[:, ds(hp * 2 + u, 1), :].rearrange("p a c -> p (a c)")
                                         ).then_inc(s_small, 1)
                        pool.tensor_copy(decay_h[:, u, :], decay[:, ds(hp * 2 + u, 1), :].rearrange("p a c -> p (a c)")
                                         ).then_inc(s_small, 1)
                        pool.wait_ge(loaded[u], (b * (H // 2) + hp) * LOADS + LOADS)
                        pool.sem_inc(pool_passed, 1)
                        wait_here(pool, s_KV, KV_CR + n, pool_passed)
                        k3 = kh[:, u, :].rearrange("p (t d) -> p t d", t=NT)
                        v3 = vh[:, u, :].rearrange("p (t d) -> p t d", t=NT)
                        for t in range(NT):
                            ins = pool.tensor_tensor(
                                out=kvo[:, t, 0:DH * DH].rearrange("p (d e) -> p d e", d=DH),
                                in0=k3[:, t, :].unsqueeze(2).to_broadcast([P, DH, DH]),
                                in1=v3[:, t, :].unsqueeze(1).to_broadcast([P, DH, DH]), op=ALU.mult)
                        ins.then_inc(s_kvo, 1)
                        wait_here(pool, s_Oe, n * NT + NT, pool_passed)
                        pool.tensor_copy(Y[:, ds(b, 1), :, ds(hp * (2 * DH) + u * DH, DH)].rearrange(
                            "p a t e -> p (a t) e"), Y_h[:, u, :, :]).then_inc(s_Y, 1)

        @block.scalar
        def _(act):
            act.wait_ge(cin, 80)
            act.wait_ge(made, 8)
            nc.scalar.activation(tw[:, :], tmix[:, :], ACT.Sigmoid).then_inc(cdone, 1)
            for u in range(2):
                nc.scalar.activation(eid[u * SEG:(u + 1) * SEG, :, u], dec[u * SEG:(u + 1) * SEG, :],
                                     ACT.Exp).then_inc(cdone, 1)
            act.wait_ge(s_den, 3)
            for h in range(H):
                nc.scalar.activation(decay[:, h, :], gap[:, :], ACT.Exp, scale=lam[:, h:h + 1]).then_inc(cdone, 1)

            def window(n, i, u):
                for j, (lo, hi) in enumerate(((0, SEG), (SEG, TW))):
                    if i == 0 and j == 0:
                        continue
                    acc = rp[:, i:i + 1] if j == 0 else rs[:, i, 0:1]
                    nc.scalar.activation(Tt[:, i % 2, lo:hi], Wm[:, i % 2, lo:hi], ACT.Exp, bias=nm[:, i, 0:1],
                                         scale=SCALE, accum_out=acc).then_inc(s_T, 1)

            def keep_transposed(n, i):
                act.wait_ge(s_TT, n * NT + i + 1)
                act.wait_ge(s_O, O_CR + n * NT + i)
                if i:
                    nc.scalar.copy(TTs[:, P:2 * P], TT[:, P:2 * P])
                    nc.scalar.copy(TTs[0:SEG, 0:P], TT[0:SEG, 0:P]).then_inc(s_TTs, 1)
                else:
                    nc.scalar.copy(TTs[:, P:2 * P], TT[:, P:2 * P]).then_inc(s_TTs, 1)

            with act.Fori(0, B) as b:
                with act.Fori(0, H // 2) as hp:
                    for u in range(2):
                        n = b * H + hp * 2 + u
                        for i in range(NT):
                            act.wait_ge(s_nm, n * NT + i + 1)
                            act.wait_ge(s_P, P_CR - 1 + n * NT + i)
                            for j, (c0, w) in enumerate(chunks[i]):
                                g = first_chunk[i] + j
                                nc.scalar.activation(E[:, i % 2, c0:c0 + w], S[g % 2][:, 0:w], ACT.Exp,
                                                     bias=nm[:, i, 1 + j:2 + j], scale=SCALE,
                                                     accum_out=rs[:, i, 1 + j:2 + j]).then_inc(s_E, 1)
                            if i:
                                keep_transposed(n, i - 1)
                            window(n, i, u)
                            act.wait_ge(s_dm, n * NT + i + 1)
                            k = 1 + len(chunks[i])
                            nc.scalar.activation(f[:, i, 0:k], dm[:, i, 0:k], ACT.Exp).then_inc(s_f, 1)
                        keep_transposed(n, NT - 1)

        @block.vector
        def _(dve):
            nc.vector.memset(pcs[:, :], 0.0).then_inc(s_den, 1)
            dve.wait_ge(cin, 80)
            dve.wait_ge(made, 8)
            nc.vector.tensor_scalar(lam[:, :], lam_raw[:, :], float(SEG), float(np.log(2.0)), ALU.mult,
                                    ALU.min).then_inc(s_den, 1)
            nc.vector.tensor_scalar(gap[:, :], gap_i[:, :], 0.0, None, ALU.max).then_inc(s_den, 1)
            dve.wait_ge(s_den, 3)
            dve.wait_ge(cdone, 1)
            DEN0 = 3

            def maxima(n, i):
                for j, (c0, w) in enumerate(chunks[i]):
                    g = first_chunk[i] + j
                    dve.wait_ge(s_S, n * NCH + g + 1)
                    nc.vector.tensor_reduce(mx[:, i, 1 + j:2 + j], S[g % 2][:, 0:w], AX.X, ALU.max).then_inc(s_mx, 1)
                lo = 0 if i else SEG
                dve.wait_ge(s_W, n * NT + i + 1)
                wait_here(dve, s_T, T_CR + n * NTX + (first_t[i - 1] if i else first_t[NT - 1] - NTX), dve_passed)
                nc.vector.tensor_tensor_reduce(
                    out=Wm[:, i % 2, lo:TW], in0=S_W[:, lo:TW], in1=mask[:, lo:TW], scale=1.0,
                    scalar=-3.0e38, op0=ALU.add, op1=ALU.max, accum_out=mx[:, i, 0:1]).then_inc(s_Wm, 1)
                dve.wait_ge(s_Wm, W_CR + n * NT + i + 1)
                if i:
                    dve.wait_ge(s_mx, n * NCH + first_chunk[i + 1])
                k = 1 + len(chunks[i])
                nc.vector.tensor_scalar(nm[:, i, 0:k], mx[:, i, 0:k], -SCALE, None, ALU.mult).then_inc(s_nm, 1)
                nc.vector.tensor_reduce(top[:, i:i + 1], mx[:, i, 0:k], AX.X, ALU.max).then_inc(s_top, 1)
                dve.wait_ge(s_top, n * NT + i + 1)
                nc.vector.tensor_scalar(dm[:, i, 0:k], mx[:, i, 0:k], top[:, i:i + 1], SCALE, ALU.subtract,
                                        ALU.mult).then_inc(s_dm, 1)

            def weights(n, i, u):
                k = 1 + len(chunks[i])
                at = (n * NT + i) * 4
                dve.wait_ge(s_f, n * NT + i + 1)
                nc.vector.tensor_tensor_reduce(out=fr[:, i, 0:k], in0=f[:, i, 0:k], in1=rs[:, i, 0:k], scale=1.0,
                                               scalar=0.0, op0=ALU.mult, op1=ALU.add,
                                               accum_out=tot[:, i, 0:1]).then_inc(s_step, 1)
                if i:
                    nc.vector.tensor_tensor(tot[:, i, 1:2], rs[:, i, 0:1], rp[:, i:i + 1], ALU.add).then_inc(s_step, 1)
                else:
                    nc.vector.tensor_copy(tot[:, i, 1:2], rs[:, i, 0:1]).then_inc(s_step, 1)
                dve.wait_ge(s_step, at + 2)
                nc.vector.reciprocal(inv[:, i, :], tot[:, i, :]).then_inc(s_step, 1)
                dve.wait_ge(s_step, at + 3)
                nc.vector.tensor_scalar(fr[:, i, 0:k], f[:, i, 0:k], inv[:, i, 0:1], None, ALU.mult).then_inc(s_step, 1)
                dve.wait_ge(s_step, at + 4)
                dve.wait_ge(s_small, n * 2 + 2)
                dve.wait_ge(s_P, P_CR - 1 + n * NT + i)
                nc.vector.tensor_tensor(c2[:, i % 2, 0:k, :], fr[:, i, 0:k].unsqueeze(2).to_broadcast([P, k, 2]),
                                        eid_h[:, u, :].unsqueeze(1).to_broadcast([P, k, 2]), ALU.mult).then_inc(s_c2, 1)

            def terrace(n, i, u):
                dve.wait_ge(s_O, O_CR + n * NT + i + 1)
                nc.vector.tensor_scalar(Y_h[:, u, i, :], misc[:, 0:DH], inv[:, i, 1:2], tw[:, 0:1], ALU.mult,
                                        ALU.mult).then_inc(s_Oe, 1)

            with dve.Fori(0, B) as b:
                with dve.Fori(0, H // 2) as hp:
                    for u in range(2):
                        n = b * H + hp * 2 + u
                        wait_here(dve, s_Y, Y_CR - 1 + n, dve_passed)
                        maxima(n, 0)
                        for i in range(NT):
                            if i + 1 < NT:
                                maxima(n, i + 1)
                            weights(n, i, u)
                            if i:
                                terrace(n, i - 1, u)
                        dve.wait_ge(s_P, P_CR + n * NT + NT)
                        nc.vector.tensor_copy(pcs_s[:, :], pcs[:, :]).then_inc(s_pc, 1)
                        terrace(n, NT - 1, u)
                        dve.wait_ge(s_KV, KV_CR + n + 1)
                        nc.vector.tensor_copy(kvr[:, :], misc[0:R, 0:KVW]).then_inc(s_kvr, 1)
                        dve.wait_ge(s_K2, K2_CR + n + 1)
                        nc.vector.tensor_scalar(den[:, :], misc[0:R, DH * DH:KVW], NOISE_EPS, None,
                                                ALU.add).then_inc(s_den, 1)
                        dve.wait_ge(s_den, n * 2 + 1 + DEN0)
                        nc.vector.reciprocal(rden[:, :], den[:, :]).then_inc(s_den, 1)
                        dve.wait_ge(s_den, n * 2 + 2 + DEN0)
                        dve.wait_ge(kv_out[u], OUT_CR + (b * (H // 2) + hp) * 16)
                        nc.vector.tensor_scalar(kvn[:, u, :], misc[0:R, 0:DH * DH], rden[:, 0:1], None,
                                                ALU.mult).then_inc(s_kvn, 1)

        @block.tensor
        def _(pe):
            pe.wait_ge(made, 2)
            pe.wait_ge(s_den, 1)

            def scores(n, i, u):
                q = sq[:, u, i * P:(i + 1) * P]
                for j, (c0, w) in enumerate(chunks[i]):
                    g = first_chunk[i] + j
                    pe.wait_ge(s_E, E_CR - 1 + n * NCH + g)
                    for o in range(0, w, 512):
                        ww = min(512, w - o)
                        ins = nc.tensor.matmul(S[g % 2][:, o:o + ww], q, sk[:, u, c0 + o:c0 + o + ww], start=True, stop=True)
                    ins.then_inc(s_S, 1)
                lo = 0 if i else SEG
                pe.wait_ge(s_Wm, W_CR + n * NT + i)
                nc.tensor.matmul(S_W[:, lo:TW], q, sk[:, u, i * P - SEG + lo:(i + 1) * P], start=True,
                                 stop=True).then_inc(s_W, 1)

            def sums(n, i, u):
                pe.wait_ge(s_T, T_CR + n * NTX + first_t[i + 1])
                pe.wait_ge(s_TTs, TTS_CR + n * NT + i)
                ins = nc.tensor.transpose(TT[:, P:2 * P], Tt[:, i % 2, SEG:TW], ident[:, :])
                if i:
                    ins = nc.tensor.transpose(TT[0:SEG, 0:P], Tt[:, i % 2, 0:SEG], ident[:, :])
                ins.then_inc(s_TT, 1)
                pe.wait_ge(s_c2, n * NT + i + 1)
                if i == 0:
                    pe.wait_ge(s_pc, PC_CR + n)
                for k in range(i):
                    nc.tensor.matmul(pcs[:, k * R + 2 * i:k * R + 2 * i + 2], E[:, i % 2, k * P:(k + 1) * P],
                                     c2[:, i % 2, 1 + k * P // CW, :], start=True, stop=True)
                nc.tensor.matmul(pcs[:, i * R + 2 * i:i * R + 2 * i + 2], Tt[:, i % 2, SEG:TW], c2[:, i % 2, 0, :],
                                 start=True, stop=True).then_inc(s_P, 1)
                pe.wait_ge(s_TTs, TTS_CR + n * NT + i + 1)
                if i:
                    pe.wait_ge(s_Oe, n * NT + i)
                else:
                    pe.wait_ge(s_kvn, KVN_CR + n)
                ins = nc.tensor.matmul(misc[:, 0:DH], TTs[:, P:2 * P], vh[:, u, i * DH:(i + 1) * DH], start=True,
                                       stop=(i == 0))
                if i:
                    ins = nc.tensor.matmul(misc[:, 0:DH], TTs[0:SEG, 0:P], vs[:, u, i * DH:(i + 1) * DH],
                                           start=False, stop=True)
                ins.then_inc(s_O, 1)

            with pe.Fori(0, B) as b:
                with pe.Fori(0, H // 2) as hp:
                    for u in range(2):
                        n = b * H + hp * 2 + u
                        pe.wait_ge(loaded[u], (b * (H // 2) + hp) * LOADS + LOADS)
                        scores(n, 0, u)
                        for i in range(NT):
                            if i + 1 < NT:
                                scores(n, i + 1, u)
                            sums(n, i, u)
                        pe.wait_ge(s_pc, PC_CR + n + 1)
                        pe.wait_ge(s_kvo, n + 1)
                        pe.wait_ge(s_Oe, n * NT + NT)
                        for t in range(NT):
                            ins = nc.tensor.matmul(misc[0:R, 0:KVW], pcs_s[:, t * R:(t + 1) * R], kvo[:, t, :],
                                                   start=(t == 0), stop=(t == NT - 1))
                        ins.then_inc(s_KV, 1)
                        pe.wait_ge(s_kvr, n + 1)
                        wait_here(pe, s_small, n * 2 + 2, pe_passed)
                        nc.tensor.matmul(misc[0:R, 0:KVW], decay_h[:, u, :], kvr[:, :], start=True,
                                         stop=True).then_inc(s_K2, 1)


def phase_merge(nc, x, q_full, y_dram, kv_dram, terrace_mix, wc, x_out):
    with ExitStack() as ctx:
        m = Mem(nc, ctx, "mg_")
        ident = m.sb("ident", [P, P])
        wc_s = m.sb("wc", [P, KC, D])
        tmix, tw, keep = m.sb("tmix", [P, 1]), m.sb("tw", [P, 1]), m.sb("keep", [P, 1])
        qT = m.sb("qT", [P, 2, KC, P])
        y_in = m.sb("y_in", [P, 2, D])
        x_s = m.sb("x", [P, 2, D])
        state = m.sb("state", [P, 2, KC, 2, P])
        y = m.sb("y", [P, 2, D])
        yT = m.sb("yT", [P, 2, KC, P])
        z = m.sb("z", [P, 2, D])
        lin = [m.ps(f"lin{u}", [P, D]) for u in range(2)]
        p_T = [m.ps(f"T{u}", [P, KC, P]) for u in range(2)]
        p_z = [m.ps(f"z{u}", [P, D]) for u in range(2)]
        made, cin, cdone = m.sem("made"), m.sem("const_in"), m.sem("const_done")
        loaded = [m.sem(f"loaded{u}") for u in range(2)]
        stored = [m.sem(f"stored{u}") for u in range(2)]
        s_lin, s_y, s_T, s_yT, s_zmm, s_z = (m.sem(k) for k in ("lin", "y", "T", "yT", "zmm", "z"))
        sp_passed, act_passed = m.sem("sp_passed"), m.sem("act_passed")
        Z_CR, OUT_CR = 2, 1
        LOADS = 16 * (3 + H)
        kv_v = kv_dram.rearrange("(b j h) r (d e) -> b h d j r e", b=B, j=2, d=DH)
        block = ctx.enter_context(nc.Block())

        @block.sync
        def _(sp):
            for u in range(2):
                sp.dma_start(tmix[u * SEG:(u + 1) * SEG, :], terrace_mix).then_inc(cin, 16)
            sp.dma_start(wc_s[:, :, :], wc).then_inc(cin, 16)
            sp.sem_inc(s_z, Z_CR)
            sp.sem_inc(stored[0], OUT_CR)
            sp.sem_inc(stored[1], OUT_CR)
            sp.wait_ge(cdone, 3)
            with sp.Fori(0, B) as b:
                with sp.Fori(0, NT // 2) as tp:
                    for u in range(2):
                        n = b * NT + tp * 2 + u
                        wait_here(sp, s_z, Z_CR - 1 + n, sp_passed)
                        at = b * L + tp * (2 * P) + u * P
                        sp.dma_start(qT[:, u, :, :], q_full[:, ds(at, P)].rearrange("(k p) t -> p k t", k=KC)
                                     ).then_inc(loaded[u], 16)
                        sp.dma_start(y_in[:, u, :], y_dram[ds(at, P), :]).then_inc(loaded[u], 16)
                        sp.dma_start(x_s[:, u, :], x[ds(at, P), :]).then_inc(loaded[u], 16)
                        for h in range(HH):
                            for j in range(KC):
                                sp.dma_start(state[h * DH:(h + 1) * DH, u, j, :, h * DH:(h + 1) * DH],
                                             kv_v[ds(b, 1), h, :, j, ds(tp * 4 + u * 2, 2), :].rearrange(
                                                 "b d r e -> (b d) r e")).then_inc(loaded[u], 16)

        @block.gpsimd
        def _(pool):
            make_identity(pool, ident, made)
            pool.memset(state[:, :, :, :, :], 0.0).then_inc(cdone, 1)

        @block.scalar
        def _(act):
            act.wait_ge(cin, 48)
            nc.scalar.activation(tw[:, :], tmix[:, :], ACT.Sigmoid).then_inc(cdone, 1)
            with act.Fori(0, B * NT // 2) as q:
                for u in range(2):
                    n = q * 2 + u
                    act.wait_ge(s_T, n + 1)
                    nc.scalar.copy(yT[:, u, :, :], p_T[u][:, :, :]).then_inc(s_yT, 1)
                    at = q * (2 * P) + u * P
                    wait_here(act, s_z, Z_CR + n + 1, act_passed)
                    act.dma_start(x_out[ds(at, P), :], z[:, u, :]).then_inc(stored[u], 16)
            for u in range(2):
                act.wait_ge(stored[u], OUT_CR + 16 * (B * NT // 2))

        @block.vector
        def _(dve):
            dve.wait_ge(cdone, 2)
            nc.vector.tensor_scalar(keep[:, :], tw[:, :], -1.0, 1.0, ALU.mult, ALU.add).then_inc(cdone, 1)
            dve.wait_ge(cdone, 3)
            with dve.Fori(0, B * NT // 2) as q:
                for u in range(2):
                    n = q * 2 + u
                    dve.wait_ge(s_lin, n + 1)
                    nc.vector.scalar_tensor_tensor(y[:, u, :], lin[u][:, :], keep[:, 0:1], y_in[:, u, :], ALU.mult,
                                                   ALU.add).then_inc(s_y, 1)
                    dve.wait_ge(s_zmm, n + 1)
                    dve.wait_ge(stored[u], OUT_CR + q * 16)
                    nc.vector.tensor_tensor(z[:, u, :], p_z[u][:, :], x_s[:, u, :], ALU.add).then_inc(s_z, 1)

        @block.tensor
        def _(pe):
            pe.wait_ge(made, 2)
            with pe.Fori(0, B * NT // 2) as q:
                for u in range(2):
                    n = q * 2 + u
                    pe.wait_ge(loaded[u], q * LOADS + LOADS)
                    for s in range(2):
                        for j in range(KC):
                            ins = nc.tensor.matmul(lin[u][s * SEG:(s + 1) * SEG, j * P:(j + 1) * P],
                                                   qT[:, u, j, s * SEG:(s + 1) * SEG], state[:, u, j, s, :],
                                                   start=True, stop=True)
                    ins.then_inc(s_lin, 1)
                    pe.wait_ge(s_y, n + 1)
                    for k in range(KC):
                        ins = nc.tensor.transpose(p_T[u][:, k, :], y[:, u, k * P:(k + 1) * P], ident[:, :])
                    ins.then_inc(s_T, 1)
                    pe.wait_ge(s_yT, n + 1)
                    for k in range(KC):
                        ins = nc.tensor.matmul(p_z[u][:, :], yT[:, u, k, :], wc_s[:, k, :], start=(k == 0),
                                               stop=(k == KC - 1))
                    ins.then_inc(s_zmm, 1)

NE, MH, TOPK = 16, 128, 2
ROUTE_SCALE = 2.5
MIN_SUM = 1e-20


def phase_moe(nc, x, gate, w_gate, w_up, w_down, x_out, tag):
    with ExitStack() as ctx:
        m = Mem(nc, ctx, tag)
        G = 4
        W = G * P
        NS = T // W
        ident = m.sb("ident", [P, P])
        iota_e, iota_i = m.sb("iota_e", [P, NE]), m.sb("iota_i", [P, NE], mybir.dt.int32)
        eps = m.sb("eps", [P, 1])
        gw = m.sb("gw", [P, KC, NE])
        wg, wu = m.sb("wg", [P, NE + 1, KC, MH]), m.sb("wu", [P, NE + 1, KC, MH])
        wd = m.sb("wd", [P, NE + 1, D])
        acc = m.sb("acc", [P, 2, G, D])
        stats, mv = m.sb("stats", [P, G, 6]), m.sb("mv", [P, G, 2])
        std, rstd = m.sb("std", [P, G]), m.sb("rstd", [P, G])
        hn = m.sb("hn", [P, G, D])
        hT = m.sb("hT", [P, 2, KC, W])
        ex, ex1, sc = m.sb("ex", [P, G, NE]), m.sb("ex1", [P, G, NE]), m.sb("sc", [P, G, NE])
        top, idx = m.sb("top", [P, G, 8]), m.sb("idx", [P, G, 8], U32)
        idx_f = m.sb("idx_f", [P, G, TOPK])
        tsum, tinv, tw = m.sb("tsum", [P, G]), m.sb("tinv", [P, G]), m.sb("tw", [P, G, TOPK])
        pick = m.sb("pick", [P, G, TOPK, NE])
        route = m.sb("route", [P, 2, G, NE])
        act_g = m.sb("act_g", [P, 2, W])
        hid = m.sb("hid", [P, 2, W])
        p_T = m.ps("T", [P, KC, W])
        p_g = [m.ps(f"g{j}", [P, W]) for j in range(2)]
        p_u = [m.ps(f"u{j}", [P, W]) for j in range(2)]
        p_d = [m.ps(f"d{j}", [P, G // 2, D]) for j in range(2)]
        made, w_in = m.sem("made"), m.sem("w_in")
        x_in, stored = [m.sem(f"x_in{u}") for u in range(2)], [m.sem(f"stored{u}") for u in range(2)]
        s_stat, s_var, s_std, s_rstd, s_hn = (m.sem(k) for k in ("stat", "var", "std", "rstd", "hn"))
        s_T, s_hT, s_log, s_ex, s_chain = (m.sem(k) for k in ("T", "hT", "log", "ex", "chain"))
        s_top, s_pick, s_route = m.sem("top"), m.sem("pick"), m.sem("route")
        s_gu, s_act, s_hid, s_d, s_acc = (m.sem(k) for k in ("gu", "silu", "hid", "down", "acc"))
        sp_passed, dve_passed = m.sem("sp_passed"), m.sem("dve_passed")
        HID_CR, D_CR, OUT_CR = 2, 2, 1
        CH = 6
        N1 = NE + 1
        block = ctx.enter_context(nc.Block())

        def steps(eng, body):
            with eng.Fori(0, NS // 2 - 1) as q:
                body(q * 2, 0, q, False)
                body(q * 2 + 1, 1, q, False)
            body(NS - 2, 0, NS // 2 - 1, False)
            body(NS - 1, 1, NS // 2 - 1, True)

        @block.sync
        def _(sp):
            sp.dma_start(gw[:, :, :], gate).then_inc(w_in, 16)
            sp.dma_start(acc[:, 0, :, :], rows(x, 0, G)).then_inc(x_in[0], 16)
            sp.dma_start(wg[:, :, :, :], w_gate).then_inc(w_in, 16)
            sp.dma_start(wu[:, :, :, :], w_up).then_inc(w_in, 16)
            sp.dma_start(wd[:, :, :], w_down).then_inc(w_in, 16)
            sp.sem_inc(s_hid, HID_CR)
            sp.sem_inc(s_acc, D_CR)
            sp.sem_inc(stored[0], OUT_CR)
            sp.sem_inc(stored[1], OUT_CR)

            def body(n, u, q, last):
                if not last:
                    wait_here(sp, stored[1 - u], OUT_CR + (q + u) * 16, sp_passed)
                    sp.dma_start(acc[:, 1 - u, :, :], rows(x, n * W + W, G)).then_inc(x_in[1 - u], 16)
                wait_here(sp, s_acc, D_CR + n * (2 * N1) + 2 * N1, sp_passed)
                sp.dma_start(rows(x_out, n * W, G), acc[:, u, :, :]).then_inc(stored[u], 16)

            steps(sp, body)
            for u in range(2):
                sp.wait_ge(stored[u], OUT_CR + NS // 2 * 16)

        @block.gpsimd
        def _(pool):
            make_identity(pool, ident, made)
            pool.memset(eps[:, :], LN_EPS).then_inc(made, 1)
            pool.iota(iota_i[:, :], pattern=[[1, NE]], base=0, channel_multiplier=0).then_inc(made, 1)
            pool.wait_ge(made, 4)
            pool.tensor_copy(iota_e[:, :], iota_i[:, :]).then_inc(made, 1)

        @block.scalar
        def _(act):
            act.wait_ge(made, 5)

            def front(n, u):
                act.wait_ge(s_var, n * G + G)
                nc.scalar.activation(std[:, :], mv[:, :, 1], ACT.Sqrt, bias=eps[:, 0:1]).then_inc(s_std, 1)
                for k in range(KC):
                    act.wait_ge(s_T, n * KC + k + 1)
                    nc.scalar.copy(hT[:, u, k, :], p_T[:, k, :]).then_inc(s_hT, 1)

            def scores(n):
                act.wait_ge(s_log, n + 1)
                nc.scalar.activation(ex[:, :, :], p_T[:, 0, 0:G * NE].rearrange("p (g e) -> p g e", g=G), ACT.Exp,
                                     scale=-1.0).then_inc(s_ex, 1)

            def body(n, u, q, last):
                for e in range(N1):
                    k = n * N1 + e
                    act.wait_ge(s_gu, k + 1)
                    act.wait_ge(s_hid, HID_CR - 1 + k)
                    nc.scalar.activation(act_g[:, (u * N1 + e) % 2, :], p_g[(u * N1 + e) % 2][:, :],
                                         ACT.Silu).then_inc(s_act, 1)
                    if e == 9 and not last:
                        front(n + 1, 1 - u)
                    if e == 12 and not last:
                        scores(n + 1)

            front(0, 0)
            scores(0)
            steps(act, body)

        @block.vector
        def _(dve):
            dve.wait_ge(made, 5)

            def front(n, u, q):
                dve.wait_ge(x_in[u], q * 16 + 16)
                for t in range(G):
                    nc.vector.bn_stats(stats[:, t, :], acc[:, u, t, :]).then_inc(s_stat, 1)
                wait_here(dve, s_stat, n * G + G, dve_passed)
                for t in range(G):
                    nc.vector.bn_aggr(mv[:, t, :], stats[:, t, :]).then_inc(s_var, 1)
                dve.wait_ge(s_std, n + 1)
                nc.vector.reciprocal(rstd[:, :], std[:, :]).then_inc(s_rstd, 1)
                dve.wait_ge(s_rstd, n + 1)
                for t in range(G):
                    nc.vector.tensor_scalar(hn[:, t, :], acc[:, u, t, :], mv[:, t, 0:1], rstd[:, t:t + 1],
                                            ALU.subtract, ALU.mult).then_inc(s_hn, 1)

            def routing(n, u):
                dve.wait_ge(s_ex, n + 1)
                nc.vector.tensor_scalar(ex1[:, :, :], ex[:, :, :], 1.0, None, ALU.add).then_inc(s_chain, 1)
                dve.wait_ge(s_chain, n * CH + 1)
                nc.vector.reciprocal(sc[:, :, :], ex1[:, :, :]).then_inc(s_chain, 1)
                wait_here(dve, s_chain, n * CH + 2, dve_passed)
                for t in range(G):
                    nc.vector.max(top[:, t, :], sc[:, t, :]).then_inc(s_top, 1)
                wait_here(dve, s_top, n * (2 * G) + G, dve_passed)
                for t in range(G):
                    nc.vector.max_index(idx[:, t, :], top[:, t, :], sc[:, t, :]).then_inc(s_top, 1)
                nc.vector.tensor_tensor(tsum[:, :], top[:, :, 0], top[:, :, 1], ALU.add).then_inc(s_chain, 1)
                dve.wait_ge(s_chain, n * CH + 3)
                nc.vector.tensor_scalar(tsum[:, :], tsum[:, :], MIN_SUM, None, ALU.add).then_inc(s_chain, 1)
                dve.wait_ge(s_chain, n * CH + 4)
                nc.vector.reciprocal(tinv[:, :], tsum[:, :]).then_inc(s_chain, 1)
                dve.wait_ge(s_top, n * (2 * G) + 2 * G)
                nc.vector.tensor_copy(idx_f[:, :, :], idx[:, :, 0:TOPK]).then_inc(s_chain, 1)
                dve.wait_ge(s_chain, n * CH + 6)
                for t in range(G):
                    nc.vector.tensor_scalar(tw[:, t, :], top[:, t, 0:TOPK], tinv[:, t:t + 1], ROUTE_SCALE, ALU.mult,
                                            ALU.mult).then_inc(s_pick, 1)
                dve.wait_ge(s_pick, n * (3 * G) + G)
                for t in range(G):
                    for j in range(TOPK):
                        nc.vector.tensor_scalar(pick[:, t, j, :], iota_e[:, :], idx_f[:, t, j:j + 1], tw[:, t, j:j + 1],
                                                ALU.is_equal, ALU.mult).then_inc(s_pick, 1)
                dve.wait_ge(s_pick, n * (3 * G) + 3 * G)
                nc.vector.tensor_tensor(route[:, u, :, :], pick[:, :, 0, :], pick[:, :, 1, :], ALU.add).then_inc(s_route, 1)

            def hidden(n, u, e):
                k = n * N1 + e
                j = (u * N1 + e) % 2
                dve.wait_ge(s_act, k + 1)
                nc.vector.tensor_tensor(hid[:, j, :], act_g[:, j, :], p_u[j][:, :], ALU.mult).then_inc(s_hid, 1)

            def add(n, u, e):
                k = n * N1 + e
                for half in range(2):
                    dve.wait_ge(s_d, k * 2 + half + 1)
                    for t in range(half * G // 2, (half + 1) * G // 2):
                        o = p_d[half][:, t % (G // 2), :]
                        if e < NE:
                            ins = nc.vector.scalar_tensor_tensor(acc[:, u, t, :], o, route[:, u, t, e:e + 1],
                                                                 acc[:, u, t, :], ALU.mult, ALU.add)
                        else:
                            ins = nc.vector.tensor_tensor(acc[:, u, t, :], o, acc[:, u, t, :], ALU.add)
                    ins.then_inc(s_acc, 1)

            def body(n, u, q, last):
                for e in range(N1):
                    hidden(n, u, e)
                    if e:
                        dve.wait_ge(s_acc, D_CR + (n * N1 + e - 1) * 2)
                        add(n, u, e - 1)
                    if e == 9 and not last:
                        front(n + 1, 1 - u, q + u)
                    if e == 12 and not last:
                        routing(n + 1, 1 - u)
                add(n, u, NE)

            front(0, 0, 0)
            routing(0, 0)
            dve.wait_ge(s_route, 1)
            steps(dve, body)

        @block.tensor
        def _(pe):
            pe.wait_ge(made, 2)
            pe.wait_ge(w_in, 64)

            def front(n, u):
                pe.wait_ge(s_hn, n * G + G)
                for k in range(KC):
                    for t in range(G):
                        ins = nc.tensor.transpose(p_T[:, k, t * P:(t + 1) * P], hn[:, t, k * P:(k + 1) * P], ident[:, :])
                    ins.then_inc(s_T, 1)

            def logits(n, u):
                pe.wait_ge(s_hT, n * KC + KC)
                for t in range(G):
                    for k in range(KC):
                        ins = nc.tensor.matmul(p_T[:, 0, t * NE:(t + 1) * NE], hT[:, u, k, t * P:(t + 1) * P],
                                               gw[:, k, :], start=(k == 0), stop=(k == KC - 1))
                ins.then_inc(s_log, 1)

            def gate_up(n, u, e):
                k = n * N1 + e
                j = (u * N1 + e) % 2
                pe.wait_ge(s_hid, HID_CR - 1 + k)
                for w, p in ((wg, p_g[j]), (wu, p_u[j])):
                    for c in range(KC):
                        ins = nc.tensor.matmul(p[:, :], w[:, e, c, :], hT[:, u, c, :], start=(c == 0), stop=(c == KC - 1))
                ins.then_inc(s_gu, 1)

            def down(n, u, e):
                k = n * N1 + e
                j = (u * N1 + e) % 2
                pe.wait_ge(s_hid, HID_CR + k + 1)
                for half in range(2):
                    pe.wait_ge(s_acc, D_CR - 1 + k * 2 + half)
                    for t in range(half * G // 2, (half + 1) * G // 2):
                        ins = nc.tensor.matmul(p_d[half][:, t % (G // 2), :], hid[:, j, t * P:(t + 1) * P],
                                               wd[:, e, :], start=True, stop=True)
                    ins.then_inc(s_d, 1)

            def body(n, u, q, last):
                gate_up(n, u, 0)
                for e in range(N1):
                    if e + 1 < N1:
                        gate_up(n, u, e + 1)
                    down(n, u, e)
                    if e == 9 and not last:
                        front(n + 1, 1 - u)
                    if e == 11 and not last:
                        logits(n + 1, 1 - u)

            front(0, 0)
            logits(0, 0)
            steps(pe, body)

NM, MS = 4, 5
GH, GK, GV = 4, 32, 64
LOW = 16
CAP = L // 2
GATE_NORM = 16.0
NTT = T // P


def phase_route(nc, x, w_gate, hT_dram, kw_dram):
    with ExitStack() as ctx:
        m = Mem(nc, ctx, "rt_")
        G = 4
        W = G * P
        NS = T // W
        ident, tri, ones = m.sb("ident", [P, P]), m.sb("tri", [P, P]), m.sb("ones", [P, P])
        iota_m, iota_i = m.sb("iota_m", [P, NM]), m.sb("iota_i", [P, NM], mybir.dt.int32)
        eps = m.sb("eps", [P, 1])
        gw = m.sb("gw", [P, KC, NM])
        x_s = m.sb("x", [P, G, D])
        stats, mv = m.sb("stats", [P, G, 6]), m.sb("mv", [P, G, 2])
        std, rstd = m.sb("std", [P, G]), m.sb("rstd", [P, G])
        hn, hT = m.sb("hn", [P, G, D]), m.sb("hT", [P, KC, W])
        mx, dist = m.sb("mx", [P, G]), m.sb("dist", [P, G, NM])
        ex, esum, einv = m.sb("ex", [P, G, NM]), m.sb("esum", [P, G]), m.sb("einv", [P, G])
        prob = m.sb("prob", [P, G, 8])
        top, idx, idx_f = m.sb("top", [P, G, 8]), m.sb("idx", [P, G, 8], U32), m.sb("idx_f", [P, G, TOPK])
        tsum, tinv = m.sb("tsum", [P, G]), m.sb("tinv", [P, G])
        pick = m.sb("pick", [P, G, TOPK, NM])
        wts = m.sb("wts", [P, G, TOPK])
        pw = m.sb("pw", [P, G, TOPK, NM])
        sel, wt = m.sb("sel", [P, NTT * NM]), m.sb("wt", [P, NTT * NM])
        later = m.sb("later", [P, B, NT, NM])
        kw = m.sb("kw", [P, NTT, 2, NM])
        zeros = m.sb("zeros", [P, 2 * P])
        p_T = m.ps("T", [P, KC, W])
        p_l = m.ps("l", [P, G, NM])
        p_c = m.ps("c", [P, NTT * NM])
        made, w_in, x_in, stored, kw_out = (m.sem(k) for k in ("made", "w_in", "x_in", "stored", "kw_out"))
        s_stat, s_var, s_std, s_rstd, s_hn = (m.sem(k) for k in ("stat", "var", "std", "rstd", "hn"))
        s_T, s_hT, s_log, s_ex, s_chain, s_top, s_pick = (m.sem(k) for k in ("T", "hT", "log", "ex", "chain", "top", "pick"))
        s_sel, s_dist, s_later, s_cnt, s_kw = m.sem("sel"), m.sem("dist"), m.sem("later"), m.sem("cnt"), m.sem("kw")
        sp_passed, dve_passed = m.sem("sp_passed"), m.sem("dve_passed")
        CH = 7
        HN_CR, OUT_CR = 1, 1
        block = ctx.enter_context(nc.Block())

        @block.sync
        def _(sp):
            sp.dma_start(gw[:, :, :], w_gate).then_inc(w_in, 16)
            sp.sem_inc(s_hn, HN_CR)
            sp.sem_inc(stored, OUT_CR)
            sp.wait_ge(made, 11)
            for k in range(KC):
                sp.dma_start(hT_dram[k, :, T:T + 2 * P], zeros[:, :]).then_inc(kw_out, 16)
            sp.dma_start(kw_dram[NTT:NTT + 2, :, :].rearrange("t p n -> p t n"),
                         zeros[:, 0:4 * NM].rearrange("p (t n) -> p t n", t=2)).then_inc(kw_out, 16)
            with sp.Fori(0, NS) as n:
                wait_here(sp, s_hn, HN_CR + n * G, sp_passed)
                sp.dma_start(x_s[:, :, :], rows(x, n * W, G)).then_inc(x_in, 16)
                wait_here(sp, s_hT, n * KC + KC, sp_passed)
                sp.dma_start(hT_dram[:, :, ds(n * W, W)].rearrange("k p t -> p k t"), hT[:, :, :]).then_inc(stored, 16)
            sp.wait_ge(s_kw, 2)
            sp.dma_start(kw_dram[0:NTT, :, :].rearrange("t p n -> p t n"), kw[:, :, :, :].rearrange("p t a m -> p t (a m)")
                         ).then_inc(kw_out, 16)
            sp.wait_ge(stored, OUT_CR + NS * 16)
            sp.wait_ge(kw_out, 16 * (KC + 2))

        @block.gpsimd
        def _(pool):
            make_identity(pool, ident, made)
            pool.memset(eps[:, :], LN_EPS).then_inc(made, 1)
            pool.memset(ones[:, :], 1.0).then_inc(made, 1)
            pool.memset(tri[:, :], 1.0).then_inc(made, 1)
            pool.memset(prob[:, :, :], -1.0).then_inc(made, 1)
            pool.memset(later[:, :, :, :], 0.0).then_inc(made, 1)
            pool.iota(iota_i[:, :], pattern=[[1, NM]], base=0, channel_multiplier=0).then_inc(made, 1)
            pool.wait_ge(made, 8)
            pool.tensor_copy(iota_m[:, :], iota_i[:, :]).then_inc(made, 1)
            pool.affine_select(out=tri[:, :], in_=tri[:, :], compare_op=ALU.is_ge, fill=0.0, base=0,
                               pattern=[[-1, P]], channel_multiplier=1).then_inc(made, 1)
            pool.memset(zeros[:, :], 0.0).then_inc(made, 1)

        @block.scalar
        def _(act):
            act.wait_ge(made, 10)
            with act.Fori(0, NS) as n:
                act.wait_ge(s_var, n * G + G)
                nc.scalar.activation(std[:, :], mv[:, :, 1], ACT.Sqrt, bias=eps[:, 0:1]).then_inc(s_std, 1)
                act.wait_ge(stored, OUT_CR + n * 16)
                for k in range(KC):
                    act.wait_ge(s_T, n * KC + k + 1)
                    nc.scalar.copy(hT[:, k, :], p_T[:, k, :]).then_inc(s_hT, 1)
                act.wait_ge(s_dist, n + 1)
                nc.scalar.activation(ex[:, :, :], dist[:, :, :], ACT.Exp).then_inc(s_ex, 1)

        @block.vector
        def _(dve):
            dve.wait_ge(made, 10)
            with dve.Fori(0, NS) as n:
                dve.wait_ge(x_in, n * 16 + 16)
                for t in range(G):
                    nc.vector.bn_stats(stats[:, t, :], x_s[:, t, :]).then_inc(s_stat, 1)
                wait_here(dve, s_stat, n * G + G, dve_passed)
                for t in range(G):
                    nc.vector.bn_aggr(mv[:, t, :], stats[:, t, :]).then_inc(s_var, 1)
                dve.wait_ge(s_std, n + 1)
                nc.vector.reciprocal(rstd[:, :], std[:, :]).then_inc(s_rstd, 1)
                dve.wait_ge(s_rstd, n + 1)
                for t in range(G):
                    nc.vector.tensor_scalar(hn[:, t, :], x_s[:, t, :], mv[:, t, 0:1], rstd[:, t:t + 1],
                                            ALU.subtract, ALU.mult).then_inc(s_hn, 1)
                dve.wait_ge(s_log, n + 1)
                nc.vector.tensor_reduce(mx[:, :], p_l[:, :, :], AX.X, ALU.max).then_inc(s_chain, 1)
                dve.wait_ge(s_chain, n * CH + 1)
                nc.vector.tensor_tensor(dist[:, :, :], p_l[:, :, :], mx[:, :].unsqueeze(2).to_broadcast([P, G, NM]),
                                        ALU.subtract).then_inc(s_dist, 1)
                dve.wait_ge(s_ex, n + 1)
                nc.vector.tensor_reduce(esum[:, :], ex[:, :, :], AX.X, ALU.add).then_inc(s_chain, 1)
                dve.wait_ge(s_chain, n * CH + 2)
                nc.vector.reciprocal(einv[:, :], esum[:, :]).then_inc(s_chain, 1)
                dve.wait_ge(s_chain, n * CH + 3)
                nc.vector.tensor_tensor(prob[:, :, 0:NM], ex[:, :, :], einv[:, :].unsqueeze(2).to_broadcast([P, G, NM]),
                                        ALU.mult).then_inc(s_chain, 1)
                wait_here(dve, s_chain, n * CH + 4, dve_passed)
                for t in range(G):
                    nc.vector.max(top[:, t, :], prob[:, t, :]).then_inc(s_top, 1)
                wait_here(dve, s_top, n * (2 * G) + G, dve_passed)
                for t in range(G):
                    nc.vector.max_index(idx[:, t, :], top[:, t, :], prob[:, t, :]).then_inc(s_top, 1)
                nc.vector.tensor_tensor(tsum[:, :], top[:, :, 0], top[:, :, 1], ALU.add).then_inc(s_chain, 1)
                dve.wait_ge(s_chain, n * CH + 5)
                nc.vector.reciprocal(tinv[:, :], tsum[:, :]).then_inc(s_chain, 1)
                dve.wait_ge(s_top, n * (2 * G) + 2 * G)
                nc.vector.tensor_copy(idx_f[:, :, :], idx[:, :, 0:TOPK]).then_inc(s_chain, 1)
                dve.wait_ge(s_chain, n * CH + 7)
                nc.vector.tensor_tensor(wts[:, :, :], top[:, :, 0:TOPK], tinv[:, :].unsqueeze(2).to_broadcast([P, G, TOPK]),
                                        ALU.mult).then_inc(s_pick, 1)
                for t in range(G):
                    for j in range(TOPK):
                        nc.vector.tensor_scalar(pick[:, t, j, :], iota_m[:, :], idx_f[:, t, j:j + 1], None,
                                                ALU.is_equal).then_inc(s_pick, 1)
                PK = 3 + G * TOPK
                dve.wait_ge(s_pick, n * PK + 1 + G * TOPK)
                nc.vector.tensor_tensor(pw[:, :, :, :].rearrange("p g j m -> p (g j) m"),
                                        pick[:, :, :, :].rearrange("p g j m -> p (g j) m"),
                                        wts[:, :, :].rearrange("p g j -> p (g j)").unsqueeze(2).to_broadcast([P, G * TOPK, NM]),
                                        ALU.mult).then_inc(s_pick, 1)
                nc.vector.tensor_tensor(sel[:, ds(n * (G * NM), G * NM)].rearrange("p (g m) -> p g m", g=G),
                                        pick[:, :, 0, :], pick[:, :, 1, :], ALU.add).then_inc(s_sel, 1)
                dve.wait_ge(s_pick, n * PK + 2 + G * TOPK)
                nc.vector.tensor_tensor(wt[:, ds(n * (G * NM), G * NM)].rearrange("p (g m) -> p g m", g=G),
                                        pw[:, :, 0, :], pw[:, :, 1, :], ALU.add).then_inc(s_pick, 1)
            dve.wait_ge(s_pick, NS * (3 + G * TOPK))
            dve.wait_ge(s_sel, NS)
            sel4 = sel[:, :].rearrange("p (b i m) -> p b i m", b=B, m=NM)
            for i in range(NT - 2, -1, -1):
                if i < NT - 2:
                    dve.wait_ge(s_later, NT - 2 - i)
                nc.vector.tensor_tensor(later[:, :, i, :], later[:, :, i + 1, :], sel4[:, :, i + 1, :],
                                        ALU.add).then_inc(s_later, 1)
            dve.wait_ge(s_cnt, 1)
            nc.vector.scalar_tensor_tensor(kw[:, :, 0, :], p_c[:, :].rearrange("p (t m) -> p t m", m=NM), float(CAP),
                                           sel[:, :].rearrange("p (t m) -> p t m", m=NM), ALU.is_le,
                                           ALU.mult).then_inc(s_kw, 1)
            dve.wait_ge(s_kw, 1)
            nc.vector.tensor_tensor(kw[:, :, 1, :], kw[:, :, 0, :], wt[:, :].rearrange("p (t m) -> p t m", m=NM),
                                    ALU.mult).then_inc(s_kw, 1)

        @block.tensor
        def _(pe):
            pe.wait_ge(made, 10)
            pe.wait_ge(w_in, 16)
            with pe.Fori(0, NS) as n:
                pe.wait_ge(s_hn, HN_CR + n * G + G)
                for k in range(KC):
                    for t in range(G):
                        ins = nc.tensor.transpose(p_T[:, k, t * P:(t + 1) * P], hn[:, t, k * P:(k + 1) * P], ident[:, :])
                    ins.then_inc(s_T, 1)
                pe.wait_ge(s_hT, n * KC + KC)
                for t in range(G):
                    for k in range(KC):
                        ins = nc.tensor.matmul(p_l[:, t, :], hT[:, k, t * P:(t + 1) * P], gw[:, k, :],
                                               start=(k == 0), stop=(k == KC - 1))
                ins.then_inc(s_log, 1)
            pe.wait_ge(s_later, NT - 1)
            nc.tensor.matmul(p_c[:, :], tri[:, :], sel[:, :], start=True, stop=False)
            nc.tensor.matmul(p_c[:, :], ones[:, :], later[:, :, :, :].rearrange("p b i m -> p (b i m)"),
                             start=False, stop=True).then_inc(s_cnt, 1)


def phase_gla(nc, hT_dram, kw_dram, w_q, w_k, w_v, w_gk1, w_gk2, b_gk, o_dram):
    with ExitStack() as ctx:
        m = Mem(nc, ctx, "gl_")
        HALVES = (64, 32, 16, 8, 4, 2)
        NL = len(HALVES) + 1
        DIRECT = 3
        MP = MS * P
        HKD = GH * GK
        assert HKD == P and GH * GV == D
        FLOOR = -80.0
        ident = m.sb("ident", [P, P])
        masks = m.sb("masks", [P, NL - DIRECT, P])
        restart = m.sb("restart", [P, MS, P])
        wq, wk = m.sb("wq", [P, KC, P]), m.sb("wk", [P, MS, KC, P])
        wv = m.sb("wv", [P, MS, KC, D])
        w1, w2 = m.sb("w1", [P, KC, MS, 32]), m.sb("w2", [P, NM, P])
        w2s = m.sb("w2s", [32, P])
        bg = m.sb("bg", [P, MS])
        hT = m.sb("hT", [P, 2, KC, P])
        kw = m.sb("kw", [P, 2, 2 * NM])
        keep_m = m.sb("keep_m", [P, NM, P])
        qS, kS = m.sb("qS", [P, P]), m.sb("kS", [P, MP])
        low, low_s = m.sb("low", [P, P]), m.sb("low_s", [32, P])
        zb, az, ln = m.sb("zb", [P, MP]), m.sb("az", [P, MP]), m.sb("ln", [P, MP])
        zn = m.sb("zn", [P, MP])
        g, Gs = m.sb("g", [P, MP]), m.sb("Gs", [P, MP])
        dist = m.sb("dist", [P, NL, MP])
        gc = m.sb("gc", [P, MP // 2])
        ex = m.sb("ex", [P, NL, MP])
        exG, exE = m.sb("exG", [P, MP]), m.sb("exE", [P, MP])
        qt, kt = m.sb("qt", [P, 2, NL, MP]), m.sb("kt", [P, 2, NL, MP])
        q0, kend = m.sb("q0", [P, 2, MP]), m.sb("kend", [P, 2, MP])
        dend = m.sb("dend", [P, 2, MS])
        V = m.sb("V", [P, 2, MS, D])
        A = m.sb("A", [P, 2, GH * P])
        kE = m.sb("kE", [P, P])
        state = m.sb("state", [P, MS, D])
        acc = m.sb("acc", [P, 2, D])
        pd = m.ps("pd", [P, GH * P])
        pl = [m.ps(f"pl{j}", [P, GH * P]) for j in range(2)]
        po, pu = m.ps("po", [P, D]), m.ps("pu", [P, 512])
        f = [m.ps(f"f{j}", [P, 512]) for j in range(3)]
        made, w_in = m.sem("made"), m.sem("w_in")
        ld = [m.sem(f"ld{u}") for u in range(2)]
        stored = [m.sem(f"stored{u}") for u in range(2)]
        s_kM, s_F1, s_F1e, s_Z, s_KB, s_Ze, s_gate = (m.sem(k) for k in ("kM", "F1", "F1e", "Z", "KB", "Ze", "gate"))
        s_chain, s_g, s_D, s_V, s_Ve, s_ex, s_mul = (m.sem(k) for k in ("chain", "g", "D", "V", "Ve", "ex", "mul"))
        s_dir, s_A, s_cp, s_T, s_kE, s_U = (m.sem(k) for k in ("dir", "A", "cp", "T", "kE", "U"))
        s_lv = [m.sem(f"lv{j}") for j in range(2)]
        s_o, s_out, s_S, s_reset = (m.sem(k) for k in ("o", "out", "S", "reset"))
        sp_passed, dve_passed, pe_passed, act_passed, pool_passed = (
            m.sem(k) for k in ("sp_passed", "dve_passed", "pe_passed", "act_passed", "pool_passed"))
        MUL_CR, VE_CR, A_CR, CP_CR, OUT_CR, S_CR, ST_CR, O_CR, DIR_CR, LV_CR = 1, 3, 1, 2, 1, MS, 1, 2, 1, 1
        NX = 2 * (NL - 1) + 2 + 2
        NMUL = 2 * (NL - 1) + 4 + 2
        NLV = NL - DIRECT
        block = ctx.enter_context(nc.Block())

        def tiles(eng, body, before=None):
            with eng.Fori(0, B) as b:
                if before is not None:
                    before(b)
                with eng.Fori(0, NT // 2) as p:
                    for u in range(2):
                        body(b * NT + p * 2 + u, u, b * (NT // 2) + p)

        @block.sync
        def _(sp):
            for dst, src in ((wq[:, :, :], w_q), (wk[:, :, :, :], w_k), (wv[:, :, :, :], w_v), (bg[:, :], b_gk)):
                sp.dma_start(dst, src).then_inc(w_in, 16)
            sp.wait_ge(made, 6)
            sp.dma_start(w1[:, :, :, 0:LOW], w_gk1).then_inc(w_in, 16)
            for j in range(NM):
                sp.dma_start(w2[j * 32:j * 32 + LOW, j, :], w_gk2[j, :, :]).then_inc(w_in, 16)
            sp.dma_start(w2s[0:LOW, :], w_gk2[NM, :, :]).then_inc(w_in, 16)
            for sem, credits in ((s_mul, MUL_CR), (s_Ve, VE_CR), (s_A, A_CR), (s_cp, CP_CR), (s_out, OUT_CR),
                                 (s_S, S_CR), (s_dir, DIR_CR), (s_lv[0], LV_CR), (s_lv[1], LV_CR), (stored[0], ST_CR), (stored[1], ST_CR), (s_o, O_CR)):
                sp.sem_inc(sem, credits)

            def load(n, u):
                sp.dma_start(hT[:, u, :, :], hT_dram[:, :, ds(n * P, P)].rearrange("k p t -> p k t")).then_inc(ld[u], 16)
                sp.dma_start(kw[:, u, :], kw_dram[ds(n, 1), :, :].rearrange("a p n -> (a p) n")).then_inc(ld[u], 16)

            load(0, 0)
            load(1, 1)

            def body(n, u, q):
                wait_here(sp, s_out, OUT_CR + n * MS + MS, sp_passed)
                sp.dma_start(o_dram[ds(n * P, P), :], acc[:, u, :]).then_inc(stored[u], 16)
                wait_here(sp, s_S, S_CR + n * MS + MS, sp_passed)
                load(n + 2, u)

            tiles(sp, body)
            for u in range(2):
                sp.wait_ge(stored[u], ST_CR + NTT // 2 * 16)
                sp.wait_ge(ld[u], 32 * (NTT // 2 + 1))

        @block.gpsimd
        def _(pool):
            make_identity(pool, ident, made)
            pool.memset(w1[:, :, :, :], 0.0).then_inc(made, 1)
            pool.memset(w2[:, :, :], 0.0).then_inc(made, 1)
            pool.memset(w2s[:, :], 0.0).then_inc(made, 1)
            pool.memset(masks[:, :, :], 0.0).then_inc(made, 1)
            pool.memset(restart[:, :, :], 1.0).then_inc(made, 1)
            pool.wait_ge(made, 7)
            pool.memset(restart[:, :, 0:1], 0.0).then_inc(made, 1)
            pool.memset(qt[:, :, :, :], 0.0).then_inc(made, 1)
            pool.memset(kt[:, :, :, :], 0.0).then_inc(made, 1)
            at = 10
            for l in range(DIRECT, NL):
                s = HALVES[l] if l < NL - 1 else 1
                v = masks[:, l - DIRECT, :].rearrange("p (n r) -> p n r", r=2 * s)
                v = v[:, :, s:2 * s] if l < NL - 1 else v
                r = s if l < NL - 1 else 2
                pool.wait_ge(made, at)
                pool.memset(v, 1.0).then_inc(made, 1)
                pool.wait_ge(made, at + 1)
                pool.affine_select(out=v, in_=v, compare_op=ALU.is_ge, fill=0.0, base=0,
                                   pattern=[[-2 * s, P // (2 * s)], [0, r]], channel_multiplier=1).then_inc(made, 1)
                pool.wait_ge(made, at + 2)
                pool.affine_select(out=v, in_=v, compare_op=ALU.is_ge, fill=0.0, base=s - 1,
                                   pattern=[[2 * s, P // (2 * s)], [1 if l == NL - 1 else 0, r]],
                                   channel_multiplier=-1).then_inc(made, 1)
                at += 3

            def keep_rows(fn, u, qf):
                pool.wait_ge(ld[u], qf * 32 + 32)
                pool.sem_inc(pool_passed, 1)
                pool.tensor_copy(keep_m[:, :, :], kw[:, u, 0:NM].unsqueeze(2).to_broadcast([P, NM, P])).then_inc(s_kM, 1)

            def products(fn, u):
                q3 = qS[:, :]
                done = 0
                for l, s in enumerate(HALVES):
                    nb = P // (2 * s)
                    wait_here(pool, s_ex, fn * NX + 2 * l + 2, pool_passed)
                    for c in range(MS):
                        ins = pool.tensor_tensor(
                            out=qt[:, u, l, c * P:(c + 1) * P].rearrange("p (n r) -> p n r", r=2 * s)[:, :, s:2 * s],
                            in0=q3.rearrange("p (n r) -> p n r", r=2 * s)[:, :, s:2 * s],
                            in1=ex[:, l, c * P:(c + 1) * P].rearrange("p (n r) -> p n r", r=2 * s)[:, :, s:2 * s], op=ALU.mult)
                    ins.then_inc(s_mul, 1)
                    pool.tensor_tensor(
                        out=kt[:, u, l, :].rearrange("p (n r) -> p n r", r=2 * s)[:, :, 0:s],
                        in0=kS[:, :].rearrange("p (n r) -> p n r", r=2 * s)[:, :, 0:s],
                        in1=ex[:, l, :].rearrange("p (n r) -> p n r", r=2 * s)[:, :, 0:s], op=ALU.mult).then_inc(s_mul, 1)
                l = NL - 1
                wait_here(pool, s_ex, fn * NX + NX, pool_passed)
                pairs = lambda a: a.rearrange("p (n r) -> p n r", r=2)
                half = MP // 2
                qb = pairs(q3)
                qt4 = qt[:, u, l, :].rearrange("p (c n r) -> p c n r", c=MS, r=2)
                pool.tensor_copy(qt4[:, :, :, 0], qb[:, :, 0].unsqueeze(1).to_broadcast([P, MS, P // 2])).then_inc(s_mul, 1)
                pool.tensor_tensor(out=qt4[:, :, :, 1], in0=qb[:, :, 1].unsqueeze(1).to_broadcast([P, MS, P // 2]),
                                   in1=ex[:, l, 0:half].rearrange("p (c n) -> p c n", c=MS), op=ALU.mult).then_inc(s_mul, 1)
                pool.tensor_copy(pairs(kt[:, u, l, :])[:, :, 0], pairs(kS[:, :])[:, :, 0]).then_inc(s_mul, 1)
                pool.tensor_tensor(out=pairs(kt[:, u, l, :])[:, :, 1], in0=pairs(kS[:, :])[:, :, 1],
                                   in1=ex[:, l, half:MP], op=ALU.mult).then_inc(s_mul, 1)
                pool.tensor_tensor(out=q0[:, u, :].rearrange("p (c n) -> p c n", c=MS),
                                   in0=q3.unsqueeze(1).to_broadcast([P, MS, P]),
                                   in1=exG[:, :].rearrange("p (c n) -> p c n", c=MS), op=ALU.mult).then_inc(s_mul, 1)
                pool.tensor_tensor(out=kend[:, u, :], in0=kS[:, :], in1=exE[:, :], op=ALU.mult).then_inc(s_mul, 1)

            keep_rows(0, 0, 0)
            products(0, 0)

            def body(n, u, q):
                wait_here(pool, s_KB, n + 1, pool_passed)
                keep_rows(n + 1, 1 - u, q + u)
                products(n + 1, 1 - u)

            tiles(pool, body)

        @block.scalar
        def _(act):
            act.wait_ge(w_in, 16 * 10)
            act.wait_ge(made, 10)

            def front1(fn, u):
                act.wait_ge(s_mul, MUL_CR + fn * NMUL)
                act.wait_ge(s_F1, fn * 2 + 1)
                nc.scalar.mul(qS[:, :], f[0][:, 0:P], float(GK) ** -0.5)
                nc.scalar.copy(kS[:, 0:3 * P], f[0][:, P:4 * P]).then_inc(s_F1e, 1)
                act.wait_ge(s_F1, fn * 2 + 2)
                nc.scalar.copy(kS[:, 3 * P:MP], f[1][:, 0:2 * P])
                nc.scalar.copy(low[:, :], f[1][:, 2 * P:3 * P])
                nc.scalar.copy(low_s[:, :], f[1][0:32, 3 * P:4 * P]).then_inc(s_F1e, 1)

            def front2(fn, u):
                act.wait_ge(s_Z, fn * 2 + 2)
                for c in range(MS):
                    src = f[2][:, c * P:(c + 1) * P] if c < NM else f[0][:, 0:P]
                    ins = nc.scalar.activation(zb[:, c * P:(c + 1) * P], src, ACT.Identity, bias=bg[:, c:c + 1])
                ins.then_inc(s_Ze, 1)
                act.wait_ge(s_Ze, fn + 1)
                nc.scalar.activation(az[:, :], zb[:, :], ACT.Abs).then_inc(s_gate, 1)
                act.wait_ge(s_gate, fn * 3 + 1)
                nc.scalar.activation(az[:, :], az[:, :], ACT.Exp, scale=-1.0).then_inc(s_gate, 1)
                act.wait_ge(s_gate, fn * 3 + 2)
                nc.scalar.activation(ln[:, :], az[:, :], ACT.Ln, bias=1.0).then_inc(s_gate, 1)

            def front3(fn, u):
                for j, (bank, mems) in enumerate(((2, (0, 1)), (1, (2, 3)), (0, (4,)))):
                    act.wait_ge(s_V, fn * 3 + j + 1)
                    for x, c in enumerate(mems):
                        src = f[bank][:, x * D:(x + 1) * D]
                        if c < NM:
                            ins = nc.scalar.activation(V[:, u, c, :], src, ACT.Copy, scale=kw[:, u, c:c + 1])
                        else:
                            ins = nc.scalar.copy(V[:, u, c, :], src)
                    ins.then_inc(s_Ve, 1)

            def front4(fn, u):
                act.wait_ge(s_mul, MUL_CR + fn * NMUL)
                for l, s in enumerate(HALVES):
                    act.wait_ge(s_D, fn * (NL + 1) + l + 1)
                    d3 = dist[:, l, :].rearrange("p (n r) -> p n r", r=2 * s)
                    e3 = ex[:, l, :].rearrange("p (n r) -> p n r", r=2 * s)
                    nc.scalar.activation(e3[:, :, s:2 * s], d3[:, :, s:2 * s], ACT.Exp).then_inc(s_ex, 1)
                    nc.scalar.activation(e3[:, :, 0:s], d3[:, :, 0:s], ACT.Exp, scale=-1.0).then_inc(s_ex, 1)
                act.wait_ge(s_D, fn * (NL + 1) + NL + 1)
                half = MP // 2
                nc.scalar.activation(ex[:, NL - 1, 0:half], gc[:, :], ACT.Exp).then_inc(s_ex, 1)
                nc.scalar.activation(ex[:, NL - 1, half:MP], gc[:, :], ACT.Exp, scale=-1.0).then_inc(s_ex, 1)
                nc.scalar.activation(dend[:, u, :], Gs[:, :].rearrange("p (c n) -> p c n", c=MS)[:, :, P - 1], ACT.Exp)
                nc.scalar.activation(exG[:, :], Gs[:, :], ACT.Exp).then_inc(s_ex, 1)
                nc.scalar.activation(exE[:, :], dist[:, NL - 1, :], ACT.Exp, scale=-1.0).then_inc(s_ex, 1)

            fronts = (front1, front2, front3, front4)
            for front in fronts:
                front(0, 0)

            def body(n, u, q):
                for c in range(MS):
                    k = n * MS + c
                    j = (u * MS + c) % 2
                    act.wait_ge(s_dir, DIR_CR + k * GH + GH)
                    act.wait_ge(s_o, O_CR - 1 + k)
                    nc.scalar.copy(A[:, j, :], pd[:, :]).then_inc(s_A, 1)
                    act.wait_ge(s_T, k + 1)
                    nc.scalar.copy(kE[:, :], pu[:, D:D + P]).then_inc(s_kE, 1)
                    if c < len(fronts):
                        fronts[c](n + 1, 1 - u)

            tiles(act, body)

        @block.vector
        def _(dve):
            dve.wait_ge(made, 10 + 3 * NLV)

            def front2(fn, u):
                c0 = fn * 3
                dve.wait_ge(s_Ze, fn + 1)
                nc.vector.tensor_scalar(zn[:, :], zb[:, :], 0.0, None, ALU.min).then_inc(s_chain, 1)
                dve.wait_ge(s_chain, c0 + 1)
                dve.wait_ge(s_gate, fn * 3 + 3)
                nc.vector.tensor_tensor(zn[:, :], zn[:, :], ln[:, :], ALU.subtract).then_inc(s_chain, 1)
                dve.wait_ge(s_chain, c0 + 2)
                dve.wait_ge(s_KB, fn + 1)
                nc.vector.scalar_tensor_tensor(g[:, 0:NM * P], zn[:, 0:NM * P], 1.0 / GATE_NORM, f[1][:, :], ALU.mult,
                                               ALU.mult).then_inc(s_g, 1)
                nc.vector.tensor_scalar(g[:, NM * P:MP], zn[:, NM * P:MP], 1.0 / GATE_NORM, None, ALU.mult).then_inc(s_g, 1)
                dve.wait_ge(s_g, fn * 2 + 2)
                nc.vector.tensor_tensor_scan(Gs[:, :], restart[:, :, :].rearrange("p c n -> p (c n)"), g[:, :], 0.0,
                                             ALU.mult, ALU.add).then_inc(s_chain, 1)

            def front3(fn, u):
                dve.wait_ge(s_chain, fn * 3 + 3)
                for l, s in enumerate(HALVES):
                    G3 = Gs[:, :].rearrange("p (n r) -> p n r", r=2 * s)
                    nc.vector.tensor_tensor(dist[:, l, :].rearrange("p (n r) -> p n r", r=2 * s), G3,
                                            G3[:, :, s - 1:s].to_broadcast([P, MP // (2 * s), 2 * s]),
                                            ALU.subtract).then_inc(s_D, 1)
                G3 = Gs[:, :].rearrange("p (n r) -> p n r", r=P)
                nc.vector.tensor_tensor(dist[:, NL - 1, :].rearrange("p (n r) -> p n r", r=P), G3,
                                        G3[:, :, P - 1:P].to_broadcast([P, MS, P]), ALU.subtract).then_inc(s_D, 1)
                nc.vector.tensor_scalar(gc[:, :], g[:, :].rearrange("p (n r) -> p n r", r=2)[:, :, 1], FLOOR, None,
                                        ALU.max).then_inc(s_D, 1)

            def output(n, u, c):
                k = n * MS + c
                dve.wait_ge(s_o, O_CR + k + 1)
                w = kw[:, u, NM + c:NM + c + 1] if c < NM else None
                if c == 0:
                    nc.vector.tensor_scalar(acc[:, u, :], po[:, :], w, None, ALU.mult).then_inc(s_out, 1)
                else:
                    dve.wait_ge(s_out, OUT_CR + k)
                    if c < NM:
                        nc.vector.scalar_tensor_tensor(acc[:, u, :], po[:, :], w, acc[:, u, :], ALU.mult,
                                                       ALU.add).then_inc(s_out, 1)
                    else:
                        nc.vector.tensor_tensor(acc[:, u, :], po[:, :], acc[:, u, :], ALU.add).then_inc(s_out, 1)
                dve.wait_ge(s_U, k + 1)
                for h in range(GH):
                    r = slice(h * GK, (h + 1) * GK)
                    ins = nc.vector.scalar_tensor_tensor(state[r, c, h * GV:(h + 1) * GV], state[r, c, h * GV:(h + 1) * GV],
                                                         dend[r, u, c:c + 1], pu[r, h * GV:(h + 1) * GV], ALU.mult, ALU.add)
                ins.then_inc(s_S, 1)

            front2(0, 0)
            front3(0, 0)

            def reset(b):
                wait_here(dve, s_S, S_CR + b * (NT * MS), dve_passed)
                nc.vector.memset(state[:, :, :], 0.0).then_inc(s_reset, 1)
                wait_here(dve, s_reset, b + 1, dve_passed)

            def body(n, u, q):
                wait_here(dve, stored[u], ST_CR + q * 16, dve_passed)
                for c in range(MS):
                    k = n * MS + c
                    j = (u * MS + c) % 2
                    if c:
                        output(n, u, c - 1)
                    dve.wait_ge(s_A, A_CR + k + 1)
                    for l in range(NLV):
                        wait_here(dve, s_lv[l % 2], LV_CR + (k * 2 + l // 2) * GH + GH, dve_passed)
                        if l:
                            wait_here(dve, s_cp, CP_CR + k * NLV + l, dve_passed)
                        nc.vector.copy_predicated(
                            A[:, j, :].rearrange("p (h i) -> p h i", h=GH),
                            masks[:, l, :].bitcast(U32).unsqueeze(1).to_broadcast([P, GH, P]),
                            pl[l % 2][:, :].rearrange("p (h i) -> p h i", h=GH)).then_inc(s_cp, 1)
                    if c == 1:
                        front2(n + 1, 1 - u)
                    if c == 2:
                        front3(n + 1, 1 - u)
                output(n, u, MS - 1)

            tiles(dve, body, reset)

        @block.tensor
        def _(pe):
            pe.wait_ge(made, 10)
            pe.wait_ge(w_in, 16 * 10)

            def two(out, lhs, rhs):
                for c in range(KC):
                    ins = nc.tensor.matmul(out, lhs(c), rhs(c), start=(c == 0), stop=(c == KC - 1))
                return ins

            def front1(fn, u, qf):
                pe.wait_ge(ld[u], qf * 32 + 32)
                pe.wait_ge(s_Ve, VE_CR + fn * 3)
                h = lambda c: hT[:, u, c, :]
                two(f[0][:, 0:P], lambda c: wq[:, c, :], h)
                for x in range(3):
                    ins = two(f[0][:, (x + 1) * P:(x + 2) * P], lambda c: wk[:, x, c, :], h)
                ins.then_inc(s_F1, 1)
                for x in range(3, MS):
                    two(f[1][:, (x - 3) * P:(x - 2) * P], lambda c: wk[:, x, c, :], h)
                two(f[1][:, 2 * P:3 * P], lambda c: w1[:, c, 0:NM, :].rearrange("p m r -> p (m r)"), h)
                two(f[1][0:32, 3 * P:4 * P], lambda c: w1[:, c, NM, :], h).then_inc(s_F1, 1)

            def front2(fn, u, qf):
                pe.wait_ge(s_F1e, fn * 2 + 2)
                for x in range(NM):
                    nc.tensor.matmul(f[2][:, x * P:(x + 1) * P], w2[:, x, :], low[:, :], start=True, stop=True)
                ins = nc.tensor.matmul(f[0][:, 0:P], w2s[:, :], low_s[:, :], start=True, stop=True)
                ins.then_inc(s_Z, 2)
                pe.wait_ge(s_kM, fn + 1)
                for x in range(NM):
                    ins = nc.tensor.matmul(f[1][:, x * P:(x + 1) * P], keep_m[:, x, :], ident[:, :], start=True, stop=True)
                ins.then_inc(s_KB, 1)

            def front3(fn, u, qf):
                h = lambda c: hT[:, u, c, :]
                pe.wait_ge(s_Ze, fn + 1)
                for x in range(2):
                    ins = two(f[2][:, x * D:(x + 1) * D], h, lambda c: wv[:, x, c, :])
                ins.then_inc(s_V, 1)
                pe.wait_ge(s_g, fn * 2 + 1)
                for x in range(2):
                    ins = two(f[1][:, x * D:(x + 1) * D], h, lambda c: wv[:, 2 + x, c, :])
                ins.then_inc(s_V, 1)
                two(f[0][:, 0:D], h, lambda c: wv[:, NM, c, :]).then_inc(s_V, 1)

            def direct(n, u, c, h):
                k = n * MS + c
                wait_here(pe, s_dir, DIR_CR + k * GH + h, pe_passed)
                r = slice(h * GK, (h + 1) * GK)
                for l in range(DIRECT):
                    s2 = 2 * HALVES[l]
                    for x in range(P // s2):
                        cols = slice(c * P + x * s2, c * P + (x + 1) * s2)
                        ins = nc.tensor.matmul(pd[x * s2:(x + 1) * s2, h * P + x * s2:h * P + (x + 1) * s2],
                                               kt[r, u, l, cols], qt[r, u, l, cols], start=(l == 0),
                                               stop=(l == DIRECT - 1), skip_group_check=True)
                ins.then_inc(s_dir, 1)

            def level(n, u, c, l, h):
                k = n * MS + c
                if h == 0:
                    pe.wait_ge(s_cp, CP_CR - 1 + k * NLV + l)
                pe.wait_ge(s_lv[l % 2], LV_CR + (k * 2 + l // 2) * GH + h)
                r = slice(h * GK, (h + 1) * GK)
                nc.tensor.matmul(pl[l % 2][:, h * P:(h + 1) * P], kt[r, u, DIRECT + l, c * P:(c + 1) * P],
                                 qt[r, u, DIRECT + l, c * P:(c + 1) * P], start=True, stop=True
                                 ).then_inc(s_lv[l % 2], 1)

            def output(n, u, c):
                k = n * MS + c
                j = (u * MS + c) % 2
                pe.wait_ge(s_cp, CP_CR + k * NLV + NLV)
                pe.wait_ge(s_out, OUT_CR + k)
                pe.wait_ge(s_S, S_CR + k + 1 - MS)
                nc.tensor.matmul(po[:, :], q0[:, u, c * P:(c + 1) * P], state[:, c, :], start=True, stop=False,
                                 skip_group_check=True)
                for h in range(GH):
                    ins = nc.tensor.matmul(po[:, h * GV:(h + 1) * GV], A[:, j, h * P:(h + 1) * P],
                                           V[:, u, c, h * GV:(h + 1) * GV], start=False, stop=True, skip_group_check=True)
                ins.then_inc(s_o, 1)

            front1(0, 0, 0)
            front2(0, 0, 0)
            front3(0, 0, 0)
            fronts = (front1, front2, front3)

            def body(n, u, q):
                pe.wait_ge(s_mul, MUL_CR + n * NMUL + NMUL)
                pe.wait_ge(s_Ve, VE_CR + n * 3 + 3)
                for c in range(MS):
                    k = n * MS + c
                    pe.wait_ge(s_A, A_CR + k)
                    for h in range(GH):
                        direct(n, u, c, h)
                        level(n, u, c, 0, h)
                        level(n, u, c, 1, h)
                    if c:
                        output(n, u, c - 1)
                    pe.wait_ge(s_S, S_CR + k)
                    nc.tensor.transpose(pu[:, D:D + P], kend[:, u, c * P:(c + 1) * P], ident[:, :]).then_inc(s_T, 1)
                    for h in range(GH):
                        level(n, u, c, 2, h)
                        level(n, u, c, 3, h)
                    pe.wait_ge(s_kE, k + 1)
                    nc.tensor.matmul(pu[:, 0:D], kE[:, :], V[:, u, c, :], start=True, stop=True).then_inc(s_U, 1)
                    if c < len(fronts):
                        fronts[c](n + 1, 1 - u, q + u)
                output(n, u, MS - 1)

            tiles(pe, body, lambda b: wait_here(pe, s_reset, b + 1, pe_passed))


RMS_EPS = 1e-5


def phase_final(nc, x, hT_dram, o_dram, w_g, w_o, norm_w, x_out):
    with ExitStack() as ctx:
        m = Mem(nc, ctx, "fn_")
        G = 4
        W = G * P
        NS = T // W
        ident, eps = m.sb("ident", [P, P]), m.sb("eps", [P, 1])
        wg, wo = m.sb("wg", [P, KC, D]), m.sb("wo", [P, KC, D])
        nw = m.sb("nw", [P, GV])
        o, x_s = m.sb("o", [P, 2, G, D]), m.sb("x", [P, 2, G, D])
        hT = m.sb("hT", [P, 2, KC, W])
        sq = m.sb("sq", [P, G * D])
        ss, rms, inv = m.sb("ss", [P, G * GH]), m.sb("rms", [P, G * GH]), m.sb("inv", [P, G * GH])
        silu = m.sb("silu", [P, G * D])
        gate, y = m.sb("gate", [P, G * D]), m.sb("y", [P, G * D])
        yT = m.sb("yT", [P, KC, W])
        z = m.sb("z", [P, 2, G, D])
        p_g, p_T, p_z = m.ps("p_g", [P, G * D]), m.ps("p_T", [P, KC, W]), m.ps("p_z", [P, G * D])
        made, w_in = m.sem("made"), m.sem("w_in")
        o_in, xh_in = [m.sem(f"o_in{u}") for u in range(2)], [m.sem(f"xh_in{u}") for u in range(2)]
        stored = [m.sem(f"stored{u}") for u in range(2)]
        s_g, s_silu, s_gate, s_chain, s_rms, s_y = (m.sem(k) for k in ("g", "silu", "gate", "chain", "rms", "y"))
        s_T, s_yT, s_zmm, s_z = (m.sem(k) for k in ("T", "yT", "zmm", "z"))
        sp_passed = m.sem("sp_passed")
        CH = 4
        Z_CR, Y_CR, OUT_CR, GATE_CR, SILU_CR = 1, 1, 1, 1, 1
        block = ctx.enter_context(nc.Block())

        @block.sync
        def _(sp):
            sp.dma_start(wg[:, :, :], w_g).then_inc(w_in, 16)
            sp.dma_start(wo[:, :, :], w_o).then_inc(w_in, 16)
            sp.dma_start(nw[:, :], norm_w.to_broadcast([P, GV])).then_inc(w_in, 16)
            for sem, credits in ((s_z, Z_CR), (s_y, Y_CR), (stored[0], OUT_CR), (stored[1], OUT_CR), (s_gate, GATE_CR), (s_silu, SILU_CR)):
                sp.sem_inc(sem, credits)

            def load(n, u):
                sp.dma_start(o[:, u, :, :], rows(o_dram, n * W, G)).then_inc(o_in[u], 16)
                sp.dma_start(hT[:, u, :, :], hT_dram[:, :, ds(n * W, W)].rearrange("k p t -> p k t")).then_inc(xh_in[u], 16)
                sp.dma_start(x_s[:, u, :, :], rows(x, n * W, G)).then_inc(xh_in[u], 16)

            def store(n, u):
                wait_here(sp, s_z, Z_CR + n + 1, sp_passed)
                sp.dma_start(rows(x_out, n * W, G), z[:, u, :, :]).then_inc(stored[u], 16)

            load(0, 0)
            load(1, 1)
            with sp.Fori(0, NS // 2 - 1) as q:
                for u in range(2):
                    store(q * 2 + u, u)
                    load(q * 2 + (u + 2), u)
            for u in range(2):
                store(NS - 2 + u, u)
            for u in range(2):
                sp.wait_ge(stored[u], OUT_CR + NS // 2 * 16)

        @block.gpsimd
        def _(pool):
            make_identity(pool, ident, made)
            pool.memset(eps[:, :], RMS_EPS).then_inc(made, 1)
            pool.wait_ge(w_in, 48)
            with pool.Fori(0, NS) as n:
                pool.wait_ge(s_silu, SILU_CR + n + 1)
                pool.wait_ge(s_y, Y_CR + n)
                pool.tensor_tensor(out=gate[:, :].rearrange("p (n e) -> p n e", e=GV),
                                   in0=silu[:, :].rearrange("p (n e) -> p n e", e=GV),
                                   in1=nw[:, :].unsqueeze(1).to_broadcast([P, G * GH, GV]), op=ALU.mult
                                   ).then_inc(s_gate, 1)

        @block.scalar
        def _(act):
            act.wait_ge(made, 3)
            with act.Fori(0, NS) as n:
                act.wait_ge(s_chain, n * CH + 2)
                nc.scalar.activation(rms[:, :], ss[:, :], ACT.Sqrt, bias=eps[:, 0:1], scale=1.0 / GV).then_inc(s_rms, 1)
                act.wait_ge(s_g, n + 1)
                act.wait_ge(s_gate, GATE_CR + n)
                nc.scalar.activation(silu[:, :], p_g[:, :], ACT.Silu).then_inc(s_silu, 1)
                for k in range(KC):
                    act.wait_ge(s_T, n * KC + k + 1)
                    nc.scalar.copy(yT[:, k, :], p_T[:, k, :]).then_inc(s_yT, 1)

        @block.vector
        def _(dve):
            def norm(n, u, q):
                dve.wait_ge(o_in[u], q * 16 + 16)
                of = o[:, u, :, :].rearrange("p t d -> p (t d)")
                nc.vector.tensor_tensor(sq[:, :], of, of, ALU.mult).then_inc(s_chain, 1)
                dve.wait_ge(s_chain, n * CH + 1)
                nc.vector.tensor_reduce(ss[:, :], sq[:, :].rearrange("p (n e) -> p n e", e=GV), AX.X,
                                        ALU.add).then_inc(s_chain, 1)
                dve.wait_ge(s_rms, n + 1)
                nc.vector.reciprocal(inv[:, :], rms[:, :]).then_inc(s_chain, 1)
                dve.wait_ge(s_chain, n * CH + 3)
                nc.vector.tensor_tensor(sq[:, :].rearrange("p (n e) -> p n e", e=GV),
                                        of.rearrange("p (n e) -> p n e", e=GV),
                                        inv[:, :].unsqueeze(2).to_broadcast([P, G * GH, GV]), ALU.mult).then_inc(s_chain, 1)

            def residual(n, u, q):
                dve.wait_ge(s_zmm, n + 1)
                dve.wait_ge(xh_in[u], q * 32 + 32)
                dve.wait_ge(stored[u], OUT_CR + q * 16)
                nc.vector.tensor_tensor(z[:, u, :, :].rearrange("p t d -> p (t d)"), p_z[:, :],
                                        x_s[:, u, :, :].rearrange("p t d -> p (t d)"), ALU.add).then_inc(s_z, 1)

            with dve.Fori(0, NS // 2) as q:
                for u in range(2):
                    n = q * 2 + u
                    norm(n, u, q)
                    dve.wait_ge(s_chain, n * CH + 4)
                    dve.wait_ge(s_gate, GATE_CR + n + 1)
                    nc.vector.tensor_tensor(y[:, :], sq[:, :], gate[:, :], ALU.mult).then_inc(s_y, 1)
                    residual(n, u, q)

        @block.tensor
        def _(pe):
            pe.wait_ge(made, 2)
            pe.wait_ge(w_in, 48)

            def gates(n, u, q):
                pe.wait_ge(xh_in[u], q * 32 + 32)
                pe.wait_ge(s_silu, SILU_CR + n)
                for t in range(G):
                    for k in range(KC):
                        ins = nc.tensor.matmul(p_g[:, t * D:(t + 1) * D], hT[:, u, k, t * P:(t + 1) * P], wg[:, k, :],
                                               start=(k == 0), stop=(k == KC - 1))
                ins.then_inc(s_g, 1)

            with pe.Fori(0, NS // 2) as q:
                for u in range(2):
                    n = q * 2 + u
                    gates(n, u, q)
                    pe.wait_ge(s_y, Y_CR + n + 1)
                    for k in range(KC):
                        for t in range(G):
                            ins = nc.tensor.transpose(p_T[:, k, t * P:(t + 1) * P], y[:, t * D + k * P:t * D + (k + 1) * P],
                                                      ident[:, :])
                        ins.then_inc(s_T, 1)
                    pe.wait_ge(s_yT, n * KC + KC)
                    pe.wait_ge(s_z, Z_CR + n)
                    for t in range(G):
                        for k in range(KC):
                            ins = nc.tensor.matmul(p_z[:, t * D:(t + 1) * D], yT[:, k, t * P:(t + 1) * P], wo[:, k, :],
                                                   start=(k == 0), stop=(k == KC - 1))
                    ins.then_inc(s_zmm, 1)


def build(nc, a):
    def scratch(name, shape, dt=F32):
        return nc.dram_tensor(name, shape, dt).ap()

    x1, x2, x3 = (scratch(k, [T, D]) for k in ("x_attn_a", "x_ffn", "x_attn_b"))

    q_parts, k_parts = scratch("q_parts", [3, B * D, L], BF16), scratch("k_parts", [3, B * D, L], BF16)
    q_full = scratch("q_full", [D, T])
    k_tok, v_tok = scratch("k_tok", [B * H, P, NT * DH]), scratch("v_tok", [B * H, P, NT * DH])
    y_dram, kv_dram = scratch("y_terrace", [T, D]), scratch("kv_sums", [B * H, R, DH * DH])
    phase_project(nc, a["x"], a["a_wq"], a["a_wk"], a["a_wkv"], q_parts, k_parts, q_full, k_tok, v_tok)
    phase_attend(nc, q_parts, k_parts, k_tok, v_tok, a["a_mix"], a["a_index_decays"], a["a_mega_decays"], y_dram,
                 kv_dram)
    phase_merge(nc, a["x"], q_full, y_dram, kv_dram, a["a_mix"], a["a_wc"], x1)

    phase_moe(nc, x1, a["f_gate"], a["f_wg"], a["f_wu"], a["f_wd"], x2, "m1_")

    hT_dram = scratch("hT", [KC, P, T + 2 * P])
    kw_dram = scratch("keep_weights", [NTT + 2, P, 2 * NM])
    o_dram = scratch("o_gla", [T, D])
    phase_route(nc, x2, a["b_gate"], hT_dram, kw_dram)
    phase_gla(nc, hT_dram, kw_dram, a["b_wq"], a["b_wk"], a["b_wv"], a["b_gk1"], a["b_gk2"], a["b_bias"], o_dram)
    phase_final(nc, x2, hT_dram, o_dram, a["b_wg"], a["b_wo"], a["b_norm"], x3)

    phase_moe(nc, x3, a["f_gate"], a["f_wg"], a["f_wu"], a["f_wd"], a["out"], "m2_")


def kernel(**inputs):
    import concourse.bacc as bacc
    from concourse.bass_utils import run_bass_kernel_spmd

    def chunks(w):
        return np.ascontiguousarray(w.reshape(KC, P, -1).transpose(1, 0, 2))

    def stacked(w, shared):
        return np.concatenate([w, shared[None]]).reshape(len(w) + 1, KC, P, -1).transpose(2, 0, 1, 3)

    def part(prefix):
        return {k[len(prefix):]: np.asarray(v) for k, v in inputs.items() if k.startswith(prefix)}

    a, b, f = part("L0_attn_a_"), part("L0_attn_b_"), part("L0_ffn_")
    arrays = {
        "x": a["hidden_states"].reshape(T, D),
        "a_wq": chunks(a["Wq"].T),
        "a_wk": chunks(a["Wk"].T),
        "a_wc": chunks(a["Wc"].T),
        "a_wkv": np.concatenate([chunks(a["Wk"].T), chunks(a["Wv"].T)], axis=2),
        "a_mix": a["terrace_mix"].reshape(SEG, 1),
        "a_index_decays": a["index_decays"].T,
        "a_mega_decays": a["mega_decays"].reshape(1, H),
        "b_gate": chunks(b["w_gate"]),
        "b_wq": chunks(b["w_q"]),
        "b_wk": stacked(b["w_k"], b["w_ks"]),
        "b_wv": stacked(b["w_v"], b["w_vs"]),
        "b_gk1": stacked(b["w_gk1"], b["w_gk1s"]).transpose(0, 2, 1, 3),
        "b_gk2": np.concatenate([b["w_gk2"], b["w_gk2s"][None]]),
        "b_bias": np.concatenate([b["b_gk"], b["b_gks"][None]]).T,
        "b_wg": chunks(b["w_g"]),
        "b_wo": chunks(b["w_o"]),
        "b_norm": b["norm_w"].reshape(1, GV),
        "f_gate": chunks(f["gate_w"].T),
        "f_wg": stacked(f["w_gate"], f["ws_gate"]),
        "f_wu": stacked(f["w_up"], f["ws_up"]),
        "f_wd": np.concatenate([f["w_down"], f["ws_down"][None]]).transpose(1, 0, 2),
    }
    nc = bacc.Bacc("TRN2", target_bir_lowering=False, num_devices=1)
    sent, aps = {}, {}
    for name, v in arrays.items():
        v = np.ascontiguousarray(v)
        sent["in_" + name] = v
        aps[name] = nc.dram_tensor("in_" + name, v.shape, mybir.dt.from_np(v.dtype), kind="ExternalInput").ap()
    aps["out"] = nc.dram_tensor("out", [T, D], F32, kind="ExternalOutput").ap()
    build(nc, aps)
    r = run_bass_kernel_spmd(nc, [sent], core_ids=[0])
    return r.results[0]["out"].reshape(B, L, D)
```

```python
import numpy as np
import concourse.bass as bass
from concourse import mybir
from contextlib import ExitStack

F32 = mybir.dt.float32
BF16 = mybir.dt.bfloat16
U32 = mybir.dt.uint32
ALU = mybir.AluOpType
ACT = mybir.ActivationFunctionType
AX = mybir.AxisListType
ds = bass.ds

P = 128
B, L, D = 2, 2048, 256
T = B * L
KC = D // P
NT = L // P
LN_EPS = 1e-5

H, DH, SEG = 16, 16, 64
R = L // SEG
HH = H // 2
NOISE_EPS = 1e-5
MASKED = 1.0e30
CW = 512
NCQ = L // CW
SCALE = float(DH) ** -0.5
Q_PARTS = ((0, 3), (0, 2), (0, 1))
K_REPS = (3, 2, 1)
SLOTS = 6


class Mem:

    def __init__(self, nc, ctx, tag):
        self.nc, self.ctx, self.tag = nc, ctx, tag
        self.sems = []
        ctx.callback(self.clear)

    def sb(self, name, shape, dt=F32):
        return self.ctx.enter_context(self.nc.sbuf_tensor(self.tag + name, shape, dt))

    def ps(self, name, shape, dt=F32):
        return self.ctx.enter_context(self.nc.psum_tensor(self.tag + name, shape, dt))

    def sem(self, name):
        self.sems.append(self.nc.alloc_semaphore(self.tag + name))
        return self.sems[-1]

    def clear(self):
        self.nc.clear_and_free_semaphores(self.sems)
        self.nc.all_engine_barrier()


def wait_here(eng, sem, value, passed):
    eng.wait_ge(sem, value)
    eng.sem_inc(passed, 1)


def rows(dram, at, tiles):
    return dram[ds(at, tiles * P), :].rearrange("(t p) n -> p t n", p=P)


def make_identity(pool, ident, made):
    pool.memset(ident[:, :], 0.0).then_inc(made, 1)
    pool.wait_ge(made, 1)
    pool.affine_select(out=ident[:, :], in_=ident[:, :], compare_op=ALU.not_equal, fill=1.0, base=0,
                       pattern=[[-1, P]], channel_multiplier=1).then_inc(made, 1)


def phase_project(nc, x, wq, wk, wkv, q_parts, k_parts, q_full, k_tok, v_tok):
    with ExitStack() as ctx:
        m = Mem(nc, ctx, "pj_")
        G = 4
        W = G * P
        ident = m.sb("ident", [P, P])
        wq_s, wk_s = m.sb("wq", [P, KC, D]), m.sb("wk", [P, KC, D])
        wkv_s = m.sb("wkv", [P, KC, 2 * D])
        x_s = m.sb("x", [P, G, D])
        stats, mv = m.sb("stats", [P, G, 6]), m.sb("mv", [P, G, 2])
        std, rstd = m.sb("std", [P, G]), m.sb("rstd", [P, G])
        eps = m.sb("eps", [P, 1])
        hn = m.sb("hn", [P, G, D])
        hT = m.sb("hT", [P, KC, W])
        full = m.sb("full", [P, 4, W])
        part = m.sb("part", [P, 4, 3, W], BF16)
        rest = m.sb("rest", [P, 2, W])
        kv = m.sb("kv", [P, 2, B, H, NT * DH])
        p_T = m.ps("T", [P, KC, W])
        p_qk = [m.ps(f"qk{j}", [P, W]) for j in range(4)]
        p_kv = [m.ps(f"kv{j}", [P, 2 * D]) for j in range(2)]
        w_in, x_in = m.sem("w_in"), m.sem("x_in")
        made, eps_set = m.sem("made"), m.sem("eps_set")
        stat_done, var_done, std_done, rstd_done = m.sem("stat"), m.sem("var"), m.sem("std"), m.sem("rstd")
        hn_done, T_done, hT_done = m.sem("hn"), m.sem("T"), m.sem("hT")
        qk_done, full_done, kv_done, kv_kept = m.sem("qk"), m.sem("full"), m.sem("kv_mm"), m.sem("kv_kept")
        part_done, stored, kv_stored = m.sem("part"), m.sem("stored"), m.sem("kv_stored")
        steps = L // W
        NS = B * steps
        sp_passed, dve_passed = m.sem("sp_passed"), m.sem("dve_passed")
        block = ctx.enter_context(nc.Block())

        @block.sync
        def _(sp):
            sp.dma_start(wq_s[:, :, :], wq).then_inc(w_in, 16)
            sp.dma_start(wk_s[:, :, :], wk).then_inc(w_in, 16)
            sp.dma_start(wkv_s[:, :, :], wkv).then_inc(w_in, 16)
            sp.sem_inc(hn_done, 1)
            sp.sem_inc(stored, 1)
            with sp.Fori(0, B) as b:
                with sp.Fori(0, steps) as st:
                    n = b * steps + st
                    wait_here(sp, hn_done, n * G + 1, sp_passed)
                    sp.dma_start(x_s[:, :, :], rows(x, b * L + st * W, G)).then_inc(x_in, 16)
                    for j in range(4):
                        wait_here(sp, part_done, n * 16 + 4 * j + 4, sp_passed)
                        dst, half = (q_parts, k_parts)[j // 2], j % 2 * P
                        sp.dma_start(dst[:, ds(b * D + half, P), ds(st * W, W)].rearrange("s p t -> p s t"),
                                     part[:, j, :, :]).then_inc(stored, 16)
                        if j < 2:
                            sp.dma_start(q_full[half:half + P, ds(b * L + st * W, W)], full[:, j, :]).then_inc(stored, 16)
            sp.wait_ge(kv_kept, NS * G + 2)
            for j, dst in enumerate((k_tok, v_tok)):
                sp.dma_start(dst.rearrange("h p n -> p h n"),
                             kv[:, j, :, :, :].rearrange("p b h n -> p (b h) n")).then_inc(kv_stored, 16)
            sp.wait_ge(kv_stored, 32)
            sp.wait_ge(stored, NS * 96 + 1)

        @block.gpsimd
        def _(pool):
            make_identity(pool, ident, made)
            pool.memset(eps[:, :], LN_EPS).then_inc(eps_set, 1)

        @block.vector
        def _(dve):
            with dve.Fori(0, NS) as n:
                dve.wait_ge(x_in, n * 16 + 16)
                for t in range(G):
                    nc.vector.bn_stats(stats[:, t, :], x_s[:, t, :]).then_inc(stat_done, 1)
                wait_here(dve, stat_done, n * G + G, dve_passed)
                for t in range(G):
                    nc.vector.bn_aggr(mv[:, t, :], stats[:, t, :]).then_inc(var_done, 1)
                dve.wait_ge(std_done, n + 1)
                nc.vector.reciprocal(rstd[:, :], std[:, :]).then_inc(rstd_done, 1)
                dve.wait_ge(rstd_done, n + 1)
                for t in range(G):
                    ins = nc.vector.tensor_scalar(hn[:, t, :], x_s[:, t, :], mv[:, t, 0:1], rstd[:, t:t + 1],
                                                  ALU.subtract, ALU.mult)
                    ins.then_inc(hn_done, 1)
                dve.wait_ge(stored, n * 96 + 1)
                for j in range(4):
                    dve.wait_ge(full_done, n * 4 + j + 1)
                    factor = -SCALE if j < 2 else 1.0
                    nc.vector.tensor_scalar(part[:, j, 0, :], full[:, j, :], factor, None, ALU.mult).then_inc(part_done, 1)
                    dve.wait_ge(part_done, n * 16 + 4 * j + 1)
                    nc.vector.scalar_tensor_tensor(rest[:, j % 2, :], full[:, j, :], factor, part[:, j, 0, :],
                                                   ALU.mult, ALU.subtract).then_inc(part_done, 1)
                    dve.wait_ge(part_done, n * 16 + 4 * j + 2)
                    nc.vector.tensor_copy(part[:, j, 1, :], rest[:, j % 2, :]).then_inc(part_done, 1)
                    dve.wait_ge(part_done, n * 16 + 4 * j + 3)
                    nc.vector.tensor_tensor(part[:, j, 2, :], rest[:, j % 2, :], part[:, j, 1, :],
                                            ALU.subtract).then_inc(part_done, 1)

        @block.scalar
        def _(act):
            act.wait_ge(eps_set, 1)
            with act.Fori(0, B) as b:
                with act.Fori(0, steps) as s:
                    n = b * steps + s
                    act.wait_ge(var_done, n * G + G)
                    nc.scalar.activation(std[:, :], mv[:, :, 1], ACT.Sqrt, bias=eps[:, 0:1]).then_inc(std_done, 1)
                    for k in range(KC):
                        act.wait_ge(T_done, n * KC + k + 1)
                        nc.scalar.copy(hT[:, k, :], p_T[:, k, :]).then_inc(hT_done, 1)
                    act.wait_ge(stored, n * 96 + 1)
                    for j in range(4):
                        act.wait_ge(qk_done, n * 4 + j + 1)
                        nc.scalar.copy(full[:, j, :], p_qk[j][:, :]).then_inc(full_done, 1)
                    for t in range(G):
                        act.wait_ge(kv_done, n * G + t + 1)
                        for j in range(2):
                            dst = kv[:, j, ds(b, 1), :, ds(s * (G * DH) + t * DH, DH)].rearrange(
                                "p a h e -> p (a h) e")
                            ins = nc.scalar.copy(dst, p_kv[t % 2][:, j * D:(j + 1) * D].rearrange(
                                "p (h e) -> p h e", h=H))
                        ins.then_inc(kv_kept, 1)

        @block.tensor
        def _(pe):
            pe.wait_ge(made, 2)
            pe.wait_ge(w_in, 48)
            pe.sem_inc(kv_kept, 2)
            with pe.Fori(0, NS) as n:
                pe.wait_ge(hn_done, n * G + G + 1)
                for k in range(KC):
                    for t in range(G):
                        ins = nc.tensor.transpose(p_T[:, k, t * P:(t + 1) * P], hn[:, t, k * P:(k + 1) * P], ident[:, :])
                    ins.then_inc(T_done, 1)
                pe.wait_ge(hT_done, n * KC + KC)
                for j in range(4):
                    w = (wq_s, wk_s)[j // 2]
                    for k in range(KC):
                        ins = nc.tensor.matmul(p_qk[j][:, :], w[:, k, (j % 2) * P:(j % 2 + 1) * P], hT[:, k, :],
                                               start=(k == 0), stop=(k == KC - 1))
                    ins.then_inc(qk_done, 1)
                for t in range(G):
                    pe.wait_ge(kv_kept, n * G + t + 1)
                    for k in range(KC):
                        ins = nc.tensor.matmul(p_kv[t % 2][:, :], hT[:, k, t * P:(t + 1) * P], wkv_s[:, k, :],
                                               start=(k == 0), stop=(k == KC - 1))
                    ins.then_inc(kv_done, 1)
                pe.wait_ge(full_done, n * 4 + 4)


def phase_attend(nc, q_parts, k_parts, k_tok, v_tok, terrace_mix, index_decays, mega_decays, y_dram, kv_dram):
    with ExitStack() as ctx:
        m = Mem(nc, ctx, "at_")
        TW = SEG + P
        KVW = DH * DH + 1
        chunks = [[(c, min(CW, i * P - c)) for c in range(0, i * P, CW)] for i in range(NT)]
        first_chunk = [sum(len(c) for c in chunks[:i]) for i in range(NT + 1)]
        NCH = first_chunk[NT]
        NS_B = 3
        assert NCH % NS_B == 0 and R == 32
        first_t = [0] + [1 + 2 * i for i in range(NT)]
        NTX = first_t[NT]
        KK = 1 + NCQ
        EB = 4
        PAD = R - 2
        ident = m.sb("ident", [P, P])
        mask = m.sb("mask", [P, TW])
        tw, tmix = m.sb("tw", [P, 1]), m.sb("tmix", [P, 1])
        dec = m.sb("dec", [P, H])
        eid = m.sb("eid", [P, H + 1, 2])
        lam, lam_raw = m.sb("lam", [R, H]), m.sb("lam_raw", [R, H])
        gap = m.sb("gap", [R, R])
        gap_i = m.sb("gap_i", [R, R], mybir.dt.int32)
        decay = m.sb("decay", [R, H + 1, R])
        sq, sk = m.sb("sq", [SLOTS * DH, 2, L], BF16), m.sb("sk", [SLOTS * DH, 2, L], BF16)
        kh, vh = m.sb("kh", [P, 2, NT * DH]), m.sb("vh", [P, 2, (NT + 1) * DH])
        vs = m.sb("vs", [SEG, 2, (NT + 1) * DH])
        kvo = m.sb("kvo", [P, NT, KVW])
        eid_h, decay_h = m.sb("eid_h", [P, 2, 2]), m.sb("decay_h", [R, 2, R])
        E = m.sb("E", [P, EB, L])
        Wm = m.sb("Wm", [P, EB, TW])
        Tt = m.sb("Tt", [P, EB, TW])
        TTs = m.sb("TTs", [P, 2 * P])
        mn, top = m.sb("mn", [P, 2, NT, KK]), m.sb("top", [P, 2, NT])
        f, rs, rp = m.sb("f", [P, 2, NT, KK]), m.sb("rs", [P, 2, NT, KK]), m.sb("rp", [P, 2, NT])
        fr, tot, inv = m.sb("fr", [P, NT, KK]), m.sb("tot", [P, NT]), m.sb("inv", [P, NT])
        tot_t, inv_t = m.sb("tot_t", [P, NT]), m.sb("inv_t", [P, NT])
        c2 = m.sb("c2", [P, 2, KK, 2 * PAD + 2])
        Y_h = m.sb("Y_h", [P, 2, NT, DH])
        Y = m.sb("Y", [P, B, NT, D])
        pcs_s, pcsT = m.sb("pcs_s", [P, CW]), m.sb("pcsT", [P, CW])
        OT_s = m.sb("OT_s", [P, CW])
        kvr, kvn = m.sb("kvr", [R, KVW]), m.sb("kvn", [R, 2, DH * DH])
        den, rden = m.sb("den", [R, 1]), m.sb("rden", [R, 1])
        S = [m.ps(f"S{j}", [P, CW]) for j in range(NS_B)]
        S_W = m.ps("S_W", [P, 512])
        TT = m.ps("TT", [P, 512])
        pcs = m.ps("pcs", [P, CW])
        OT = m.ps("OT", [P, CW])
        misc = m.ps("misc", [P, 512])

        made, cin, cdone = m.sem("made"), m.sem("const_in"), m.sem("const_done")
        loaded = [m.sem(f"loaded{u}") for u in range(2)]
        LOADS = 16 * (2 * SLOTS + 3)
        passed, pool_passed, dve_passed, pe_passed, act_passed = (
            m.sem(k + "passed") for k in ("sp_", "pool_", "dve_", "pe_", "act_"))
        s_small, s_kvo = m.sem("small"), m.sem("kvo")
        s_S, s_mn, s_E = m.sem("S_done"), m.sem("mn"), m.sem("E_done")
        s_W, s_Wm, s_T = m.sem("W_done"), m.sem("W_read"), m.sem("T_done")
        s_top, s_f = m.sem("top"), m.sem("f")
        s_step, s_c2 = m.sem("step"), m.sem("c2")
        s_TT, s_TTs, s_O = m.sem("TT"), m.sem("TTs"), m.sem("O")
        s_P, s_pc = m.sem("pcs_mm"), m.sem("pcs_copy")
        s_pT, s_pTs, s_OTs, s_OTT = m.sem("pT"), m.sem("pTs"), m.sem("OTs"), m.sem("OTT")
        s_KV, s_kvr, s_K2 = m.sem("KV"), m.sem("kvr"), m.sem("KV2")
        s_den, s_kvn, s_inv = m.sem("den"), m.sem("kvn"), m.sem("inv")
        s_Yh, s_Y, y_out = m.sem("Yh"), m.sem("Y"), m.sem("y_out")
        kv_out = [m.sem(f"kv_out{u}") for u in range(2)]
        E_CR, W_CR, T_CR, P_CR, O_CR = NS_B, 1, 2 * EB, EB, 1
        KV_CR, K2_CR, Y_CR, KVN_CR, PC_CR, TTS_CR, OUT_CR, OTS_CR, YH_CR = 1, 2, 2, 1, 1, 1, 1, 1, 1
        NHEAD = B * H
        block = ctx.enter_context(nc.Block())

        @block.sync
        def _(sp):
            for u in range(2):
                sp.dma_start(tmix[u * SEG:(u + 1) * SEG, :], terrace_mix).then_inc(cin, 16)
                sp.dma_start(dec[u * SEG:(u + 1) * SEG, :], index_decays).then_inc(cin, 16)
            sp.dma_start(lam_raw[:, :], mega_decays.to_broadcast([R, H])).then_inc(cin, 16)
            for sem, credits in ((s_E, E_CR), (s_Wm, W_CR), (s_T, T_CR), (s_P, P_CR), (s_O, O_CR), (s_KV, KV_CR),
                                 (s_K2, K2_CR), (s_Y, Y_CR), (s_kvn, KVN_CR), (s_TTs, TTS_CR),
                                 (s_OTs, OTS_CR), (s_Yh, YH_CR), (kv_out[0], OUT_CR), (kv_out[1], OUT_CR)):
                sp.sem_inc(sem, credits)

            def load(head, u):
                slot = 0
                for lo, hi in Q_PARTS:
                    for part in range(lo, hi):
                        sp.dma_start(sq[slot * DH:(slot + 1) * DH, u, :],
                                     q_parts[part, ds(head * DH, DH), :]).then_inc(loaded[u], 16)
                        slot += 1
                slot = 0
                for part, reps in enumerate(K_REPS):
                    for _ in range(reps):
                        sp.dma_start(sk[slot * DH:(slot + 1) * DH, u, :],
                                     k_parts[part, ds(head * DH, DH), :]).then_inc(loaded[u], 16)
                        slot += 1
                for dst, src in ((kh[:, u, :], k_tok[ds(head, 1), :, :]),
                                 (vh[:, u, 0:NT * DH], v_tok[ds(head, 1), :, :]),
                                 (vs[:, u, DH:NT * DH], v_tok[ds(head, 1), SEG:P, 0:(NT - 1) * DH])):
                    sp.dma_start(dst, src.rearrange("a p n -> (a p) n")).then_inc(loaded[u], 16)

            def store(head, u):
                wait_here(sp, s_kvn, KVN_CR + head + 1, passed)
                sp.dma_start(kv_dram[ds(head, 1), :, :].rearrange("a r n -> (a r) n"), kvn[:, u, :]
                             ).then_inc(kv_out[u], 16)

            load(0, 0)
            load(1, 1)
            with sp.Fori(0, NHEAD // 2 - 1) as q:
                for u in range(2):
                    store(q * 2 + u, u)
                    load(q * 2 + (u + 2), u)
            store(NHEAD - 2, 0)
            load(0, 0)
            store(NHEAD - 1, 1)
            sp.wait_ge(s_Y, Y_CR + NHEAD)
            for b in range(B):
                sp.dma_start(y_dram[b * L:(b + 1) * L, :].rearrange("(t p) n -> p t n", p=P),
                             Y[:, b, :, :]).then_inc(y_out, 16)
            sp.wait_ge(y_out, 16 * B)
            for u in range(2):
                sp.wait_ge(kv_out[u], OUT_CR + 8 * NHEAD)
            sp.wait_ge(loaded[0], (NHEAD // 2 + 1) * LOADS)

        @block.gpsimd
        def _(pool):
            make_identity(pool, ident, made)
            pool.memset(mask[:, :], 0.0).then_inc(made, 1)
            pool.wait_ge(made, 3)
            pool.affine_select(out=mask[:, :], in_=mask[:, :], compare_op=ALU.is_ge, fill=MASKED, base=SEG,
                               pattern=[[-1, TW]], channel_multiplier=1).then_inc(made, 1)
            pool.wait_ge(made, 4)
            pool.memset(mask[SEG:P, 0:SEG], MASKED).then_inc(made, 1)
            pool.wait_ge(made, 5)
            pool.memset(eid[:, :, :], 0.0).then_inc(made, 1)
            pool.iota(gap_i[:, :], pattern=[[1, R]], base=-1, channel_multiplier=-1).then_inc(made, 1)
            pool.memset(kvo[:, :, DH * DH:KVW], 1.0).then_inc(made, 1)
            pool.memset(c2[:, :, :, :], 0.0).then_inc(made, 1)
            pool.memset(vh[:, :, NT * DH:(NT + 1) * DH], 0.0).then_inc(made, 1)
            pool.memset(vs[:, :, NT * DH:(NT + 1) * DH], 0.0).then_inc(made, 1)
            pool.wait_ge(cdone, 3 + H)
            pool.affine_select(out=decay[:, 0:H, :], in_=decay[:, 0:H, :], compare_op=ALU.is_gt, fill=0.0, base=0,
                               pattern=[[0, H], [1, R]], channel_multiplier=-1).then_inc(made, 1)
            pool.wait_ge(made, 12)
            pool.tensor_copy(eid[:, H, :], eid[:, 0, :]).then_inc(made, 1)
            pool.tensor_copy(decay[:, H, :], decay[:, 0, :]).then_inc(made, 1)
            pool.wait_ge(made, 14)

            def constants(h, u):
                pool.tensor_copy(eid_h[:, u, :], eid[:, ds(h, 1), :].rearrange("p a c -> p (a c)")).then_inc(s_small, 1)
                pool.tensor_copy(decay_h[:, u, :], decay[:, ds(h, 1), :].rearrange("p a c -> p (a c)")
                                 ).then_inc(s_small, 1)

            constants(0, 0)
            with pool.Fori(0, B) as b:
                with pool.Fori(0, H // 2) as hp:
                    for u in range(2):
                        n = b * H + hp * 2 + u
                        pool.wait_ge(loaded[u], (b * (H // 2) + hp) * LOADS + LOADS)
                        pool.sem_inc(pool_passed, 1)
                        wait_here(pool, s_KV, KV_CR + n, pool_passed)
                        k3 = kh[:, u, :].rearrange("p (t d) -> p t d", t=NT)
                        v3 = vh[:, u, 0:NT * DH].rearrange("p (t d) -> p t d", t=NT)
                        for t in range(NT):
                            ins = pool.tensor_tensor(
                                out=kvo[:, t, 0:DH * DH].rearrange("p (d e) -> p d e", d=DH),
                                in0=k3[:, t, :].unsqueeze(2).to_broadcast([P, DH, DH]),
                                in1=v3[:, t, :].unsqueeze(1).to_broadcast([P, DH, DH]), op=ALU.mult)
                        ins.then_inc(s_kvo, 1)
                        wait_here(pool, s_K2, K2_CR + n, pool_passed)
                        constants(hp * 2 + (u + 1), 1 - u)
                        wait_here(pool, s_Yh, YH_CR + n + 1, pool_passed)
                        pool.tensor_copy(Y[:, ds(b, 1), :, ds(hp * (2 * DH) + u * DH, DH)].rearrange(
                            "p a t e -> p (a t) e"), Y_h[:, u, :, :]).then_inc(s_Y, 1)

        @block.scalar
        def _(act):
            act.wait_ge(cin, 80)
            act.wait_ge(made, 11)
            nc.scalar.activation(tw[:, :], tmix[:, :], ACT.Sigmoid).then_inc(cdone, 1)
            for u in range(2):
                nc.scalar.activation(eid[u * SEG:(u + 1) * SEG, 0:H, u], dec[u * SEG:(u + 1) * SEG, :],
                                     ACT.Exp).then_inc(cdone, 1)
            act.wait_ge(s_den, 3)
            for h in range(H):
                nc.scalar.activation(decay[:, h, :], gap[:, :], ACT.Exp, scale=lam[:, h:h + 1]).then_inc(cdone, 1)

            def exponentials(n, i, u):
                act.wait_ge(s_P, P_CR + 1 - EB + n * NT + i)
                act.wait_ge(s_Wm, W_CR + n * NT + i + 1)
                for j, (lo, hi) in enumerate(((0, SEG), (SEG, TW))):
                    if i or j:
                        acc = rs[:, u, i, 0:1] if j else rp[:, u, i:i + 1]
                        nc.scalar.activation(Tt[:, i % EB, lo:hi], Wm[:, i % EB, lo:hi], ACT.Exp, bias=mn[:, u, i, 0:1],
                                             scale=-1.0, accum_out=acc).then_inc(s_T, 1)
                for j, (c0, w) in enumerate(chunks[i]):
                    g = first_chunk[i] + j
                    act.wait_ge(s_mn, n * NCH + g + 1)
                    nc.scalar.activation(E[:, i % EB, c0:c0 + w], S[g % NS_B][:, 0:w], ACT.Exp,
                                         bias=mn[:, u, i, 1 + j:2 + j], scale=-1.0,
                                         accum_out=rs[:, u, i, 1 + j:2 + j]).then_inc(s_E, 1)
                act.wait_ge(s_top, n * NT + i + 1)
                k = 1 + len(chunks[i])
                nc.scalar.activation(f[:, u, i, 0:k], mn[:, u, i, 0:k], ACT.Exp, bias=top[:, u, i:i + 1],
                                     scale=-1.0).then_inc(s_f, 1)

            def keep_transposed(n, i):
                act.wait_ge(s_TT, n * NT + i + 1)
                act.wait_ge(s_O, O_CR + n * NT + i)
                if i:
                    nc.scalar.copy(TTs[0:SEG, 0:P], TT[0:SEG, 0:P])
                nc.scalar.copy(TTs[:, P:2 * P], TT[:, P:2 * P]).then_inc(s_TTs, 1)

            exponentials(0, 0, 0)
            exponentials(0, 1, 0)
            with act.Fori(0, B) as b:
                with act.Fori(0, H // 2) as hp:
                    for u in range(2):
                        n = b * H + hp * 2 + u
                        for i in range(NT):
                            if i + 2 < NT:
                                exponentials(n, i + 2, u)
                            else:
                                exponentials(n + 1, i + 2 - NT, 1 - u)
                            keep_transposed(n, i)
                        act.wait_ge(s_O, O_CR + n * NT + NT)
                        nc.scalar.copy(OT_s[:, :], OT[:, :]).then_inc(s_OTs, 1)
                        act.wait_ge(s_KV, KV_CR + n + 1)
                        nc.scalar.copy(kvr[:, :], misc[0:R, 0:KVW]).then_inc(s_kvr, 1)

        @block.vector
        def _(dve):
            dve.wait_ge(cin, 80)
            dve.wait_ge(made, 11)
            nc.vector.tensor_scalar(lam[:, :], lam_raw[:, :], float(SEG), float(np.log(2.0)), ALU.mult,
                                    ALU.min).then_inc(s_den, 1)
            nc.vector.tensor_scalar(gap[:, :], gap_i[:, :], 0.0, None, ALU.max).then_inc(s_den, 2)
            dve.wait_ge(s_den, 3)
            dve.wait_ge(cdone, 1)
            DEN0 = 3

            def minima(n, i, u):
                lo = 0 if i else SEG
                dve.wait_ge(s_W, n * NT + i + 1)
                wait_here(dve, s_T, T_CR + n * NTX + (first_t[i - 3] if i > 3 else first_t[NT + i - 3] - NTX), dve_passed)
                nc.vector.tensor_tensor_reduce(
                    out=Wm[:, i % EB, lo:TW], in0=S_W[:, lo:TW], in1=mask[:, lo:TW], scale=1.0,
                    scalar=3.0e38, op0=ALU.add, op1=ALU.min, accum_out=mn[:, u, i, 0:1]).then_inc(s_Wm, 1)
                for j, (c0, w) in enumerate(chunks[i]):
                    g = first_chunk[i] + j
                    dve.wait_ge(s_S, n * NCH + g + 1)
                    nc.vector.tensor_reduce(mn[:, u, i, 1 + j:2 + j], S[g % NS_B][:, 0:w], AX.X, ALU.min).then_inc(s_mn, 1)
                dve.wait_ge(s_Wm, W_CR + n * NT + i + 1)
                if i:
                    dve.wait_ge(s_mn, n * NCH + first_chunk[i + 1])
                k = 1 + len(chunks[i])
                nc.vector.tensor_reduce(top[:, u, i:i + 1], mn[:, u, i, 0:k], AX.X, ALU.min).then_inc(s_top, 1)

            def weights(n, i, u):
                k = 1 + len(chunks[i])
                at = (n * NT + i) * 2
                dve.wait_ge(s_f, n * NT + i + 1)
                nc.vector.tensor_tensor_reduce(out=fr[:, i, 0:k], in0=f[:, u, i, 0:k], in1=rs[:, u, i, 0:k], scale=1.0,
                                               scalar=0.0, op0=ALU.mult, op1=ALU.add,
                                               accum_out=tot[:, i:i + 1]).then_inc(s_step, 1)
                dve.wait_ge(s_step, at + 1)
                nc.vector.reciprocal(inv[:, i:i + 1], tot[:, i:i + 1]).then_inc(s_step, 1)
                dve.wait_ge(s_step, at + 2)
                if i == 0:
                    dve.wait_ge(s_small, n * 2 + 2)
                dve.wait_ge(s_P, P_CR - 1 + n * NT + i)
                nc.vector.scalar_tensor_tensor(
                    c2[:, i % 2, 0:k, PAD:PAD + 2], f[:, u, i, 0:k].unsqueeze(2).to_broadcast([P, k, 2]), inv[:, i:i + 1],
                    eid_h[:, u, :].unsqueeze(1).to_broadcast([P, k, 2]), ALU.mult, ALU.mult).then_inc(s_c2, 1)

            nc.vector.memset(pcs[:, :], 0.0).then_inc(s_pc, 1)
            minima(0, 0, 0)
            minima(0, 1, 0)
            weights(0, 0, 0)
            minima(0, 2, 0)
            with dve.Fori(0, B) as b:
                with dve.Fori(0, H // 2) as hp:
                    for u in range(2):
                        n = b * H + hp * 2 + u
                        for i in range(NT):
                            if i + 1 < NT:
                                weights(n, i + 1, u)
                            else:
                                weights(n + 1, 0, 1 - u)
                            if i + 3 < NT:
                                minima(n, i + 3, u)
                            else:
                                minima(n + 1, i + 3 - NT, 1 - u)
                        dve.wait_ge(s_P, P_CR + n * NT + NT)
                        nc.vector.tensor_copy(pcs_s[:, :], pcs[:, :]).then_inc(s_pc, 1)
                        dve.wait_ge(s_pc, PC_CR + n * 2 + 1)
                        nc.vector.memset(pcs[:, :], 0.0).then_inc(s_pc, 1)
                        nc.vector.tensor_tensor(tot_t[:, 1:NT], rs[:, u, 1:NT, 0], rp[:, u, 1:NT], ALU.add).then_inc(s_inv, 1)
                        nc.vector.tensor_copy(tot_t[:, 0:1], rs[:, u, 0, 0:1]).then_inc(s_inv, 1)
                        dve.wait_ge(s_inv, n * 3 + 2)
                        nc.vector.reciprocal(inv_t[:, :], tot_t[:, :]).then_inc(s_inv, 1)
                        dve.wait_ge(s_pT, n + 1)
                        nc.vector.tensor_copy(pcsT[:, :], misc[:, :]).then_inc(s_pTs, 1)
                        dve.wait_ge(s_inv, n * 3 + 3)
                        dve.wait_ge(s_OTT, n + 1)
                        dve.wait_ge(s_Y, Y_CR - 1 + n)
                        nc.vector.scalar_tensor_tensor(
                            Y_h[:, u, :, :], TT[:, :].rearrange("p (t e) -> p t e", t=NT)[:, :, 0:DH], tw[:, 0:1],
                            inv_t[:, :].unsqueeze(2).to_broadcast([P, NT, DH]), ALU.mult, ALU.mult).then_inc(s_Yh, 1)
                        dve.wait_ge(s_K2, K2_CR + n + 1)
                        nc.vector.tensor_scalar(den[:, :], misc[0:R, DH * DH:KVW], NOISE_EPS, None,
                                                ALU.add).then_inc(s_den, 1)
                        dve.wait_ge(s_den, n * 2 + 1 + DEN0)
                        nc.vector.reciprocal(rden[:, :], den[:, :]).then_inc(s_den, 1)
                        dve.wait_ge(s_den, n * 2 + 2 + DEN0)
                        dve.wait_ge(kv_out[u], OUT_CR + (b * (H // 2) + hp) * 16)
                        nc.vector.tensor_scalar(kvn[:, u, :], misc[0:R, 0:DH * DH], rden[:, 0:1], None,
                                                ALU.mult).then_inc(s_kvn, 1)

        @block.tensor
        def _(pe):
            pe.wait_ge(made, 11)

            def window(n, i, u):
                lo = 0 if i else SEG
                pe.wait_ge(s_Wm, W_CR + n * NT + i)
                nc.tensor.matmul(S_W[:, lo:TW], sq[:, u, i * P:(i + 1) * P], sk[:, u, i * P - SEG + lo:(i + 1) * P],
                                 start=True, stop=True).then_inc(s_W, 1)

            def scores(n, i, u, j):
                g, (c0, w) = first_chunk[i] + j, chunks[i][j]
                pe.wait_ge(s_E, E_CR + 1 - NS_B + n * NCH + g)
                nc.tensor.matmul(S[g % NS_B][:, 0:w], sq[:, u, i * P:(i + 1) * P], sk[:, u, c0:c0 + w], start=True,
                                 stop=True).then_inc(s_S, 1)

            def transposes(n, i):
                pe.wait_ge(s_T, T_CR + n * NTX + first_t[i + 1])
                if i:
                    pe.wait_ge(s_TTs, TTS_CR + n * NT + i)
                else:
                    pe.wait_ge(s_Yh, YH_CR + n)
                ins = nc.tensor.transpose(TT[:, P:2 * P], Tt[:, i % EB, SEG:TW], ident[:, :])
                if i:
                    ins = nc.tensor.transpose(TT[0:SEG, 0:P], Tt[:, i % EB, 0:SEG], ident[:, :])
                ins.then_inc(s_TT, 1)

            def pair(i, k):
                return c2[:, i % 2, k, PAD - 2 * i:PAD - 2 * i + R]

            def sums(n, i, j):
                if j < 0:
                    pe.wait_ge(s_c2, n * NT + i + 1)
                    if i == 0:
                        pe.wait_ge(s_pc, PC_CR + n * 2)
                    q, b0 = i // NCQ, i % NCQ * P
                    return nc.tensor.matmul(pcs[q * R:(q + 1) * R, b0:b0 + P], pair(i, 0), Tt[:, i % EB, SEG:TW],
                                            start=False, stop=False, skip_group_check=True)
                c0, w = chunks[i][j]
                return nc.tensor.matmul(pcs[j * R:(j + 1) * R, 0:w], pair(i, 1 + j), E[:, i % EB, c0:c0 + w], start=False,
                                        stop=True, skip_group_check=True)

            def values(n, i, u):
                pe.wait_ge(s_TTs, TTS_CR + n * NT + i + 1)
                if i == 0:
                    pe.wait_ge(s_OTs, OTS_CR + n)
                out = OT[i % 4 * R:i % 4 * R + R, i // 4 * P:(i // 4 + 1) * P]
                ins = nc.tensor.matmul(out, vh[:, u, i * DH:(i + 2) * DH], TTs[:, P:2 * P], start=True, stop=(i == 0))
                if i:
                    ins = nc.tensor.matmul(out, vs[:, u, i * DH:(i + 2) * DH], TTs[0:SEG, 0:P], start=False, stop=True)
                ins.then_inc(s_O, 1)

            pe.wait_ge(loaded[0], LOADS)
            window(0, 0, 0)
            window(0, 1, 0)
            scores(0, 1, 0, 0)
            window(0, 2, 0)
            scores(0, 2, 0, 0)
            with pe.Fori(0, B) as b:
                with pe.Fori(0, H // 2) as hp:
                    for u in range(2):
                        n = b * H + hp * 2 + u
                        for i in range(NT):
                            ahead = (n, i + 3, u) if i + 3 < NT else (n + 1, i + 3 - NT, 1 - u)
                            ai = ahead[1]
                            if ai == 0:
                                pe.wait_ge(loaded[1 - u], (b * (H // 2) + hp + u) * LOADS + LOADS)
                            window(*ahead)
                            if ai and chunks[ai]:
                                scores(*ahead, 0)
                            if i:
                                values(n, i - 1, u)
                            transposes(n, i)
                            ins = sums(n, i, -1)
                            for j in range(max(len(chunks[i]), len(chunks[ai]) - 1)):
                                if j < len(chunks[i]):
                                    ins = sums(n, i, j)
                                if j == len(chunks[i]) - 1 or (not chunks[i] and j == 0):
                                    ins.then_inc(s_P, 1)
                                if j + 1 < len(chunks[ai]):
                                    scores(*ahead, j + 1)
                            if not chunks[i] and len(chunks[ai]) <= 1:
                                ins.then_inc(s_P, 1)
                        values(n, NT - 1, u)
                        pe.wait_ge(s_pc, PC_CR + n * 2 + 1)
                        pe.wait_ge(s_kvn, KVN_CR + n)
                        for q in range(NCQ):
                            ins = nc.tensor.transpose(misc[:, q * P:(q + 1) * P], pcs_s[:, q * P:(q + 1) * P], ident[:, :])
                        ins.then_inc(s_pT, 1)
                        pe.wait_ge(s_OTs, OTS_CR + n + 1)
                        pe.wait_ge(s_TTs, TTS_CR + n * NT + NT)
                        for q in range(NCQ):
                            ins = nc.tensor.transpose(TT[:, q * P:(q + 1) * P], OT_s[:, q * P:(q + 1) * P], ident[:, :])
                        ins.then_inc(s_OTT, 1)
                        pe.wait_ge(s_pTs, n + 1)
                        pe.wait_ge(s_kvo, n + 1)
                        for t in range(NT):
                            col = t % NCQ * P + t // NCQ * R
                            ins = nc.tensor.matmul(misc[0:R, 0:KVW], pcsT[:, col:col + R], kvo[:, t, :],
                                                   start=(t == 0), stop=(t == NT - 1))
                        ins.then_inc(s_KV, 1)
                        pe.wait_ge(s_kvr, n + 1)
                        wait_here(pe, s_small, n * 2 + 2, pe_passed)
                        nc.tensor.matmul(misc[0:R, 0:KVW], decay_h[:, u, :], kvr[:, :], start=True,
                                         stop=True).then_inc(s_K2, 1)


def phase_merge(nc, x, q_full, y_dram, kv_dram, terrace_mix, wc, x_out):
    with ExitStack() as ctx:
        m = Mem(nc, ctx, "mg_")
        G = 4
        W = G * P
        NS = T // W
        ident = m.sb("ident", [P, P])
        wc_s = m.sb("wc", [P, KC, D])
        tmix, tw, keep = m.sb("tmix", [P, 1]), m.sb("tw", [P, 1]), m.sb("keep", [P, 1])
        SS = G * P // SEG
        state = m.sb("state", [P, 2, KC, SS, P])
        qT = m.sb("qT", [P, 2, KC, W])
        y_in, x_s = m.sb("y_in", [P, 2, G, D]), m.sb("x", [P, 2, G, D])
        y = m.sb("y", [P, G * D])
        yT = m.sb("yT", [P, KC, W])
        z = m.sb("z", [P, 2, G, D])
        lin, p_T, p_z = m.ps("lin", [P, G * D]), m.ps("T", [P, KC, W]), m.ps("p_z", [P, G * D])
        made, cin, cdone, zeroed = (m.sem(k) for k in ("made", "const_in", "const_done", "zeroed"))
        loaded = [m.sem(f"loaded{u}") for u in range(2)]
        stored = [m.sem(f"stored{u}") for u in range(2)]
        s_lin, s_y, s_T, s_yT, s_zmm, s_z = (m.sem(k) for k in ("lin", "y", "T", "yT", "zmm", "z"))
        LOADS = 16 * (3 + H)
        sp_passed, act_passed = m.sem("sp_passed"), m.sem("act_passed")
        Y_CR, Z_CR, OUT_CR = 1, 2, 1
        kv_v = kv_dram.rearrange("(b j h) r (d e) -> b h d j r e", b=B, j=2, d=DH)
        block = ctx.enter_context(nc.Block())

        @block.sync
        def _(sp):
            for u in range(2):
                sp.dma_start(tmix[u * SEG:(u + 1) * SEG, :], terrace_mix).then_inc(cin, 16)
            sp.dma_start(wc_s[:, :, :], wc).then_inc(cin, 16)
            for sem, credits in ((s_z, Z_CR), (s_y, Y_CR), (stored[0], OUT_CR), (stored[1], OUT_CR)):
                sp.sem_inc(sem, credits)
            sp.wait_ge(zeroed, 2)
            with sp.Fori(0, B) as b:
                with sp.Fori(0, NS // B // 2) as p:
                    for u in range(2):
                        n = b * (NS // B) + p * 2 + u
                        wait_here(sp, s_z, Z_CR - 1 + n, sp_passed)
                        for h in range(HH):
                            for j in range(KC):
                                sp.dma_start(state[h * DH:(h + 1) * DH, u, j, :, h * DH:(h + 1) * DH],
                                             kv_v[ds(b, 1), h, :, j, ds(p * (2 * SS) + u * SS, SS), :].rearrange(
                                                 "b d r e -> (b d) r e")).then_inc(loaded[u], 16)
                        sp.dma_start(qT[:, u, :, :], q_full[:, ds(n * W, W)].rearrange("(k p) t -> p k t", k=KC)
                                     ).then_inc(loaded[u], 16)
                        sp.dma_start(y_in[:, u, :, :], rows(y_dram, n * W, G)).then_inc(loaded[u], 16)
                        sp.dma_start(x_s[:, u, :, :], rows(x, n * W, G)).then_inc(loaded[u], 16)

        @block.gpsimd
        def _(pool):
            pool.memset(state[:, 0, :, :, :], 0.0).then_inc(zeroed, 1)
            make_identity(pool, ident, made)

        @block.scalar
        def _(act):
            act.wait_ge(cin, 48)
            nc.scalar.activation(tw[:, :], tmix[:, :], ACT.Sigmoid).then_inc(cdone, 1)
            with act.Fori(0, NS // 2) as q:
                for u in range(2):
                    n = q * 2 + u
                    for k in range(KC):
                        act.wait_ge(s_T, n * KC + k + 1)
                        nc.scalar.copy(yT[:, k, :], p_T[:, k, :]).then_inc(s_yT, 1)
                    wait_here(act, s_z, Z_CR + n + 1, act_passed)
                    act.dma_start(rows(x_out, n * W, G), z[:, u, :, :]).then_inc(stored[u], 16)
            for u in range(2):
                act.wait_ge(stored[u], OUT_CR + NS // 2 * 16)

        @block.vector
        def _(dve):
            nc.vector.memset(state[:, 1, :, :, :], 0.0).then_inc(zeroed, 1)
            dve.wait_ge(cdone, 1)
            nc.vector.tensor_scalar(keep[:, :], tw[:, :], -1.0, 1.0, ALU.mult, ALU.add).then_inc(cdone, 1)
            dve.wait_ge(cdone, 2)
            with dve.Fori(0, NS // 2) as q:
                for u in range(2):
                    n = q * 2 + u
                    dve.wait_ge(s_lin, n + 1)
                    nc.vector.scalar_tensor_tensor(y[:, :], lin[:, :], keep[:, 0:1],
                                                   y_in[:, u, :, :].rearrange("p t d -> p (t d)"), ALU.mult,
                                                   ALU.add).then_inc(s_y, 1)
                    dve.wait_ge(s_zmm, n + 1)
                    dve.wait_ge(stored[u], OUT_CR + q * 16)
                    nc.vector.tensor_tensor(z[:, u, :, :].rearrange("p t d -> p (t d)"), p_z[:, :],
                                            x_s[:, u, :, :].rearrange("p t d -> p (t d)"), ALU.add).then_inc(s_z, 1)

        @block.tensor
        def _(pe):
            pe.wait_ge(made, 2)
            pe.wait_ge(cin, 48)
            with pe.Fori(0, NS // 2) as q:
                for u in range(2):
                    n = q * 2 + u
                    pe.wait_ge(loaded[u], q * LOADS + LOADS)
                    pe.wait_ge(s_y, Y_CR + n)
                    for t in range(G):
                        for s in range(2):
                            for j in range(KC):
                                ins = nc.tensor.matmul(lin[s * SEG:(s + 1) * SEG, t * D + j * P:t * D + (j + 1) * P],
                                                       qT[:, u, j, t * P + s * SEG:t * P + (s + 1) * SEG],
                                                       state[:, u, j, 2 * t + s, :], start=True, stop=True)
                    ins.then_inc(s_lin, 1)
                    pe.wait_ge(s_y, Y_CR + n + 1)
                    for k in range(KC):
                        for t in range(G):
                            ins = nc.tensor.transpose(p_T[:, k, t * P:(t + 1) * P],
                                                      y[:, t * D + k * P:t * D + (k + 1) * P], ident[:, :])
                        ins.then_inc(s_T, 1)
                    pe.wait_ge(s_yT, n * KC + KC)
                    pe.wait_ge(s_z, Z_CR + n)
                    for t in range(G):
                        for k in range(KC):
                            ins = nc.tensor.matmul(p_z[:, t * D:(t + 1) * D], yT[:, k, t * P:(t + 1) * P],
                                                   wc_s[:, k, :], start=(k == 0), stop=(k == KC - 1))
                    ins.then_inc(s_zmm, 1)

NE, MH, TOPK = 16, 128, 2
ROUTE_SCALE = 2.5
MIN_SUM = 1e-20


def phase_moe(nc, x, gate, w_gate, w_up, w_down, x_out, tag):
    with ExitStack() as ctx:
        m = Mem(nc, ctx, tag)
        G = 4
        W = G * P
        NS = T // W
        ident = m.sb("ident", [P, P])
        iota_e, iota_i = m.sb("iota_e", [P, NE]), m.sb("iota_i", [P, NE], mybir.dt.int32)
        eps = m.sb("eps", [P, 1])
        gw = m.sb("gw", [P, KC, NE])
        wg, wu = m.sb("wg", [P, NE + 1, KC, MH]), m.sb("wu", [P, NE + 1, KC, MH])
        wd = m.sb("wd", [P, NE + 1, D])
        acc = m.sb("acc", [P, 2, G, D])
        stats, mv = m.sb("stats", [P, G, 6]), m.sb("mv", [P, G, 2])
        std, rstd = m.sb("std", [P, G]), m.sb("rstd", [P, G])
        hn = m.sb("hn", [P, G, D])
        hT = m.sb("hT", [P, 2, KC, W])
        ex, ex1, sc = m.sb("ex", [P, G, NE]), m.sb("ex1", [P, G, NE]), m.sb("sc", [P, G, NE])
        top, idx = m.sb("top", [P, G, 8]), m.sb("idx", [P, G, 8], U32)
        idx_f = m.sb("idx_f", [P, G, TOPK])
        tsum, tinv, tw = m.sb("tsum", [P, G]), m.sb("tinv", [P, G]), m.sb("tw", [P, G, TOPK])
        pick = m.sb("pick", [P, G, TOPK, NE])
        route = m.sb("route", [P, 2, G, NE])
        act_g = m.sb("act_g", [P, 2, W])
        hid = m.sb("hid", [P, 2, W])
        p_T = m.ps("T", [P, KC, W])
        p_g = [m.ps(f"g{j}", [P, W]) for j in range(2)]
        p_u = [m.ps(f"u{j}", [P, W]) for j in range(2)]
        p_d = [m.ps(f"d{j}", [P, G // 2, D]) for j in range(2)]
        made, gate_in, gu_in, down_in = (m.sem(k) for k in ("made", "gate_in", "gu_in", "down_in"))
        x_in, stored = [m.sem(f"x_in{u}") for u in range(2)], [m.sem(f"stored{u}") for u in range(2)]
        s_stat, s_var, s_std, s_rstd, s_hn = (m.sem(k) for k in ("stat", "var", "std", "rstd", "hn"))
        s_T, s_hT, s_log, s_ex, s_chain = (m.sem(k) for k in ("T", "hT", "log", "ex", "chain"))
        s_top, s_pick, s_route = m.sem("top"), m.sem("pick"), m.sem("route")
        s_gu, s_act, s_hid, s_d, s_acc = (m.sem(k) for k in ("gu", "silu", "hid", "down", "acc"))
        sp_passed, dve_passed = m.sem("sp_passed"), m.sem("dve_passed")
        HID_CR, D_CR, OUT_CR = 2, 2, 1
        CH = 6
        N1 = NE + 1
        block = ctx.enter_context(nc.Block())

        def steps(eng, body):
            with eng.Fori(0, NS // 2 - 1) as q:
                body(q * 2, 0, q, False)
                body(q * 2 + 1, 1, q, False)
            body(NS - 2, 0, NS // 2 - 1, False)
            body(NS - 1, 1, NS // 2 - 1, True)

        @block.sync
        def _(sp):
            sp.dma_start(gw[:, :, :], gate).then_inc(gate_in, 16)
            sp.dma_start(acc[:, 0, :, :], rows(x, 0, G)).then_inc(x_in[0], 16)
            sp.dma_start(wg[:, :, :, :], w_gate).then_inc(gu_in, 16)
            sp.dma_start(wu[:, :, :, :], w_up).then_inc(gu_in, 16)
            sp.dma_start(wd[:, :, :], w_down).then_inc(down_in, 16)
            sp.sem_inc(s_hid, HID_CR)
            sp.sem_inc(s_acc, D_CR)
            sp.sem_inc(stored[0], OUT_CR)
            sp.sem_inc(stored[1], OUT_CR)

            def body(n, u, q, last):
                if not last:
                    wait_here(sp, stored[1 - u], OUT_CR + (q + u) * 16, sp_passed)
                    sp.dma_start(acc[:, 1 - u, :, :], rows(x, n * W + W, G)).then_inc(x_in[1 - u], 16)
                wait_here(sp, s_acc, D_CR + n * (2 * N1) + 2 * N1, sp_passed)
                sp.dma_start(rows(x_out, n * W, G), acc[:, u, :, :]).then_inc(stored[u], 16)

            steps(sp, body)
            for u in range(2):
                sp.wait_ge(stored[u], OUT_CR + NS // 2 * 16)

        @block.gpsimd
        def _(pool):
            make_identity(pool, ident, made)
            pool.memset(eps[:, :], LN_EPS).then_inc(made, 1)
            pool.iota(iota_i[:, :], pattern=[[1, NE]], base=0, channel_multiplier=0).then_inc(made, 1)
            pool.wait_ge(made, 4)
            pool.tensor_copy(iota_e[:, :], iota_i[:, :]).then_inc(made, 1)

        @block.scalar
        def _(act):
            act.wait_ge(made, 5)

            def front(n, u):
                act.wait_ge(s_var, n * G + G)
                nc.scalar.activation(std[:, :], mv[:, :, 1], ACT.Sqrt, bias=eps[:, 0:1]).then_inc(s_std, 1)
                for k in range(KC):
                    act.wait_ge(s_T, n * KC + k + 1)
                    nc.scalar.copy(hT[:, u, k, :], p_T[:, k, :]).then_inc(s_hT, 1)

            def scores(n):
                act.wait_ge(s_log, n + 1)
                nc.scalar.activation(ex[:, :, :], p_T[:, 0, 0:G * NE].rearrange("p (g e) -> p g e", g=G), ACT.Exp,
                                     scale=-1.0).then_inc(s_ex, 1)

            def body(n, u, q, last):
                for e in range(N1):
                    k = n * N1 + e
                    act.wait_ge(s_gu, k + 1)
                    act.wait_ge(s_hid, HID_CR - 1 + k)
                    nc.scalar.activation(act_g[:, (u * N1 + e) % 2, :], p_g[(u * N1 + e) % 2][:, :],
                                         ACT.Silu).then_inc(s_act, 1)
                    if e == 9 and not last:
                        front(n + 1, 1 - u)
                    if e == 12 and not last:
                        scores(n + 1)

            front(0, 0)
            scores(0)
            steps(act, body)

        @block.vector
        def _(dve):
            dve.wait_ge(made, 5)

            def front(n, u, q):
                dve.wait_ge(x_in[u], q * 16 + 16)
                for t in range(G):
                    nc.vector.bn_stats(stats[:, t, :], acc[:, u, t, :]).then_inc(s_stat, 1)
                wait_here(dve, s_stat, n * G + G, dve_passed)
                for t in range(G):
                    nc.vector.bn_aggr(mv[:, t, :], stats[:, t, :]).then_inc(s_var, 1)
                dve.wait_ge(s_std, n + 1)
                nc.vector.reciprocal(rstd[:, :], std[:, :]).then_inc(s_rstd, 1)
                dve.wait_ge(s_rstd, n + 1)
                for t in range(G):
                    nc.vector.tensor_scalar(hn[:, t, :], acc[:, u, t, :], mv[:, t, 0:1], rstd[:, t:t + 1],
                                            ALU.subtract, ALU.mult).then_inc(s_hn, 1)

            def routing(n, u):
                dve.wait_ge(s_ex, n + 1)
                nc.vector.tensor_scalar(ex1[:, :, :], ex[:, :, :], 1.0, None, ALU.add).then_inc(s_chain, 1)
                dve.wait_ge(s_chain, n * CH + 1)
                nc.vector.reciprocal(sc[:, :, :], ex1[:, :, :]).then_inc(s_chain, 1)
                wait_here(dve, s_chain, n * CH + 2, dve_passed)
                for t in range(G):
                    nc.vector.max(top[:, t, :], sc[:, t, :]).then_inc(s_top, 1)
                wait_here(dve, s_top, n * (2 * G) + G, dve_passed)
                for t in range(G):
                    nc.vector.max_index(idx[:, t, :], top[:, t, :], sc[:, t, :]).then_inc(s_top, 1)
                nc.vector.tensor_tensor(tsum[:, :], top[:, :, 0], top[:, :, 1], ALU.add).then_inc(s_chain, 1)
                dve.wait_ge(s_chain, n * CH + 3)
                nc.vector.tensor_scalar(tsum[:, :], tsum[:, :], MIN_SUM, None, ALU.add).then_inc(s_chain, 1)
                dve.wait_ge(s_chain, n * CH + 4)
                nc.vector.reciprocal(tinv[:, :], tsum[:, :]).then_inc(s_chain, 1)
                dve.wait_ge(s_top, n * (2 * G) + 2 * G)
                nc.vector.tensor_copy(idx_f[:, :, :], idx[:, :, 0:TOPK]).then_inc(s_chain, 1)
                dve.wait_ge(s_chain, n * CH + 6)
                for t in range(G):
                    nc.vector.tensor_scalar(tw[:, t, :], top[:, t, 0:TOPK], tinv[:, t:t + 1], ROUTE_SCALE, ALU.mult,
                                            ALU.mult).then_inc(s_pick, 1)
                dve.wait_ge(s_pick, n * (3 * G) + G)
                for t in range(G):
                    for j in range(TOPK):
                        nc.vector.tensor_scalar(pick[:, t, j, :], iota_e[:, :], idx_f[:, t, j:j + 1], tw[:, t, j:j + 1],
                                                ALU.is_equal, ALU.mult).then_inc(s_pick, 1)
                dve.wait_ge(s_pick, n * (3 * G) + 3 * G)
                nc.vector.tensor_tensor(route[:, u, :, :], pick[:, :, 0, :], pick[:, :, 1, :], ALU.add).then_inc(s_route, 1)

            def hidden(n, u, e):
                k = n * N1 + e
                j = (u * N1 + e) % 2
                dve.wait_ge(s_act, k + 1)
                nc.vector.tensor_tensor(hid[:, j, :], act_g[:, j, :], p_u[j][:, :], ALU.mult).then_inc(s_hid, 1)

            def add(n, u, e):
                k = n * N1 + e
                for half in range(2):
                    dve.wait_ge(s_d, k * 2 + half + 1)
                    for t in range(half * G // 2, (half + 1) * G // 2):
                        o = p_d[half][:, t % (G // 2), :]
                        if e < NE:
                            ins = nc.vector.scalar_tensor_tensor(acc[:, u, t, :], o, route[:, u, t, e:e + 1],
                                                                 acc[:, u, t, :], ALU.mult, ALU.add)
                        else:
                            ins = nc.vector.tensor_tensor(acc[:, u, t, :], o, acc[:, u, t, :], ALU.add)
                    ins.then_inc(s_acc, 1)

            def body(n, u, q, last):
                for e in range(N1):
                    hidden(n, u, e)
                    if e:
                        dve.wait_ge(s_acc, D_CR + (n * N1 + e - 1) * 2)
                        add(n, u, e - 1)
                    if e == 9 and not last:
                        front(n + 1, 1 - u, q + u)
                    if e == 12 and not last:
                        routing(n + 1, 1 - u)
                add(n, u, NE)

            front(0, 0, 0)
            routing(0, 0)
            dve.wait_ge(s_route, 1)
            steps(dve, body)

        @block.tensor
        def _(pe):
            pe.wait_ge(made, 2)

            def front(n, u):
                pe.wait_ge(s_hn, n * G + G)
                for k in range(KC):
                    for t in range(G):
                        ins = nc.tensor.transpose(p_T[:, k, t * P:(t + 1) * P], hn[:, t, k * P:(k + 1) * P], ident[:, :])
                    ins.then_inc(s_T, 1)

            def logits(n, u):
                pe.wait_ge(s_hT, n * KC + KC)
                for t in range(G):
                    for k in range(KC):
                        ins = nc.tensor.matmul(p_T[:, 0, t * NE:(t + 1) * NE], hT[:, u, k, t * P:(t + 1) * P],
                                               gw[:, k, :], start=(k == 0), stop=(k == KC - 1))
                ins.then_inc(s_log, 1)

            def gate_up(n, u, e):
                k = n * N1 + e
                j = (u * N1 + e) % 2
                pe.wait_ge(s_hid, HID_CR - 1 + k)
                for w, p in ((wg, p_g[j]), (wu, p_u[j])):
                    for c in range(KC):
                        ins = nc.tensor.matmul(p[:, :], w[:, e, c, :], hT[:, u, c, :], start=(c == 0), stop=(c == KC - 1))
                ins.then_inc(s_gu, 1)

            def down(n, u, e):
                k = n * N1 + e
                j = (u * N1 + e) % 2
                pe.wait_ge(s_hid, HID_CR + k + 1)
                for half in range(2):
                    pe.wait_ge(s_acc, D_CR - 1 + k * 2 + half)
                    for t in range(half * G // 2, (half + 1) * G // 2):
                        ins = nc.tensor.matmul(p_d[half][:, t % (G // 2), :], hid[:, j, t * P:(t + 1) * P],
                                               wd[:, e, :], start=True, stop=True)
                    ins.then_inc(s_d, 1)

            def body(n, u, q, last):
                for e in range(N1):
                    if e + 1 < N1:
                        gate_up(n, u, e + 1)
                    elif not last:
                        gate_up(n + 1, 1 - u, 0)
                    down(n, u, e)
                    if e == 9 and not last:
                        front(n + 1, 1 - u)
                    if e == 11 and not last:
                        logits(n + 1, 1 - u)

            front(0, 0)
            pe.wait_ge(gate_in, 16)
            logits(0, 0)
            pe.wait_ge(gu_in, 32)
            gate_up(0, 0, 0)
            pe.wait_ge(down_in, 16)
            steps(pe, body)

NM, MS = 4, 5
GH, GK, GV = 4, 32, 64
LOW = 16
CAP = L // 2
GATE_NORM = 16.0
NTT = T // P


def phase_route(nc, x, w_gate, hT_dram, kw_dram):
    with ExitStack() as ctx:
        m = Mem(nc, ctx, "rt_")
        G = 4
        W = G * P
        NS = T // W
        ident, tri, ones = m.sb("ident", [P, P]), m.sb("tri", [P, P]), m.sb("ones", [P, P])
        iota_m, iota_i = m.sb("iota_m", [P, NM]), m.sb("iota_i", [P, NM], mybir.dt.int32)
        eps = m.sb("eps", [P, 1])
        gw = m.sb("gw", [P, KC, NM])
        x_s = m.sb("x", [P, G, D])
        stats, mv = m.sb("stats", [P, G, 6]), m.sb("mv", [P, G, 2])
        std, rstd = m.sb("std", [P, G]), m.sb("rstd", [P, G])
        hn, hT = m.sb("hn", [P, G, D]), m.sb("hT", [P, KC, W])
        mx, dist = m.sb("mx", [P, G]), m.sb("dist", [P, G, NM])
        ex, esum, einv = m.sb("ex", [P, G, NM]), m.sb("esum", [P, G]), m.sb("einv", [P, G])
        prob = m.sb("prob", [P, G, 8])
        top, idx, idx_f = m.sb("top", [P, G, 8]), m.sb("idx", [P, G, 8], U32), m.sb("idx_f", [P, G, TOPK])
        tsum, tinv = m.sb("tsum", [P, G]), m.sb("tinv", [P, G])
        pick = m.sb("pick", [P, G, TOPK, NM])
        wts = m.sb("wts", [P, G, TOPK])
        pw = m.sb("pw", [P, G, TOPK, NM])
        sel, wt = m.sb("sel", [P, NTT * NM]), m.sb("wt", [P, NTT * NM])
        later = m.sb("later", [P, B, NT, NM])
        kw = m.sb("kw", [P, NTT, 2, NM])
        zeros = m.sb("zeros", [P, 2 * P])
        p_T = m.ps("T", [P, KC, W])
        p_l = m.ps("l", [P, G, NM])
        p_c = m.ps("c", [P, NTT * NM])
        made, w_in, x_in, stored, kw_out = (m.sem(k) for k in ("made", "w_in", "x_in", "stored", "kw_out"))
        s_stat, s_var, s_std, s_rstd, s_hn = (m.sem(k) for k in ("stat", "var", "std", "rstd", "hn"))
        s_T, s_hT, s_log, s_ex, s_chain, s_top, s_pick = (m.sem(k) for k in ("T", "hT", "log", "ex", "chain", "top", "pick"))
        s_sel, s_dist, s_later, s_cnt, s_kw = m.sem("sel"), m.sem("dist"), m.sem("later"), m.sem("cnt"), m.sem("kw")
        sp_passed, dve_passed = m.sem("sp_passed"), m.sem("dve_passed")
        CH = 7
        HN_CR, OUT_CR = 1, 1
        block = ctx.enter_context(nc.Block())

        @block.sync
        def _(sp):
            sp.dma_start(gw[:, :, :], w_gate).then_inc(w_in, 16)
            sp.sem_inc(s_hn, HN_CR)
            sp.sem_inc(stored, OUT_CR)
            sp.wait_ge(made, 11)
            for k in range(KC):
                sp.dma_start(hT_dram[k, :, T:T + 2 * P], zeros[:, :]).then_inc(kw_out, 16)
            sp.dma_start(kw_dram[NTT:NTT + 2, :, :].rearrange("t p n -> p t n"),
                         zeros[:, 0:4 * NM].rearrange("p (t n) -> p t n", t=2)).then_inc(kw_out, 16)
            with sp.Fori(0, NS) as n:
                wait_here(sp, s_hn, HN_CR + n * G, sp_passed)
                sp.dma_start(x_s[:, :, :], rows(x, n * W, G)).then_inc(x_in, 16)
                wait_here(sp, s_hT, n * KC + KC, sp_passed)
                sp.dma_start(hT_dram[:, :, ds(n * W, W)].rearrange("k p t -> p k t"), hT[:, :, :]).then_inc(stored, 16)
            sp.wait_ge(s_kw, 2)
            sp.dma_start(kw_dram[0:NTT, :, :].rearrange("t p n -> p t n"), kw[:, :, :, :].rearrange("p t a m -> p t (a m)")
                         ).then_inc(kw_out, 16)
            sp.wait_ge(stored, OUT_CR + NS * 16)
            sp.wait_ge(kw_out, 16 * (KC + 2))

        @block.gpsimd
        def _(pool):
            make_identity(pool, ident, made)
            pool.memset(eps[:, :], LN_EPS).then_inc(made, 1)
            pool.memset(ones[:, :], 1.0).then_inc(made, 1)
            pool.memset(tri[:, :], 1.0).then_inc(made, 1)
            pool.memset(prob[:, :, :], -1.0).then_inc(made, 1)
            pool.memset(later[:, :, :, :], 0.0).then_inc(made, 1)
            pool.iota(iota_i[:, :], pattern=[[1, NM]], base=0, channel_multiplier=0).then_inc(made, 1)
            pool.wait_ge(made, 8)
            pool.tensor_copy(iota_m[:, :], iota_i[:, :]).then_inc(made, 1)
            pool.affine_select(out=tri[:, :], in_=tri[:, :], compare_op=ALU.is_ge, fill=0.0, base=0,
                               pattern=[[-1, P]], channel_multiplier=1).then_inc(made, 1)
            pool.memset(zeros[:, :], 0.0).then_inc(made, 1)

        @block.scalar
        def _(act):
            act.wait_ge(made, 10)
            with act.Fori(0, NS) as n:
                act.wait_ge(s_var, n * G + G)
                nc.scalar.activation(std[:, :], mv[:, :, 1], ACT.Sqrt, bias=eps[:, 0:1]).then_inc(s_std, 1)
                act.wait_ge(stored, OUT_CR + n * 16)
                for k in range(KC):
                    act.wait_ge(s_T, n * KC + k + 1)
                    nc.scalar.copy(hT[:, k, :], p_T[:, k, :]).then_inc(s_hT, 1)
                act.wait_ge(s_dist, n + 1)
                nc.scalar.activation(ex[:, :, :], dist[:, :, :], ACT.Exp).then_inc(s_ex, 1)

        @block.vector
        def _(dve):
            dve.wait_ge(made, 10)
            with dve.Fori(0, NS) as n:
                dve.wait_ge(x_in, n * 16 + 16)
                for t in range(G):
                    nc.vector.bn_stats(stats[:, t, :], x_s[:, t, :]).then_inc(s_stat, 1)
                wait_here(dve, s_stat, n * G + G, dve_passed)
                for t in range(G):
                    nc.vector.bn_aggr(mv[:, t, :], stats[:, t, :]).then_inc(s_var, 1)
                dve.wait_ge(s_std, n + 1)
                nc.vector.reciprocal(rstd[:, :], std[:, :]).then_inc(s_rstd, 1)
                dve.wait_ge(s_rstd, n + 1)
                for t in range(G):
                    nc.vector.tensor_scalar(hn[:, t, :], x_s[:, t, :], mv[:, t, 0:1], rstd[:, t:t + 1],
                                            ALU.subtract, ALU.mult).then_inc(s_hn, 1)
                dve.wait_ge(s_log, n + 1)
                nc.vector.tensor_reduce(mx[:, :], p_l[:, :, :], AX.X, ALU.max).then_inc(s_chain, 1)
                dve.wait_ge(s_chain, n * CH + 1)
                nc.vector.tensor_tensor(dist[:, :, :], p_l[:, :, :], mx[:, :].unsqueeze(2).to_broadcast([P, G, NM]),
                                        ALU.subtract).then_inc(s_dist, 1)
                dve.wait_ge(s_ex, n + 1)
                nc.vector.tensor_reduce(esum[:, :], ex[:, :, :], AX.X, ALU.add).then_inc(s_chain, 1)
                dve.wait_ge(s_chain, n * CH + 2)
                nc.vector.reciprocal(einv[:, :], esum[:, :]).then_inc(s_chain, 1)
                dve.wait_ge(s_chain, n * CH + 3)
                nc.vector.tensor_tensor(prob[:, :, 0:NM], ex[:, :, :], einv[:, :].unsqueeze(2).to_broadcast([P, G, NM]),
                                        ALU.mult).then_inc(s_chain, 1)
                wait_here(dve, s_chain, n * CH + 4, dve_passed)
                for t in range(G):
                    nc.vector.max(top[:, t, :], prob[:, t, :]).then_inc(s_top, 1)
                wait_here(dve, s_top, n * (2 * G) + G, dve_passed)
                for t in range(G):
                    nc.vector.max_index(idx[:, t, :], top[:, t, :], prob[:, t, :]).then_inc(s_top, 1)
                nc.vector.tensor_tensor(tsum[:, :], top[:, :, 0], top[:, :, 1], ALU.add).then_inc(s_chain, 1)
                dve.wait_ge(s_chain, n * CH + 5)
                nc.vector.reciprocal(tinv[:, :], tsum[:, :]).then_inc(s_chain, 1)
                dve.wait_ge(s_top, n * (2 * G) + 2 * G)
                nc.vector.tensor_copy(idx_f[:, :, :], idx[:, :, 0:TOPK]).then_inc(s_chain, 1)
                dve.wait_ge(s_chain, n * CH + 7)
                nc.vector.tensor_tensor(wts[:, :, :], top[:, :, 0:TOPK], tinv[:, :].unsqueeze(2).to_broadcast([P, G, TOPK]),
                                        ALU.mult).then_inc(s_pick, 1)
                for t in range(G):
                    for j in range(TOPK):
                        nc.vector.tensor_scalar(pick[:, t, j, :], iota_m[:, :], idx_f[:, t, j:j + 1], None,
                                                ALU.is_equal).then_inc(s_pick, 1)
                PK = 3 + G * TOPK
                dve.wait_ge(s_pick, n * PK + 1 + G * TOPK)
                nc.vector.tensor_tensor(pw[:, :, :, :].rearrange("p g j m -> p (g j) m"),
                                        pick[:, :, :, :].rearrange("p g j m -> p (g j) m"),
                                        wts[:, :, :].rearrange("p g j -> p (g j)").unsqueeze(2).to_broadcast([P, G * TOPK, NM]),
                                        ALU.mult).then_inc(s_pick, 1)
                nc.vector.tensor_tensor(sel[:, ds(n * (G * NM), G * NM)].rearrange("p (g m) -> p g m", g=G),
                                        pick[:, :, 0, :], pick[:, :, 1, :], ALU.add).then_inc(s_sel, 1)
                dve.wait_ge(s_pick, n * PK + 2 + G * TOPK)
                nc.vector.tensor_tensor(wt[:, ds(n * (G * NM), G * NM)].rearrange("p (g m) -> p g m", g=G),
                                        pw[:, :, 0, :], pw[:, :, 1, :], ALU.add).then_inc(s_pick, 1)
            dve.wait_ge(s_pick, NS * (3 + G * TOPK))
            dve.wait_ge(s_sel, NS)
            sel4 = sel[:, :].rearrange("p (b i m) -> p b i m", b=B, m=NM)
            for i in range(NT - 2, -1, -1):
                if i < NT - 2:
                    dve.wait_ge(s_later, NT - 2 - i)
                nc.vector.tensor_tensor(later[:, :, i, :], later[:, :, i + 1, :], sel4[:, :, i + 1, :],
                                        ALU.add).then_inc(s_later, 1)
            dve.wait_ge(s_cnt, 1)
            nc.vector.scalar_tensor_tensor(kw[:, :, 0, :], p_c[:, :].rearrange("p (t m) -> p t m", m=NM), float(CAP),
                                           sel[:, :].rearrange("p (t m) -> p t m", m=NM), ALU.is_le,
                                           ALU.mult).then_inc(s_kw, 1)
            dve.wait_ge(s_kw, 1)
            nc.vector.tensor_tensor(kw[:, :, 1, :], kw[:, :, 0, :], wt[:, :].rearrange("p (t m) -> p t m", m=NM),
                                    ALU.mult).then_inc(s_kw, 1)

        @block.tensor
        def _(pe):
            pe.wait_ge(made, 10)
            pe.wait_ge(w_in, 16)
            with pe.Fori(0, NS) as n:
                pe.wait_ge(s_hn, HN_CR + n * G + G)
                for k in range(KC):
                    for t in range(G):
                        ins = nc.tensor.transpose(p_T[:, k, t * P:(t + 1) * P], hn[:, t, k * P:(k + 1) * P], ident[:, :])
                    ins.then_inc(s_T, 1)
                pe.wait_ge(s_hT, n * KC + KC)
                for t in range(G):
                    for k in range(KC):
                        ins = nc.tensor.matmul(p_l[:, t, :], hT[:, k, t * P:(t + 1) * P], gw[:, k, :],
                                               start=(k == 0), stop=(k == KC - 1))
                ins.then_inc(s_log, 1)
            pe.wait_ge(s_later, NT - 1)
            nc.tensor.matmul(p_c[:, :], tri[:, :], sel[:, :], start=True, stop=False)
            nc.tensor.matmul(p_c[:, :], ones[:, :], later[:, :, :, :].rearrange("p b i m -> p (b i m)"),
                             start=False, stop=True).then_inc(s_cnt, 1)


def phase_gla(nc, hT_dram, kw_dram, w_q, w_k, w_v, w_gk1, w_gk2, b_gk, o_dram):
    with ExitStack() as ctx:
        m = Mem(nc, ctx, "gl_")
        HALVES = (64, 32, 16, 8, 4, 2)
        NL = len(HALVES) + 1
        DIRECT = 3
        MP = MS * P
        HKD = GH * GK
        assert HKD == P and GH * GV == D
        FLOOR = -80.0
        ident = m.sb("ident", [P, P])
        BK = 32
        masks = m.sb("masks", [P, NL - DIRECT, P])
        masks_b = m.sb("masks_b", [P, NL - DIRECT, BK])
        restart = m.sb("restart", [P, MS, P])
        wq, wk = m.sb("wq", [P, KC, P]), m.sb("wk", [P, MS, KC, P])
        wv = m.sb("wv", [P, MS, KC, D])
        w1, w2 = m.sb("w1", [P, KC, MS, 32]), m.sb("w2", [P, NM, P])
        w2s = m.sb("w2s", [32, P])
        bg = m.sb("bg", [P, MS])
        hT = m.sb("hT", [P, 2, KC, P])
        kw = m.sb("kw", [P, 2, 2 * NM])
        keep_m = m.sb("keep_m", [P, NM, P], BF16)
        ones = m.sb("ones", [P, P], BF16)
        qS, kS = m.sb("qS", [P, P]), m.sb("kS", [P, MP])
        low, low_s = m.sb("low", [P, P]), m.sb("low_s", [32, P])
        zb, az, ln = m.sb("zb", [P, MP]), m.sb("az", [P, MP]), m.sb("ln", [P, MP])
        zn = m.sb("zn", [P, MP])
        g, Gs = m.sb("g", [P, MP]), m.sb("Gs", [P, MP])
        dist = m.sb("dist", [P, NL, MP])
        gc = m.sb("gc", [P, MP // 2])
        ex = m.sb("ex", [P, NL, MP])
        exG, exE = m.sb("exG", [P, MP]), m.sb("exE", [P, MP])
        qt, kt = m.sb("qt", [P, 2, NL, MP]), m.sb("kt", [P, 2, NL, MP])
        q0, kend = m.sb("q0", [P, 2, MP]), m.sb("kend", [P, 2, MP])
        dend = m.sb("dend", [P, 2, MS])
        V = m.sb("V", [P, 2, MS, D])
        A = m.sb("A", [P, 2, GH * P])
        small = m.sb("small", [P, GH * BK])
        kE = m.sb("kE", [P, P])
        state = m.sb("state", [P, MS, D])
        acc = m.sb("acc", [P, 2, D])
        pd = m.ps("pd", [P, GH * P])
        pl = [m.ps(f"pl{j}", [P, GH * P]) for j in range(2)]
        po, pu = m.ps("po", [P, D]), m.ps("pu", [P, 512])
        f = [m.ps(f"f{j}", [P, 512]) for j in range(3)]
        made, w_in = m.sem("made"), m.sem("w_in")
        ld = [m.sem(f"ld{u}") for u in range(2)]
        stored = [m.sem(f"stored{u}") for u in range(2)]
        s_kM, s_F1, s_F1e, s_Z, s_KB, s_Ze, s_gate = (m.sem(k) for k in ("kM", "F1", "F1e", "Z", "KB", "Ze", "gate"))
        s_chain, s_g, s_D, s_V, s_Ve, s_ex, s_mul = (m.sem(k) for k in ("chain", "g", "D", "V", "Ve", "ex", "mul"))
        s_dir, s_A, s_Ad, s_T, s_kE, s_U = (m.sem(k) for k in ("dir", "A", "Ad", "T", "kE", "U"))
        s_ends = m.sem("ends")
        s_lv, s_cp, s_mask = m.sem("lv"), m.sem("cp"), m.sem("mask")
        s_o, s_out, s_S, s_reset = (m.sem(k) for k in ("o", "out", "S", "reset"))
        sp_passed, dve_passed, pe_passed, act_passed, pool_passed = (
            m.sem(k) for k in ("sp_passed", "dve_passed", "pe_passed", "act_passed", "pool_passed"))
        MUL_CR, VE_CR, A_CR, CP_CR, OUT_CR, S_CR, ST_CR, O_CR, DIR_CR, LV_CR, AD_CR, ENDS_CR = 1, 3, 1, 8, 1, MS, 1, 2, 1, 1, 1, 1
        NX = 2 * (NL - 1) + 2 + 2
        NMUL = 2 * (NL - 1) + 4
        NLV = NL - DIRECT
        block = ctx.enter_context(nc.Block())

        def tiles(eng, body, before=None):
            with eng.Fori(0, B) as b:
                if before is not None:
                    before(b)
                with eng.Fori(0, NT // 2) as p:
                    for u in range(2):
                        body(b * NT + p * 2 + u, u, b * (NT // 2) + p)

        @block.sync
        def _(sp):
            for dst, src in ((wq[:, :, :], w_q), (wk[:, :, :, :], w_k), (wv[:, :, :, :], w_v), (bg[:, :], b_gk)):
                sp.dma_start(dst, src).then_inc(w_in, 16)
            sp.wait_ge(made, 6)
            sp.dma_start(w1[:, :, :, 0:LOW], w_gk1).then_inc(w_in, 16)
            for j in range(NM):
                sp.dma_start(w2[j * 32:j * 32 + LOW, j, :], w_gk2[j, :, :]).then_inc(w_in, 16)
            sp.dma_start(w2s[0:LOW, :], w_gk2[NM, :, :]).then_inc(w_in, 16)
            for sem, credits in ((s_mul, MUL_CR), (s_Ve, VE_CR), (s_A, A_CR), (s_cp, CP_CR), (s_out, OUT_CR),
                                 (s_S, S_CR), (s_dir, DIR_CR), (s_lv, LV_CR), (s_Ad, AD_CR), (s_ends, ENDS_CR), (stored[0], ST_CR), (stored[1], ST_CR), (s_o, O_CR)):
                sp.sem_inc(sem, credits)

            def load(n, u):
                sp.dma_start(hT[:, u, :, :], hT_dram[:, :, ds(n * P, P)].rearrange("k p t -> p k t")).then_inc(ld[u], 16)
                sp.dma_start(kw[:, u, :], kw_dram[ds(n, 1), :, :].rearrange("a p n -> (a p) n")).then_inc(ld[u], 16)

            load(0, 0)
            load(1, 1)

            def body(n, u, q):
                wait_here(sp, s_out, OUT_CR + n * MS + MS, sp_passed)
                sp.dma_start(o_dram[ds(n * P, P), :], acc[:, u, :]).then_inc(stored[u], 16)
                wait_here(sp, s_S, S_CR + n * MS + MS, sp_passed)
                load(n + 2, u)

            tiles(sp, body)
            for u in range(2):
                sp.wait_ge(stored[u], ST_CR + NTT // 2 * 16)
                sp.wait_ge(ld[u], 32 * (NTT // 2 + 1))

        @block.gpsimd
        def _(pool):
            make_identity(pool, ident, made)
            pool.memset(w1[:, :, :, :], 0.0).then_inc(made, 1)
            pool.memset(w2[:, :, :], 0.0).then_inc(made, 1)
            pool.memset(w2s[:, :], 0.0).then_inc(made, 1)
            pool.memset(masks[:, :, :], 0.0).then_inc(made, 1)
            pool.memset(restart[:, :, :], 1.0).then_inc(made, 1)
            pool.wait_ge(made, 7)
            pool.memset(restart[:, :, 0:1], 0.0).then_inc(made, 1)
            pool.memset(qt[:, :, :, :], 0.0).then_inc(made, 1)
            pool.memset(kt[:, :, :, :], 0.0).then_inc(made, 1)
            pool.memset(ones[:, :], 1.0).then_inc(made, 1)
            at = 11
            for l in range(DIRECT, NL):
                s = HALVES[l] if l < NL - 1 else 1
                v = masks[:, l - DIRECT, :].rearrange("p (n r) -> p n r", r=2 * s)
                v = v[:, :, s:2 * s] if l < NL - 1 else v
                r = s if l < NL - 1 else 2
                pool.wait_ge(made, at)
                pool.memset(v, 1.0).then_inc(made, 1)
                pool.wait_ge(made, at + 1)
                pool.affine_select(out=v, in_=v, compare_op=ALU.is_ge, fill=0.0, base=0,
                                   pattern=[[-2 * s, P // (2 * s)], [0, r]], channel_multiplier=1).then_inc(made, 1)
                pool.wait_ge(made, at + 2)
                pool.affine_select(out=v, in_=v, compare_op=ALU.is_ge, fill=0.0, base=s - 1,
                                   pattern=[[2 * s, P // (2 * s)], [1 if l == NL - 1 else 0, r]],
                                   channel_multiplier=-1).then_inc(made, 1)
                at += 3

            def keep_rows(fn, u, qf):
                pool.wait_ge(ld[u], qf * 32 + 32)
                pool.sem_inc(pool_passed, 1)
                pool.tensor_tensor(out=keep_m[:, :, :], in0=ident[:, :].unsqueeze(1).to_broadcast([P, NM, P]),
                                   in1=kw[:, u, 0:NM].unsqueeze(2).to_broadcast([P, NM, P]), op=ALU.mult).then_inc(s_kM, 1)

            def products(fn, u):
                q3 = qS[:, :]
                done = 0
                for l, s in enumerate(HALVES):
                    nb = P // (2 * s)
                    wait_here(pool, s_ex, fn * NX + 2 * l + 2, pool_passed)
                    for c in range(MS):
                        ins = pool.tensor_tensor(
                            out=qt[:, u, l, c * P:(c + 1) * P].rearrange("p (n r) -> p n r", r=2 * s)[:, :, s:2 * s],
                            in0=q3.rearrange("p (n r) -> p n r", r=2 * s)[:, :, s:2 * s],
                            in1=ex[:, l, c * P:(c + 1) * P].rearrange("p (n r) -> p n r", r=2 * s)[:, :, s:2 * s], op=ALU.mult)
                    ins.then_inc(s_mul, 1)
                    pool.tensor_tensor(
                        out=kt[:, u, l, :].rearrange("p (n r) -> p n r", r=2 * s)[:, :, 0:s],
                        in0=kS[:, :].rearrange("p (n r) -> p n r", r=2 * s)[:, :, 0:s],
                        in1=ex[:, l, :].rearrange("p (n r) -> p n r", r=2 * s)[:, :, 0:s], op=ALU.mult).then_inc(s_mul, 1)
                l = NL - 1
                wait_here(pool, s_ex, fn * NX + NX, pool_passed)
                pairs = lambda a: a.rearrange("p (n r) -> p n r", r=2)
                half = MP // 2
                qb = pairs(q3)
                qt4 = qt[:, u, l, :].rearrange("p (c n r) -> p c n r", c=MS, r=2)
                pool.tensor_copy(qt4[:, :, :, 0], qb[:, :, 0].unsqueeze(1).to_broadcast([P, MS, P // 2])).then_inc(s_mul, 1)
                pool.tensor_tensor(out=qt4[:, :, :, 1], in0=qb[:, :, 1].unsqueeze(1).to_broadcast([P, MS, P // 2]),
                                   in1=ex[:, l, 0:half].rearrange("p (c n) -> p c n", c=MS), op=ALU.mult).then_inc(s_mul, 1)
                pool.tensor_copy(pairs(kt[:, u, l, :])[:, :, 0], pairs(kS[:, :])[:, :, 0]).then_inc(s_mul, 1)
                pool.tensor_tensor(out=pairs(kt[:, u, l, :])[:, :, 1], in0=pairs(kS[:, :])[:, :, 1],
                                   in1=ex[:, l, half:MP], op=ALU.mult).then_inc(s_mul, 1)

            keep_rows(0, 0, 0)
            products(0, 0)

            def body(n, u, q):
                wait_here(pool, s_KB, n + 1, pool_passed)
                keep_rows(n + 1, 1 - u, q + u)
                products(n + 1, 1 - u)

            tiles(pool, body)

        @block.scalar
        def _(act):
            act.wait_ge(w_in, 16 * 10)
            act.wait_ge(made, 11)

            def front1(fn, u):
                act.wait_ge(s_mul, MUL_CR + fn * NMUL)
                act.wait_ge(s_ends, ENDS_CR + fn * 2)
                act.wait_ge(s_F1, fn * 2 + 1)
                nc.scalar.mul(qS[:, :], f[0][:, 0:P], float(GK) ** -0.5)
                nc.scalar.copy(kS[:, 0:3 * P], f[0][:, P:4 * P]).then_inc(s_F1e, 1)
                act.wait_ge(s_F1, fn * 2 + 2)
                nc.scalar.copy(kS[:, 3 * P:MP], f[1][:, 0:2 * P])
                nc.scalar.copy(low[:, :], f[1][:, 2 * P:3 * P])
                nc.scalar.copy(low_s[:, :], f[1][0:32, 3 * P:4 * P]).then_inc(s_F1e, 1)

            def front2(fn, u):
                act.wait_ge(s_Z, fn * 2 + 2)
                for c in range(MS):
                    src = f[2][:, c * P:(c + 1) * P] if c < NM else f[0][:, 0:P]
                    ins = nc.scalar.activation(zb[:, c * P:(c + 1) * P], src, ACT.Identity, bias=bg[:, c:c + 1])
                ins.then_inc(s_Ze, 1)
                act.wait_ge(s_Ze, fn + 1)
                nc.scalar.activation(az[:, :], zb[:, :], ACT.Abs).then_inc(s_gate, 1)
                act.wait_ge(s_gate, fn * 3 + 1)
                nc.scalar.activation(az[:, :], az[:, :], ACT.Exp, scale=-1.0).then_inc(s_gate, 1)
                act.wait_ge(s_gate, fn * 3 + 2)
                nc.scalar.activation(ln[:, :], az[:, :], ACT.Ln, bias=1.0).then_inc(s_gate, 1)

            def front3(fn, u):
                for j, (bank, mems) in enumerate(((2, (0, 1)), (1, (2, 3)), (0, (4,)))):
                    act.wait_ge(s_V, fn * 3 + j + 1)
                    for x, c in enumerate(mems):
                        src = f[bank][:, x * D:(x + 1) * D]
                        if c < NM:
                            ins = nc.scalar.activation(V[:, u, c, :], src, ACT.Copy, scale=kw[:, u, c:c + 1])
                        else:
                            ins = nc.scalar.copy(V[:, u, c, :], src)
                    ins.then_inc(s_Ve, 1)

            def front4(fn, u):
                act.wait_ge(s_mul, MUL_CR + fn * NMUL)
                for l, s in enumerate(HALVES):
                    act.wait_ge(s_D, fn * (NL + 1) + l + 1)
                    d3 = dist[:, l, :].rearrange("p (n r) -> p n r", r=2 * s)
                    e3 = ex[:, l, :].rearrange("p (n r) -> p n r", r=2 * s)
                    nc.scalar.activation(e3[:, :, s:2 * s], d3[:, :, s:2 * s], ACT.Exp).then_inc(s_ex, 1)
                    nc.scalar.activation(e3[:, :, 0:s], d3[:, :, 0:s], ACT.Exp, scale=-1.0).then_inc(s_ex, 1)
                act.wait_ge(s_D, fn * (NL + 1) + NL + 1)
                half = MP // 2
                nc.scalar.activation(ex[:, NL - 1, 0:half], gc[:, :], ACT.Exp).then_inc(s_ex, 1)
                nc.scalar.activation(ex[:, NL - 1, half:MP], gc[:, :], ACT.Exp, scale=-1.0).then_inc(s_ex, 1)
                nc.scalar.activation(dend[:, u, :], Gs[:, :].rearrange("p (c n) -> p c n", c=MS)[:, :, P - 1], ACT.Exp)
                nc.scalar.activation(exG[:, :], Gs[:, :], ACT.Exp).then_inc(s_ex, 1)
                nc.scalar.activation(exE[:, :], dist[:, NL - 1, :], ACT.Exp, scale=-1.0).then_inc(s_ex, 1)

            fronts = (front1, front2, front3, front4)
            for front in fronts:
                front(0, 0)

            def body(n, u, q):
                for c in range(MS):
                    k = n * MS + c
                    j = (u * MS + c) % 2
                    act.wait_ge(s_dir, DIR_CR + k * GH + GH)
                    act.wait_ge(s_o, O_CR - 1 + k)
                    nc.scalar.copy(A[:, j, :], pd[:, :]).then_inc(s_A, 1)
                    act.wait_ge(s_T, k + 1)
                    nc.scalar.copy(kE[:, :], pu[:, D:D + P]).then_inc(s_kE, 1)
                    for front in fronts[c:c + 1] if c < 2 else fronts[2:] if c == 2 else ():
                        front(n + 1, 1 - u)

            tiles(act, body)

        @block.vector
        def _(dve):
            dve.wait_ge(made, 11 + 3 * NLV)
            for x in range(P // BK):
                nc.vector.tensor_copy(masks_b[x * BK:(x + 1) * BK, :, :], masks[x * BK:(x + 1) * BK, :, x * BK:(x + 1) * BK]
                                      ).then_inc(s_mask, 1)
            dve.wait_ge(s_mask, P // BK)

            def front2(fn, u):
                c0 = fn * 3
                dve.wait_ge(s_Ze, fn + 1)
                nc.vector.tensor_scalar(zn[:, :], zb[:, :], 0.0, None, ALU.min).then_inc(s_chain, 1)
                dve.wait_ge(s_chain, c0 + 1)
                dve.wait_ge(s_gate, fn * 3 + 3)
                nc.vector.tensor_tensor(zn[:, :], zn[:, :], ln[:, :], ALU.subtract).then_inc(s_chain, 1)
                dve.wait_ge(s_chain, c0 + 2)
                dve.wait_ge(s_KB, fn + 1)
                nc.vector.scalar_tensor_tensor(g[:, 0:NM * P], zn[:, 0:NM * P], 1.0 / GATE_NORM, f[1][:, :], ALU.mult,
                                               ALU.mult).then_inc(s_g, 1)
                nc.vector.tensor_scalar(g[:, NM * P:MP], zn[:, NM * P:MP], 1.0 / GATE_NORM, None, ALU.mult).then_inc(s_g, 1)
                dve.wait_ge(s_g, fn * 2 + 2)
                nc.vector.tensor_tensor_scan(Gs[:, :], restart[:, :, :].rearrange("p c n -> p (c n)"), g[:, :], 0.0,
                                             ALU.mult, ALU.add).then_inc(s_chain, 1)

            def front3(fn, u):
                dve.wait_ge(s_chain, fn * 3 + 3)
                for l, s in enumerate(HALVES):
                    G3 = Gs[:, :].rearrange("p (n r) -> p n r", r=2 * s)
                    nc.vector.tensor_tensor(dist[:, l, :].rearrange("p (n r) -> p n r", r=2 * s), G3,
                                            G3[:, :, s - 1:s].to_broadcast([P, MP // (2 * s), 2 * s]),
                                            ALU.subtract).then_inc(s_D, 1)
                G3 = Gs[:, :].rearrange("p (n r) -> p n r", r=P)
                nc.vector.tensor_tensor(dist[:, NL - 1, :].rearrange("p (n r) -> p n r", r=P), G3,
                                        G3[:, :, P - 1:P].to_broadcast([P, MS, P]), ALU.subtract).then_inc(s_D, 1)
                nc.vector.tensor_scalar(gc[:, :], g[:, :].rearrange("p (n r) -> p n r", r=2)[:, :, 1], FLOOR, None,
                                        ALU.max).then_inc(s_D, 1)

            def output(n, u, c):
                k = n * MS + c
                dve.wait_ge(s_o, O_CR + k + 1)
                w = kw[:, u, NM + c:NM + c + 1] if c < NM else None
                if c == 0:
                    nc.vector.tensor_scalar(acc[:, u, :], po[:, :], w, None, ALU.mult).then_inc(s_out, 1)
                else:
                    dve.wait_ge(s_out, OUT_CR + k)
                    if c < NM:
                        nc.vector.scalar_tensor_tensor(acc[:, u, :], po[:, :], w, acc[:, u, :], ALU.mult,
                                                       ALU.add).then_inc(s_out, 1)
                    else:
                        nc.vector.tensor_tensor(acc[:, u, :], po[:, :], acc[:, u, :], ALU.add).then_inc(s_out, 1)
                dve.wait_ge(s_U, k + 1)
                for h in range(GH):
                    r = slice(h * GK, (h + 1) * GK)
                    ins = nc.vector.scalar_tensor_tensor(state[r, c, h * GV:(h + 1) * GV], state[r, c, h * GV:(h + 1) * GV],
                                                         dend[r, u, c:c + 1], pu[r, h * GV:(h + 1) * GV], ALU.mult, ALU.add)
                ins.then_inc(s_S, 1)

            def ends(fn, u):
                wait_here(dve, s_ex, fn * NX + NX, dve_passed)
                nc.vector.tensor_tensor(q0[:, u, :].rearrange("p (c n) -> p c n", c=MS),
                                        qS[:, :].unsqueeze(1).to_broadcast([P, MS, P]),
                                        exG[:, :].rearrange("p (c n) -> p c n", c=MS), ALU.mult).then_inc(s_ends, 1)
                nc.vector.tensor_tensor(kend[:, u, :], kS[:, :], exE[:, :], ALU.mult).then_inc(s_ends, 1)

            def scores(k, j):
                dve.wait_ge(s_lv, LV_CR + k * GH + GH)
                dve.wait_ge(s_Ad, AD_CR + k)
                for l in range(NLV):
                    mask = masks_b[:, l, :]
                    src = pl[j][:, l * P:(l + 1) * P].rearrange("p (h i) -> p h i", h=GH)
                    dst = small[:, :].rearrange("p (h i) -> p h i", h=GH)
                    if l == 0:
                        nc.vector.tensor_tensor(dst, src, mask.unsqueeze(1).to_broadcast([P, GH, BK]),
                                                ALU.mult).then_inc(s_cp, 1)
                    else:
                        wait_here(dve, s_cp, CP_CR + k * NLV + l, dve_passed)
                        nc.vector.copy_predicated(dst, mask.bitcast(U32).unsqueeze(1).to_broadcast([P, GH, BK]), src
                                                  ).then_inc(s_cp, 1)
                dve.wait_ge(s_cp, CP_CR + k * NLV + NLV)
                dve.wait_ge(s_A, A_CR + k + 1)
                for x in range(P // BK):
                    r = slice(x * BK, (x + 1) * BK)
                    block = A[r, j, :].rearrange("p (h i) -> p h i", h=GH)[:, :, x * BK:(x + 1) * BK]
                    ins = nc.vector.tensor_tensor(block, block, small[r, :].rearrange("p (h i) -> p h i", h=GH), ALU.add)
                ins.then_inc(s_Ad, 1)

            front2(0, 0)
            front3(0, 0)
            ends(0, 0)

            def reset(b):
                wait_here(dve, s_S, S_CR + b * (NT * MS), dve_passed)
                nc.vector.memset(state[:, :, :], 0.0).then_inc(s_reset, 1)
                wait_here(dve, s_reset, b + 1, dve_passed)

            def body(n, u, q):
                wait_here(dve, stored[u], ST_CR + q * 16, dve_passed)
                for c in range(MS):
                    k = n * MS + c
                    j = (u * MS + c) % 2
                    if c:
                        output(n, u, c - 1)
                    if c == 2:
                        front3(n + 1, 1 - u)
                    scores(k, j)
                    if c == 1:
                        front2(n + 1, 1 - u)
                    if c == 3:
                        ends(n + 1, 1 - u)
                output(n, u, MS - 1)

            tiles(dve, body, reset)

        @block.tensor
        def _(pe):
            pe.wait_ge(made, 11)
            pe.wait_ge(w_in, 16 * 10)

            def two(out, lhs, rhs):
                for c in range(KC):
                    ins = nc.tensor.matmul(out, lhs(c), rhs(c), start=(c == 0), stop=(c == KC - 1))
                return ins

            def front1(fn, u, qf):
                pe.wait_ge(ld[u], qf * 32 + 32)
                pe.wait_ge(s_Ve, VE_CR + fn * 3)
                h = lambda c: hT[:, u, c, :]
                two(f[0][:, 0:P], lambda c: wq[:, c, :], h)
                for x in range(3):
                    ins = two(f[0][:, (x + 1) * P:(x + 2) * P], lambda c: wk[:, x, c, :], h)
                ins.then_inc(s_F1, 1)
                for x in range(3, MS):
                    two(f[1][:, (x - 3) * P:(x - 2) * P], lambda c: wk[:, x, c, :], h)
                two(f[1][:, 2 * P:3 * P], lambda c: w1[:, c, 0:NM, :].rearrange("p m r -> p (m r)"), h)
                two(f[1][0:32, 3 * P:4 * P], lambda c: w1[:, c, NM, :], h).then_inc(s_F1, 1)

            def front2(fn, u, qf):
                pe.wait_ge(s_F1e, fn * 2 + 2)
                for x in range(NM):
                    nc.tensor.matmul(f[2][:, x * P:(x + 1) * P], w2[:, x, :], low[:, :], start=True, stop=True)
                ins = nc.tensor.matmul(f[0][:, 0:P], w2s[:, :], low_s[:, :], start=True, stop=True)
                ins.then_inc(s_Z, 2)
                pe.wait_ge(s_kM, fn + 1)
                nc.tensor.matmul(f[1][:, :], ones[:, :], keep_m[:, :, :].rearrange("p m t -> p (m t)"), start=True,
                                 stop=True).then_inc(s_KB, 1)

            def front3(fn, u, qf):
                h = lambda c: hT[:, u, c, :]
                pe.wait_ge(s_Ze, fn + 1)
                for x in range(2):
                    ins = two(f[2][:, x * D:(x + 1) * D], h, lambda c: wv[:, x, c, :])
                ins.then_inc(s_V, 1)
                pe.wait_ge(s_g, fn * 2 + 1)
                for x in range(2):
                    ins = two(f[1][:, x * D:(x + 1) * D], h, lambda c: wv[:, 2 + x, c, :])
                ins.then_inc(s_V, 1)
                two(f[0][:, 0:D], h, lambda c: wv[:, NM, c, :]).then_inc(s_V, 1)

            def direct(n, u, c, h):
                k = n * MS + c
                wait_here(pe, s_dir, DIR_CR + k * GH + h, pe_passed)
                r = slice(h * GK, (h + 1) * GK)
                for l in range(DIRECT):
                    s2 = 2 * HALVES[l]
                    for x in range(P // s2):
                        cols = slice(c * P + x * s2, c * P + (x + 1) * s2)
                        ins = nc.tensor.matmul(pd[x * s2:(x + 1) * s2, h * P + x * s2:h * P + (x + 1) * s2],
                                               kt[r, u, l, cols], qt[r, u, l, cols], start=(l == 0),
                                               stop=(l == DIRECT - 1), skip_group_check=True)
                ins.then_inc(s_dir, 1)

            def levels(n, u, c, h):
                k = n * MS + c
                j = (u * MS + c) % 2
                if h == 0:
                    pe.wait_ge(s_cp, CP_CR - NLV + k * NLV)
                wait_here(pe, s_lv, LV_CR + k * GH + h, pe_passed)
                r = slice(h * GK, (h + 1) * GK)
                for l in range(NLV):
                    for x in range(P // BK):
                        cols = slice(c * P + x * BK, c * P + (x + 1) * BK)
                        ins = nc.tensor.matmul(pl[j][x * BK:(x + 1) * BK, l * P + h * BK:l * P + (h + 1) * BK],
                                               kt[r, u, DIRECT + l, cols], qt[r, u, DIRECT + l, cols], start=True,
                                               stop=True)
                ins.then_inc(s_lv, 1)

            def output(n, u, c):
                k = n * MS + c
                j = (u * MS + c) % 2
                pe.wait_ge(s_Ad, AD_CR + k + 1)
                pe.wait_ge(s_out, OUT_CR + k)
                pe.wait_ge(s_S, S_CR + k + 1 - MS)
                nc.tensor.matmul(po[:, :], q0[:, u, c * P:(c + 1) * P], state[:, c, :], start=True, stop=False,
                                 skip_group_check=True)
                for h in range(GH):
                    ins = nc.tensor.matmul(po[:, h * GV:(h + 1) * GV], A[:, j, h * P:(h + 1) * P],
                                           V[:, u, c, h * GV:(h + 1) * GV], start=False, stop=True, skip_group_check=True)
                ins.then_inc(s_o, 1)

            front1(0, 0, 0)
            front2(0, 0, 0)
            front3(0, 0, 0)
            fronts = (front1, front2, front3)

            def body(n, u, q):
                pe.wait_ge(s_mul, MUL_CR + n * NMUL + 2 * DIRECT)
                pe.wait_ge(s_Ve, VE_CR + n * 3 + 3)
                for c in range(MS):
                    k = n * MS + c
                    pe.wait_ge(s_A, A_CR + k)
                    for h in range(GH):
                        if c and h == GH // 2:
                            output(n, u, c - 1)
                        if h == GH - 1:
                            pe.wait_ge(s_S, S_CR + k)
                            nc.tensor.transpose(pu[:, D:D + P], kend[:, u, c * P:(c + 1) * P], ident[:, :]).then_inc(s_T, 1)
                        direct(n, u, c, h)
                        if c == 0 and h == 0:
                            pe.wait_ge(s_mul, MUL_CR + n * NMUL + NMUL)
                            pe.wait_ge(s_ends, ENDS_CR + n * 2 + 2)
                        levels(n, u, c, h)
                    if c < len(fronts):
                        fronts[c](n + 1, 1 - u, q + u)
                    pe.wait_ge(s_kE, k + 1)
                    nc.tensor.matmul(pu[:, 0:D], kE[:, :], V[:, u, c, :], start=True, stop=True).then_inc(s_U, 1)
                output(n, u, MS - 1)

            tiles(pe, body, lambda b: wait_here(pe, s_reset, b + 1, pe_passed))


RMS_EPS = 1e-5


def phase_final(nc, x, hT_dram, o_dram, w_g, w_o, norm_w, x_out):
    with ExitStack() as ctx:
        m = Mem(nc, ctx, "fn_")
        G = 4
        W = G * P
        NS = T // W
        ident, eps = m.sb("ident", [P, P]), m.sb("eps", [P, 1])
        wg, wo = m.sb("wg", [P, KC, D]), m.sb("wo", [P, KC, D])
        nw = m.sb("nw", [P, GV])
        o, x_s = m.sb("o", [P, 2, G, D]), m.sb("x", [P, 2, G, D])
        hT = m.sb("hT", [P, 2, KC, W])
        sq = m.sb("sq", [P, G * D])
        ss, rms, inv = m.sb("ss", [P, G * GH]), m.sb("rms", [P, G * GH]), m.sb("inv", [P, G * GH])
        silu = m.sb("silu", [P, G * D])
        gate, y = m.sb("gate", [P, G * D]), m.sb("y", [P, G * D])
        yT = m.sb("yT", [P, KC, W])
        z = m.sb("z", [P, 2, G, D])
        p_g, p_T, p_z = m.ps("p_g", [P, G * D]), m.ps("p_T", [P, KC, W]), m.ps("p_z", [P, G * D])
        made, w_in = m.sem("made"), m.sem("w_in")
        o_in, xh_in = [m.sem(f"o_in{u}") for u in range(2)], [m.sem(f"xh_in{u}") for u in range(2)]
        stored = [m.sem(f"stored{u}") for u in range(2)]
        s_g, s_silu, s_gate, s_chain, s_rms, s_y = (m.sem(k) for k in ("g", "silu", "gate", "chain", "rms", "y"))
        s_T, s_yT, s_zmm, s_z = (m.sem(k) for k in ("T", "yT", "zmm", "z"))
        sp_passed = m.sem("sp_passed")
        CH = 4
        Z_CR, Y_CR, OUT_CR, GATE_CR, SILU_CR = 1, 1, 1, 1, 1
        block = ctx.enter_context(nc.Block())

        @block.sync
        def _(sp):
            sp.dma_start(wg[:, :, :], w_g).then_inc(w_in, 16)
            sp.dma_start(wo[:, :, :], w_o).then_inc(w_in, 16)
            sp.dma_start(nw[:, :], norm_w.to_broadcast([P, GV])).then_inc(w_in, 16)
            for sem, credits in ((s_z, Z_CR), (s_y, Y_CR), (stored[0], OUT_CR), (stored[1], OUT_CR), (s_gate, GATE_CR), (s_silu, SILU_CR)):
                sp.sem_inc(sem, credits)

            def load(n, u):
                sp.dma_start(o[:, u, :, :], rows(o_dram, n * W, G)).then_inc(o_in[u], 16)
                sp.dma_start(hT[:, u, :, :], hT_dram[:, :, ds(n * W, W)].rearrange("k p t -> p k t")).then_inc(xh_in[u], 16)
                sp.dma_start(x_s[:, u, :, :], rows(x, n * W, G)).then_inc(xh_in[u], 16)

            def store(n, u):
                wait_here(sp, s_z, Z_CR + n + 1, sp_passed)
                sp.dma_start(rows(x_out, n * W, G), z[:, u, :, :]).then_inc(stored[u], 16)

            load(0, 0)
            load(1, 1)
            with sp.Fori(0, NS // 2 - 1) as q:
                for u in range(2):
                    store(q * 2 + u, u)
                    load(q * 2 + (u + 2), u)
            for u in range(2):
                store(NS - 2 + u, u)
            for u in range(2):
                sp.wait_ge(stored[u], OUT_CR + NS // 2 * 16)

        @block.gpsimd
        def _(pool):
            make_identity(pool, ident, made)
            pool.memset(eps[:, :], RMS_EPS).then_inc(made, 1)
            pool.wait_ge(w_in, 48)
            with pool.Fori(0, NS) as n:
                pool.wait_ge(s_silu, SILU_CR + n + 1)
                pool.wait_ge(s_y, Y_CR + n)
                pool.tensor_tensor(out=gate[:, :].rearrange("p (n e) -> p n e", e=GV),
                                   in0=silu[:, :].rearrange("p (n e) -> p n e", e=GV),
                                   in1=nw[:, :].unsqueeze(1).to_broadcast([P, G * GH, GV]), op=ALU.mult
                                   ).then_inc(s_gate, 1)

        @block.scalar
        def _(act):
            act.wait_ge(made, 3)
            with act.Fori(0, NS) as n:
                act.wait_ge(s_chain, n * CH + 2)
                nc.scalar.activation(rms[:, :], ss[:, :], ACT.Sqrt, bias=eps[:, 0:1], scale=1.0 / GV).then_inc(s_rms, 1)
                act.wait_ge(s_g, n + 1)
                act.wait_ge(s_gate, GATE_CR + n)
                nc.scalar.activation(silu[:, :], p_g[:, :], ACT.Silu).then_inc(s_silu, 1)
                for k in range(KC):
                    act.wait_ge(s_T, n * KC + k + 1)
                    nc.scalar.copy(yT[:, k, :], p_T[:, k, :]).then_inc(s_yT, 1)

        @block.vector
        def _(dve):
            def norm(n, u, q):
                dve.wait_ge(o_in[u], q * 16 + 16)
                of = o[:, u, :, :].rearrange("p t d -> p (t d)")
                nc.vector.tensor_tensor(sq[:, :], of, of, ALU.mult).then_inc(s_chain, 1)
                dve.wait_ge(s_chain, n * CH + 1)
                nc.vector.tensor_reduce(ss[:, :], sq[:, :].rearrange("p (n e) -> p n e", e=GV), AX.X,
                                        ALU.add).then_inc(s_chain, 1)
                dve.wait_ge(s_rms, n + 1)
                nc.vector.reciprocal(inv[:, :], rms[:, :]).then_inc(s_chain, 1)
                dve.wait_ge(s_chain, n * CH + 3)
                nc.vector.tensor_tensor(sq[:, :].rearrange("p (n e) -> p n e", e=GV),
                                        of.rearrange("p (n e) -> p n e", e=GV),
                                        inv[:, :].unsqueeze(2).to_broadcast([P, G * GH, GV]), ALU.mult).then_inc(s_chain, 1)

            def residual(n, u, q):
                dve.wait_ge(s_zmm, n + 1)
                dve.wait_ge(xh_in[u], q * 32 + 32)
                dve.wait_ge(stored[u], OUT_CR + q * 16)
                nc.vector.tensor_tensor(z[:, u, :, :].rearrange("p t d -> p (t d)"), p_z[:, :],
                                        x_s[:, u, :, :].rearrange("p t d -> p (t d)"), ALU.add).then_inc(s_z, 1)

            with dve.Fori(0, NS // 2) as q:
                for u in range(2):
                    n = q * 2 + u
                    norm(n, u, q)
                    dve.wait_ge(s_chain, n * CH + 4)
                    dve.wait_ge(s_gate, GATE_CR + n + 1)
                    nc.vector.tensor_tensor(y[:, :], sq[:, :], gate[:, :], ALU.mult).then_inc(s_y, 1)
                    residual(n, u, q)

        @block.tensor
        def _(pe):
            pe.wait_ge(made, 2)
            pe.wait_ge(w_in, 48)

            def gates(n, u, q):
                pe.wait_ge(xh_in[u], q * 32 + 32)
                pe.wait_ge(s_silu, SILU_CR + n)
                for t in range(G):
                    for k in range(KC):
                        ins = nc.tensor.matmul(p_g[:, t * D:(t + 1) * D], hT[:, u, k, t * P:(t + 1) * P], wg[:, k, :],
                                               start=(k == 0), stop=(k == KC - 1))
                ins.then_inc(s_g, 1)

            with pe.Fori(0, NS // 2) as q:
                for u in range(2):
                    n = q * 2 + u
                    gates(n, u, q)
                    pe.wait_ge(s_y, Y_CR + n + 1)
                    for k in range(KC):
                        for t in range(G):
                            ins = nc.tensor.transpose(p_T[:, k, t * P:(t + 1) * P], y[:, t * D + k * P:t * D + (k + 1) * P],
                                                      ident[:, :])
                        ins.then_inc(s_T, 1)
                    pe.wait_ge(s_yT, n * KC + KC)
                    pe.wait_ge(s_z, Z_CR + n)
                    for t in range(G):
                        for k in range(KC):
                            ins = nc.tensor.matmul(p_z[:, t * D:(t + 1) * D], yT[:, k, t * P:(t + 1) * P], wo[:, k, :],
                                                   start=(k == 0), stop=(k == KC - 1))
                    ins.then_inc(s_zmm, 1)


def build(nc, a):
    def scratch(name, shape, dt=F32):
        return nc.dram_tensor(name, shape, dt).ap()

    x1, x2, x3 = (scratch(k, [T, D]) for k in ("x_attn_a", "x_ffn", "x_attn_b"))

    q_parts, k_parts = scratch("q_parts", [3, B * D, L], BF16), scratch("k_parts", [3, B * D, L], BF16)
    q_full = scratch("q_full", [D, T])
    k_tok, v_tok = scratch("k_tok", [B * H, P, NT * DH]), scratch("v_tok", [B * H, P, NT * DH])
    y_dram, kv_dram = scratch("y_terrace", [T, D]), scratch("kv_sums", [B * H, R, DH * DH])
    phase_project(nc, a["x"], a["a_wq"], a["a_wk"], a["a_wkv"], q_parts, k_parts, q_full, k_tok, v_tok)
    phase_attend(nc, q_parts, k_parts, k_tok, v_tok, a["a_mix"], a["a_index_decays"], a["a_mega_decays"], y_dram,
                 kv_dram)
    phase_merge(nc, a["x"], q_full, y_dram, kv_dram, a["a_mix"], a["a_wc"], x1)

    phase_moe(nc, x1, a["f_gate"], a["f_wg"], a["f_wu"], a["f_wd"], x2, "m1_")

    hT_dram = scratch("hT", [KC, P, T + 2 * P])
    kw_dram = scratch("keep_weights", [NTT + 2, P, 2 * NM])
    o_dram = scratch("o_gla", [T, D])
    phase_route(nc, x2, a["b_gate"], hT_dram, kw_dram)
    phase_gla(nc, hT_dram, kw_dram, a["b_wq"], a["b_wk"], a["b_wv"], a["b_gk1"], a["b_gk2"], a["b_bias"], o_dram)
    phase_final(nc, x2, hT_dram, o_dram, a["b_wg"], a["b_wo"], a["b_norm"], x3)

    phase_moe(nc, x3, a["f_gate"], a["f_wg"], a["f_wu"], a["f_wd"], a["out"], "m2_")


def kernel(**inputs):
    import concourse.bacc as bacc
    from concourse.bass_utils import run_bass_kernel_spmd

    def chunks(w):
        return np.ascontiguousarray(w.reshape(KC, P, -1).transpose(1, 0, 2))

    def stacked(w, shared):
        return np.concatenate([w, shared[None]]).reshape(len(w) + 1, KC, P, -1).transpose(2, 0, 1, 3)

    def part(prefix):
        return {k[len(prefix):]: np.asarray(v) for k, v in inputs.items() if k.startswith(prefix)}

    a, b, f = part("L0_attn_a_"), part("L0_attn_b_"), part("L0_ffn_")
    arrays = {
        "x": a["hidden_states"].reshape(T, D),
        "a_wq": chunks(a["Wq"].T),
        "a_wk": chunks(a["Wk"].T),
        "a_wc": chunks(a["Wc"].T),
        "a_wkv": np.concatenate([chunks(a["Wk"].T), chunks(a["Wv"].T)], axis=2),
        "a_mix": a["terrace_mix"].reshape(SEG, 1),
        "a_index_decays": a["index_decays"].T,
        "a_mega_decays": a["mega_decays"].reshape(1, H),
        "b_gate": chunks(b["w_gate"]),
        "b_wq": chunks(b["w_q"]),
        "b_wk": stacked(b["w_k"], b["w_ks"]),
        "b_wv": stacked(b["w_v"], b["w_vs"]),
        "b_gk1": stacked(b["w_gk1"], b["w_gk1s"]).transpose(0, 2, 1, 3),
        "b_gk2": np.concatenate([b["w_gk2"], b["w_gk2s"][None]]),
        "b_bias": np.concatenate([b["b_gk"], b["b_gks"][None]]).T,
        "b_wg": chunks(b["w_g"]),
        "b_wo": chunks(b["w_o"]),
        "b_norm": b["norm_w"].reshape(1, GV),
        "f_gate": chunks(f["gate_w"].T),
        "f_wg": stacked(f["w_gate"], f["ws_gate"]),
        "f_wu": stacked(f["w_up"], f["ws_up"]),
        "f_wd": np.concatenate([f["w_down"], f["ws_down"][None]]).transpose(1, 0, 2),
    }
    nc = bacc.Bacc("TRN2", target_bir_lowering=False, num_devices=1)
    sent, aps = {}, {}
    for name, v in arrays.items():
        v = np.ascontiguousarray(v)
        sent["in_" + name] = v
        aps[name] = nc.dram_tensor("in_" + name, v.shape, mybir.dt.from_np(v.dtype), kind="ExternalInput").ap()
    aps["out"] = nc.dram_tensor("out", [T, D], F32, kind="ExternalOutput").ap()
    build(nc, aps)
    r = run_bass_kernel_spmd(nc, [sent], core_ids=[0])
    return r.results[0]["out"].reshape(B, L, D)
```
